# Optimizing a Trainium2 kernel written in Bass

```python
import numpy as np
import jax
import jax.numpy as jnp

def _softmax(x, axis=-1):
    return jax.nn.softmax(x, axis=axis)

def _gelu(x):
    return jax.nn.gelu(x, approximate=True)

def _silu(x):
    return jax.nn.silu(x)

def _sigmoid(x):
    return jax.nn.sigmoid(x)

def _layernorm(x, axis=-1, eps=1e-05):
    m = jnp.mean(x, axis=axis, keepdims=True)
    v = jnp.var(x, axis=axis, keepdims=True)
    return (x - m) / jnp.sqrt(v + eps)

def _scatter_add(tgt, idx, src, axis=0):
    return tgt.at[idx].add(src)

def _segment_sum(src, seg, n):
    return jax.ops.segment_sum(src, seg, n)
kernel_name = 'mk_seq_preln_d4_jaxref_r8_8ac91a'

def setup_inputs(seed: int=0):
    np.random.seed(seed)
    _w = jnp.asarray

    def _L0_attn_setup():
        import jax, jax.numpy as jnp
        import numpy as np
        from jax import lax
        D_MODEL = 128
        D_STATE = 16
        D_CONV = 4
        EXPAND = 2
        D_INNER = EXPAND * D_MODEL
        DT_RANK = (D_MODEL + 15) // 16
        D_FF = 4 * D_MODEL
        B, L = (4, 256)

        def _layer_norm(x, g, b, eps=1e-05):
            mu = jnp.mean(x, axis=-1, keepdims=True)
            var = jnp.mean(jnp.square(x - mu), axis=-1, keepdims=True)
            return (x - mu) * lax.rsqrt(var + eps) * g + b

        def _silu(x):
            return x * jax.nn.sigmoid(x)

        def _mamba(x, in_proj_w, conv_w, conv_b, x_proj_w, dt_proj_w, dt_proj_b, A_log, D, out_proj_w):
            xz = x @ in_proj_w
            xi, z = jnp.split(xz, 2, axis=-1)
            xc = lax.conv_general_dilated(xi.transpose(0, 2, 1), conv_w, window_strides=(1,), padding=[(D_CONV - 1, 0)], feature_group_count=D_INNER, dimension_numbers=('NCH', 'OIH', 'NCH'))
            xc = _silu(xc + conv_b[None, :, None]).transpose(0, 2, 1)
            x_dbl = xc @ x_proj_w
            dt, Bm, Cm = jnp.split(x_dbl, [DT_RANK, DT_RANK + D_STATE], axis=-1)
            dt = jax.nn.softplus(dt @ dt_proj_w + dt_proj_b)
            A = -jnp.exp(A_log)

            def step(h, inp):
                dt_t, B_t, C_t, x_t = inp
                dA = jnp.exp(dt_t[..., None] * A)
                h = dA * h + dt_t[..., None] * B_t[:, None, :] * x_t[..., None]
                y = jnp.sum(h * C_t[:, None, :], axis=-1)
                return (h, y)
            h0 = jnp.zeros((x.shape[0], D_INNER, D_STATE), x.dtype)
            xs = (dt.transpose(1, 0, 2), Bm.transpose(1, 0, 2), Cm.transpose(1, 0, 2), xc.transpose(1, 0, 2))
            _, ys = lax.scan(step, h0, xs)
            y = ys.transpose(1, 0, 2) + D * xc
            y = y * _silu(z)
            return y @ out_proj_w
        key = jax.random.key(seed)
        ks = jax.random.split(key, 16)
        s = 0.02
        inp = {'x': jax.random.normal(ks[0], (B, L, D_MODEL), dtype=jnp.float32), 'ln1_g': jnp.ones((D_MODEL,), jnp.float32), 'ln1_b': jnp.zeros((D_MODEL,), jnp.float32), 'in_proj_w': jax.random.normal(ks[1], (D_MODEL, 2 * D_INNER), jnp.float32) * s, 'conv_w': jax.random.normal(ks[2], (D_INNER, 1, D_CONV), jnp.float32) * s, 'conv_b': jnp.zeros((D_INNER,), jnp.float32), 'x_proj_w': jax.random.normal(ks[3], (D_INNER, DT_RANK + 2 * D_STATE), jnp.float32) * s, 'dt_proj_w': jax.random.normal(ks[4], (DT_RANK, D_INNER), jnp.float32) * s, 'dt_proj_b': jax.random.uniform(ks[5], (D_INNER,), jnp.float32, -4.0, -2.0), 'A_log': jnp.log(jnp.broadcast_to(jnp.arange(1, D_STATE + 1, dtype=jnp.float32), (D_INNER, D_STATE))), 'D': jnp.ones((D_INNER,), jnp.float32), 'out_proj_w': jax.random.normal(ks[6], (D_INNER, D_MODEL), jnp.float32) * s, 'ln2_g': jnp.ones((D_MODEL,), jnp.float32), 'ln2_b': jnp.zeros((D_MODEL,), jnp.float32), 'ffn_w1': jax.random.normal(ks[7], (D_MODEL, D_FF), jnp.float32) * s, 'ffn_b1': jnp.zeros((D_FF,), jnp.float32), 'ffn_w2': jax.random.normal(ks[8], (D_FF, D_MODEL), jnp.float32) * s, 'ffn_b2': jnp.zeros((D_MODEL,), jnp.float32)}
        return inp
    _L0_attn_in = _L0_attn_setup()

    def _L0_ffn_setup():
        import jax, jax.numpy as jnp
        import numpy as np
        B, S, H, F, E, K = (4, 256, 128, 512, 8, 2)
        key = jax.random.key(seed)
        ks = jax.random.split(key, 4)
        sc = lambda d: 1.0 / np.sqrt(d)
        return {'x': jax.random.normal(ks[0], (B, S, H), jnp.float32), 'gate_w': jax.random.normal(ks[1], (H, E), jnp.float32) * sc(H), 'gate_b': jnp.zeros((E,), jnp.float32), 'w1': jax.random.normal(ks[2], (E, H, F), jnp.float32) * sc(H), 'b1': jnp.zeros((E, F), jnp.float32), 'w2': jax.random.normal(ks[3], (E, F, H), jnp.float32) * sc(F), 'b2': jnp.zeros((E, H), jnp.float32)}
    _L0_ffn_in = _L0_ffn_setup()

    def _L1_attn_setup():
        import jax, jax.numpy as jnp
        import numpy as np
        EPS = 1e-06

        def _l2_norm(t):
            inv = 1.0 / jnp.linalg.norm(t, ord=2, axis=-2)
            return t * inv[:, None, :]
        key = jax.random.key(seed)
        ks = jax.random.split(key, 8)
        B, C, D = (16, 256, 128)
        s = 1.0 / np.sqrt(D)
        return {'x': jax.random.normal(ks[0], (B, C, D), dtype=jnp.float32), 'Wq': jax.random.normal(ks[1], (D, D), dtype=jnp.float32) * s, 'bq': jnp.zeros((D,), dtype=jnp.float32), 'Wk': jax.random.normal(ks[2], (D, D), dtype=jnp.float32) * s, 'bk': jnp.zeros((D,), dtype=jnp.float32), 'Wv': jax.random.normal(ks[3], (D, D), dtype=jnp.float32) * s, 'bv': jnp.zeros((D,), dtype=jnp.float32), 'gamma': jax.random.normal(ks[4], (1,), dtype=jnp.float32) * 0.1}
    _L1_attn_in = _L1_attn_setup()

    def _L1_ffn_setup():
        import jax, jax.numpy as jnp
        import numpy as np
        D_MODEL = 128
        D_FF = 512
        N_EXPERTS = 8
        TOP_K = 2
        B, T = (4, 256)
        key = jax.random.key(seed)
        ks = jax.random.split(key, 5)
        x = jax.random.normal(ks[0], (B, T, D_MODEL), dtype=jnp.float32)

        def lin(k, shape, fan_in):
            return jax.random.normal(k, shape, dtype=jnp.float32) / np.float32(np.sqrt(fan_in))
        return {'x': x, 'router_w': lin(ks[1], (N_EXPERTS, D_MODEL), D_MODEL), 'w_gate': lin(ks[2], (N_EXPERTS, D_MODEL, D_FF), D_MODEL), 'w_up': lin(ks[3], (N_EXPERTS, D_MODEL, D_FF), D_MODEL), 'w_down': lin(ks[4], (N_EXPERTS, D_FF, D_MODEL), D_FF)}
    _L1_ffn_in = _L1_ffn_setup()

    def _L2_attn_setup():
        import jax, jax.numpy as jnp
        import numpy as np
        EMBED_DIM = 128
        NUM_HEADS = 16
        HEAD_DIM = EMBED_DIM // NUM_HEADS
        ALPHA = 1.0
        key = jax.random.key(seed)
        ks = jax.random.split(key, 9)
        B, T, D = (2, 256, EMBED_DIM)
        s = 1.0 / np.sqrt(D)
        return {'x': jax.random.normal(ks[0], (B, T, D), dtype=jnp.float32), 'Wq': jax.random.uniform(ks[1], (D, D), jnp.float32, -s, s), 'bq': jax.random.uniform(ks[2], (D,), jnp.float32, -s, s), 'Wk': jax.random.uniform(ks[3], (D, D), jnp.float32, -s, s), 'bk': jax.random.uniform(ks[4], (D,), jnp.float32, -s, s), 'Wv': jax.random.uniform(ks[5], (D, D), jnp.float32, -s, s), 'bv': jax.random.uniform(ks[6], (D,), jnp.float32, -s, s), 'Wo': jax.random.uniform(ks[7], (D, D), jnp.float32, -s, s), 'bo': jax.random.uniform(ks[8], (D,), jnp.float32, -s, s)}
    _L2_attn_in = _L2_attn_setup()

    def _L2_ffn_setup():
        import jax, jax.numpy as jnp
        import numpy as np
        K = 2
        key = jax.random.key(seed)
        ks = jax.random.split(key, 9)
        B, S, D, O, E = (4, 128, 128, 128, 8)
        sc = 0.02
        return {'x': jax.random.normal(ks[0], (B, S, D), dtype=jnp.float32), 'gate_w': jax.random.normal(ks[1], (D, E), dtype=jnp.float32) * sc, 'gate_b': jax.random.normal(ks[2], (E,), dtype=jnp.float32) * sc, 'w1': jax.random.normal(ks[3], (E, D, O), dtype=jnp.float32) * sc, 'b1': jax.random.normal(ks[4], (E, O), dtype=jnp.float32) * sc, 'w2': jax.random.normal(ks[5], (E, O, O), dtype=jnp.float32) * sc, 'b2': jax.random.normal(ks[6], (E, O), dtype=jnp.float32) * sc, 'w3': jax.random.normal(ks[7], (E, O, O), dtype=jnp.float32) * sc, 'b3': jax.random.normal(ks[8], (E, O), dtype=jnp.float32) * sc}
    _L2_ffn_in = _L2_ffn_setup()

    def _L3_attn_setup():
        import jax, jax.numpy as jnp
        import numpy as np
        D_MODEL = 128
        N_HEADS = 16
        D_K = D_MODEL // N_HEADS
        WINDOW = 64
        ROPE_BASE = 10000.0

        def _apply_rope(x):
            S, D = (x.shape[2], x.shape[3])
            half = D // 2
            inv_freq = 1.0 / ROPE_BASE ** (jnp.arange(half, dtype=jnp.float32) / half)
            ang = jnp.arange(S, dtype=jnp.float32)[:, None] * inv_freq[None, :]
            cos = jnp.cos(ang).astype(x.dtype)
            sin = jnp.sin(ang).astype(x.dtype)
            x_even = x[..., ::2]
            x_odd = x[..., 1::2]
            out_even = x_even * cos - x_odd * sin
            out_odd = x_odd * cos + x_even * sin
            return jnp.stack([out_even, out_odd], axis=-1).reshape(x.shape)
        key = jax.random.key(seed)
        k1, k2, k3 = jax.random.split(key, 3)
        B, S = (2, 256)
        x = jax.random.normal(k1, (B, S, D_MODEL), dtype=jnp.float32)
        w_qkv = jax.random.normal(k2, (D_MODEL, 3 * D_MODEL), dtype=jnp.float32) * D_MODEL ** (-0.5)
        w_o = jax.random.normal(k3, (D_MODEL, D_MODEL), dtype=jnp.float32) * D_MODEL ** (-0.5)
        return {'x': x, 'w_qkv': w_qkv, 'w_o': w_o}
    _L3_attn_in = _L3_attn_setup()

    def _L3_ffn_setup():
        import jax, jax.numpy as jnp
        import numpy as np
        D_IN, D_HID = (128, 512)

        def _ternary(key, shape):
            return jax.random.randint(key, shape, -1, 2).astype(jnp.float32)

        def _tlin(x, w, s):
            return jnp.einsum('bsi,oi->bso', x, w) * s
        key = jax.random.key(seed)
        ks = jax.random.split(key, 12)
        inv = lambda fan: 1.0 / np.sqrt(fan).astype(np.float32)
        return {'x': jax.random.normal(ks[0], (4, 256, D_IN), dtype=jnp.float32), 'w1_w': _ternary(ks[1], (D_HID, D_IN)), 'w1_s': jax.random.uniform(ks[2], (D_HID,), dtype=jnp.float32) * inv(D_IN), 'w2_w': _ternary(ks[3], (D_HID, D_IN)), 'w2_s': jax.random.uniform(ks[4], (D_HID,), dtype=jnp.float32) * inv(D_IN), 'h1_w': _ternary(ks[5], (D_HID, D_HID)), 'h1_s': jax.random.uniform(ks[6], (D_HID,), dtype=jnp.float32) * inv(D_HID), 'h2_w': _ternary(ks[7], (D_HID, D_HID)), 'h2_s': jax.random.uniform(ks[8], (D_HID,), dtype=jnp.float32) * inv(D_HID), 'w3_w': _ternary(ks[9], (D_IN, D_HID)), 'w3_s': jax.random.uniform(ks[10], (D_IN,), dtype=jnp.float32) * inv(D_HID)}
    _L3_ffn_in = _L3_ffn_setup()
    _d = {'L0_attn_x': _L0_attn_in['x'], 'L0_attn_ln1_g': _L0_attn_in['ln1_g'], 'L0_attn_ln1_b': _L0_attn_in['ln1_b'], 'L0_attn_in_proj_w': _L0_attn_in['in_proj_w'], 'L0_attn_conv_w': _L0_attn_in['conv_w'], 'L0_attn_conv_b': _L0_attn_in['conv_b'], 'L0_attn_x_proj_w': _L0_attn_in['x_proj_w'], 'L0_attn_dt_proj_w': _L0_attn_in['dt_proj_w'], 'L0_attn_dt_proj_b': _L0_attn_in['dt_proj_b'], 'L0_attn_A_log': _L0_attn_in['A_log'], 'L0_attn_D': _L0_attn_in['D'], 'L0_attn_out_proj_w': _L0_attn_in['out_proj_w'], 'L0_attn_ln2_g': _L0_attn_in['ln2_g'], 'L0_attn_ln2_b': _L0_attn_in['ln2_b'], 'L0_attn_ffn_w1': _L0_attn_in['ffn_w1'], 'L0_attn_ffn_b1': _L0_attn_in['ffn_b1'], 'L0_attn_ffn_w2': _L0_attn_in['ffn_w2'], 'L0_attn_ffn_b2': _L0_attn_in['ffn_b2'], 'L0_ffn_gate_w': _L0_ffn_in['gate_w'], 'L0_ffn_gate_b': _L0_ffn_in['gate_b'], 'L0_ffn_w1': _L0_ffn_in['w1'], 'L0_ffn_b1': _L0_ffn_in['b1'], 'L0_ffn_w2': _L0_ffn_in['w2'], 'L0_ffn_b2': _L0_ffn_in['b2'], 'L1_attn_Wq': _L1_attn_in['Wq'], 'L1_attn_bq': _L1_attn_in['bq'], 'L1_attn_Wk': _L1_attn_in['Wk'], 'L1_attn_bk': _L1_attn_in['bk'], 'L1_attn_Wv': _L1_attn_in['Wv'], 'L1_attn_bv': _L1_attn_in['bv'], 'L1_attn_gamma': _L1_attn_in['gamma'], 'L1_ffn_router_w': _L1_ffn_in['router_w'], 'L1_ffn_w_gate': _L1_ffn_in['w_gate'], 'L1_ffn_w_up': _L1_ffn_in['w_up'], 'L1_ffn_w_down': _L1_ffn_in['w_down'], 'L2_attn_Wq': _L2_attn_in['Wq'], 'L2_attn_bq': _L2_attn_in['bq'], 'L2_attn_Wk': _L2_attn_in['Wk'], 'L2_attn_bk': _L2_attn_in['bk'], 'L2_attn_Wv': _L2_attn_in['Wv'], 'L2_attn_bv': _L2_attn_in['bv'], 'L2_attn_Wo': _L2_attn_in['Wo'], 'L2_attn_bo': _L2_attn_in['bo'], 'L2_ffn_gate_w': _L2_ffn_in['gate_w'], 'L2_ffn_gate_b': _L2_ffn_in['gate_b'], 'L2_ffn_w1': _L2_ffn_in['w1'], 'L2_ffn_b1': _L2_ffn_in['b1'], 'L2_ffn_w2': _L2_ffn_in['w2'], 'L2_ffn_b2': _L2_ffn_in['b2'], 'L2_ffn_w3': _L2_ffn_in['w3'], 'L2_ffn_b3': _L2_ffn_in['b3'], 'L3_attn_w_qkv': _L3_attn_in['w_qkv'], 'L3_attn_w_o': _L3_attn_in['w_o'], 'L3_ffn_w1_w': _L3_ffn_in['w1_w'], 'L3_ffn_w1_s': _L3_ffn_in['w1_s'], 'L3_ffn_w2_w': _L3_ffn_in['w2_w'], 'L3_ffn_w2_s': _L3_ffn_in['w2_s'], 'L3_ffn_h1_w': _L3_ffn_in['h1_w'], 'L3_ffn_h1_s': _L3_ffn_in['h1_s'], 'L3_ffn_h2_w': _L3_ffn_in['h2_w'], 'L3_ffn_h2_s': _L3_ffn_in['h2_s'], 'L3_ffn_w3_w': _L3_ffn_in['w3_w'], 'L3_ffn_w3_s': _L3_ffn_in['w3_s']}
    _x0 = _d['L0_attn_x']
    _d['L0_attn_x'] = jax.random.normal(jax.random.fold_in(jax.random.key(seed), 1), (1, 2048, 128), dtype=_x0.dtype)
    del _x0
    return _d

def reference(L0_attn_x, L0_attn_ln1_g, L0_attn_ln1_b, L0_attn_in_proj_w, L0_attn_conv_w, L0_attn_conv_b, L0_attn_x_proj_w, L0_attn_dt_proj_w, L0_attn_dt_proj_b, L0_attn_A_log, L0_attn_D, L0_attn_out_proj_w, L0_attn_ln2_g, L0_attn_ln2_b, L0_attn_ffn_w1, L0_attn_ffn_b1, L0_attn_ffn_w2, L0_attn_ffn_b2, L0_ffn_gate_w, L0_ffn_gate_b, L0_ffn_w1, L0_ffn_b1, L0_ffn_w2, L0_ffn_b2, L1_attn_Wq, L1_attn_bq, L1_attn_Wk, L1_attn_bk, L1_attn_Wv, L1_attn_bv, L1_attn_gamma, L1_ffn_router_w, L1_ffn_w_gate, L1_ffn_w_up, L1_ffn_w_down, L2_attn_Wq, L2_attn_bq, L2_attn_Wk, L2_attn_bk, L2_attn_Wv, L2_attn_bv, L2_attn_Wo, L2_attn_bo, L2_ffn_gate_w, L2_ffn_gate_b, L2_ffn_w1, L2_ffn_b1, L2_ffn_w2, L2_ffn_b2, L2_ffn_w3, L2_ffn_b3, L3_attn_w_qkv, L3_attn_w_o, L3_ffn_w1_w, L3_ffn_w1_s, L3_ffn_w2_w, L3_ffn_w2_s, L3_ffn_h1_w, L3_ffn_h1_s, L3_ffn_h2_w, L3_ffn_h2_s, L3_ffn_w3_w, L3_ffn_w3_s):

    def _L0_attn_ref(x, ln1_g, ln1_b, in_proj_w, conv_w, conv_b, x_proj_w, dt_proj_w, dt_proj_b, A_log, D, out_proj_w, ln2_g, ln2_b, ffn_w1, ffn_b1, ffn_w2, ffn_b2):
        import jax, jax.numpy as jnp
        import numpy as np
        from jax import lax
        D_MODEL = 128
        D_STATE = 16
        D_CONV = 4
        EXPAND = 2
        D_INNER = EXPAND * D_MODEL
        DT_RANK = (D_MODEL + 15) // 16
        D_FF = 4 * D_MODEL
        B, L = (4, 256)

        def _layer_norm(x, g, b, eps=1e-05):
            mu = jnp.mean(x, axis=-1, keepdims=True)
            var = jnp.mean(jnp.square(x - mu), axis=-1, keepdims=True)
            return (x - mu) * lax.rsqrt(var + eps) * g + b

        def _silu(x):
            return x * jax.nn.sigmoid(x)

        def _mamba(x, in_proj_w, conv_w, conv_b, x_proj_w, dt_proj_w, dt_proj_b, A_log, D, out_proj_w):
            xz = x @ in_proj_w
            xi, z = jnp.split(xz, 2, axis=-1)
            xc = lax.conv_general_dilated(xi.transpose(0, 2, 1), conv_w, window_strides=(1,), padding=[(D_CONV - 1, 0)], feature_group_count=D_INNER, dimension_numbers=('NCH', 'OIH', 'NCH'))
            xc = _silu(xc + conv_b[None, :, None]).transpose(0, 2, 1)
            x_dbl = xc @ x_proj_w
            dt, Bm, Cm = jnp.split(x_dbl, [DT_RANK, DT_RANK + D_STATE], axis=-1)
            dt = jax.nn.softplus(dt @ dt_proj_w + dt_proj_b)
            A = -jnp.exp(A_log)

            def step(h, inp):
                dt_t, B_t, C_t, x_t = inp
                dA = jnp.exp(dt_t[..., None] * A)
                h = dA * h + dt_t[..., None] * B_t[:, None, :] * x_t[..., None]
                y = jnp.sum(h * C_t[:, None, :], axis=-1)
                return (h, y)
            h0 = jnp.zeros((x.shape[0], D_INNER, D_STATE), x.dtype)
            xs = (dt.transpose(1, 0, 2), Bm.transpose(1, 0, 2), Cm.transpose(1, 0, 2), xc.transpose(1, 0, 2))
            _, ys = lax.scan(step, h0, xs)
            y = ys.transpose(1, 0, 2) + D * xc
            y = y * _silu(z)
            return y @ out_proj_w
        x = x + _mamba(_layer_norm(x, ln1_g, ln1_b), in_proj_w, conv_w, conv_b, x_proj_w, dt_proj_w, dt_proj_b, A_log, D, out_proj_w)
        h = _layer_norm(x, ln2_g, ln2_b)
        h = jax.nn.gelu(h @ ffn_w1 + ffn_b1) @ ffn_w2 + ffn_b2
        return x + h

    def _L0_ffn_ref(x, gate_w, gate_b, w1, b1, w2, b2):
        import jax, jax.numpy as jnp
        import numpy as np
        B, S, H, F, E, K = (4, 256, 128, 512, 8, 2)
        Bb, Ss, Hh = x.shape
        xf = x.reshape(-1, Hh)
        gate = jax.nn.softmax(xf @ gate_w + gate_b)
        topv, topi = jax.lax.top_k(gate, K)
        topv = topv / topv.sum(-1, keepdims=True)
        combine = (jax.nn.one_hot(topi, gate.shape[-1], dtype=xf.dtype) * topv[..., None]).sum(1)

        def body(acc, p):
            w1e, b1e, w2e, b2e, ce = p
            h = jax.nn.relu(xf @ w1e + b1e)
            y = h @ w2e + b2e
            return (acc + y * ce[:, None], None)
        acc0 = jnp.zeros_like(xf)
        out, _ = jax.lax.scan(body, acc0, (w1, b1, w2, b2, combine.T))
        return out.reshape(Bb, Ss, Hh)

    def _L1_attn_ref(x, Wq, bq, Wk, bk, Wv, bv, gamma):
        import jax, jax.numpy as jnp
        import numpy as np
        EPS = 1e-06

        def _l2_norm(t):
            inv = 1.0 / jnp.linalg.norm(t, ord=2, axis=-2)
            return t * inv[:, None, :]
        B, C, L = x.shape
        Q = x @ Wq.T + bq
        K = x @ Wk.T + bk
        V = x @ Wv.T + bv
        Q = jnp.transpose(_l2_norm(Q), (0, 2, 1))
        K = _l2_norm(K)
        tailor_sum = 1.0 / (L + jnp.einsum('bnc,bc->bn', Q, jnp.sum(K, axis=-1) + EPS))
        value_sum = jnp.sum(V, axis=-1)[:, :, None]
        matrix = jnp.einsum('bmn,bcn->bmc', K, V)
        matrix_sum = value_sum + jnp.einsum('bnm,bmc->bcn', Q, matrix)
        weight_value = matrix_sum * tailor_sum[:, None, :]
        return x + gamma * weight_value

    def _L1_ffn_ref(x, router_w, w_gate, w_up, w_down):
        import jax, jax.numpy as jnp
        import numpy as np
        D_MODEL = 128
        D_FF = 512
        N_EXPERTS = 8
        TOP_K = 2
        B, T = (4, 256)
        Bx, Tx, D = x.shape
        xf = x.reshape(-1, D)
        logits = xf @ router_w.T
        scores = jax.nn.softmax(logits, axis=-1)
        topk_scores, topk_ids = jax.lax.top_k(scores, TOP_K)
        topk_scores = topk_scores / topk_scores.sum(-1, keepdims=True)
        cw = (jax.nn.one_hot(topk_ids, N_EXPERTS, dtype=xf.dtype) * topk_scores[..., None]).sum(1)

        def body(acc, inputs):
            wg, wu, wd, w = inputs
            h = jax.nn.silu(xf @ wg) * (xf @ wu)
            acc = acc + w[:, None] * (h @ wd)
            return (acc, None)
        out, _ = jax.lax.scan(body, jnp.zeros_like(xf), (w_gate, w_up, w_down, cw.T))
        return out.reshape(Bx, Tx, D)

    def _L2_attn_ref(x, Wq, bq, Wk, bk, Wv, bv, Wo, bo):
        import jax, jax.numpy as jnp
        import numpy as np
        EMBED_DIM = 128
        NUM_HEADS = 16
        HEAD_DIM = EMBED_DIM // NUM_HEADS
        ALPHA = 1.0
        B, T, D = x.shape
        H, hd = (NUM_HEADS, HEAD_DIM)

        def proj(W, b):
            return (x @ W.T + b).reshape(B, T, H, hd).transpose(0, 2, 1, 3)
        Q = proj(Wq, bq)
        K = proj(Wk, bk)
        V = proj(Wv, bv)
        scores = jnp.einsum('bhid,bhjd->bhij', Q, K) / jnp.sqrt(jnp.float32(hd))
        ti = jnp.arange(T)
        delta = ti[:, None] - ti[None, :]
        causal = delta < 0
        deltaf = delta.astype(jnp.float32)
        decay = jnp.where(causal, 0.0, -jnp.abs(deltaf) ** ALPHA)
        scores = jnp.where(causal[None, None], -jnp.inf, scores) + decay[None, None]
        attn = jax.nn.softmax(scores, axis=-1)
        out = jnp.einsum('bhij,bhjd->bhid', attn, V)
        out = out.transpose(0, 2, 1, 3).reshape(B, T, D)
        return out @ Wo.T + bo

    def _L2_ffn_ref(x, gate_w, gate_b, w1, b1, w2, b2, w3, b3):
        import jax, jax.numpy as jnp
        import numpy as np
        K = 2
        E = gate_w.shape[-1]
        logits = jnp.einsum('bsd,de->bse', x, gate_w) + gate_b
        probs = jax.nn.softmax(logits, axis=1)
        vals, idx = jax.lax.top_k(probs, K)
        h = jax.nn.relu(jnp.einsum('bsd,edo->ebso', x, w1) + b1[:, None, None, :])
        h = jax.nn.relu(jnp.einsum('ebso,eop->ebsp', h, w2) + b2[:, None, None, :])
        y = jax.nn.relu(jnp.einsum('ebso,eop->ebsp', h, w3) + b3[:, None, None, :])
        onehot = jax.nn.one_hot(idx, E, dtype=x.dtype)
        w_tok = jnp.einsum('bske,bsk->bse', onehot, vals)
        ind = onehot.max(axis=2)
        v = jnp.einsum('ebso,bse->eo', y, w_tok)
        out = jnp.einsum('bse,eo->bso', ind, v)
        return out

    def _L3_attn_ref(x, w_qkv, w_o):
        import jax, jax.numpy as jnp
        import numpy as np
        D_MODEL = 128
        N_HEADS = 16
        D_K = D_MODEL // N_HEADS
        WINDOW = 64
        ROPE_BASE = 10000.0

        def _apply_rope(x):
            S, D = (x.shape[2], x.shape[3])
            half = D // 2
            inv_freq = 1.0 / ROPE_BASE ** (jnp.arange(half, dtype=jnp.float32) / half)
            ang = jnp.arange(S, dtype=jnp.float32)[:, None] * inv_freq[None, :]
            cos = jnp.cos(ang).astype(x.dtype)
            sin = jnp.sin(ang).astype(x.dtype)
            x_even = x[..., ::2]
            x_odd = x[..., 1::2]
            out_even = x_even * cos - x_odd * sin
            out_odd = x_odd * cos + x_even * sin
            return jnp.stack([out_even, out_odd], axis=-1).reshape(x.shape)
        B, S, _ = x.shape
        qkv = (x @ w_qkv).reshape(B, S, 3, N_HEADS, D_K)
        qkv = jnp.transpose(qkv, (2, 0, 3, 1, 4))
        q, k, v = (qkv[0], qkv[1], qkv[2])
        q = _apply_rope(q)
        k = _apply_rope(k)
        i = jnp.arange(S)[:, None]
        j = jnp.arange(S)[None, :]
        allowed = (j <= i) & (j >= i - WINDOW)
        bias = jnp.where(allowed, 0.0, -jnp.inf).astype(x.dtype)
        scores = jnp.einsum('bhqd,bhkd->bhqk', q, k) * D_K ** (-0.5) + bias
        attn = jax.nn.softmax(scores, axis=-1)
        out = jnp.einsum('bhqk,bhkd->bhqd', attn, v)
        out = jnp.transpose(out, (0, 2, 1, 3)).reshape(B, S, D_MODEL)
        return out @ w_o

    def _L3_ffn_ref(x, w1_w, w1_s, w2_w, w2_s, h1_w, h1_s, h2_w, h2_s, w3_w, w3_s):
        import jax, jax.numpy as jnp
        import numpy as np
        D_IN, D_HID = (128, 512)

        def _ternary(key, shape):
            return jax.random.randint(key, shape, -1, 2).astype(jnp.float32)

        def _tlin(x, w, s):
            return jnp.einsum('bsi,oi->bso', x, w) * s
        h = jax.nn.silu(_tlin(x, w1_w, w1_s)) * _tlin(x, w2_w, w2_s)
        h = jax.nn.gelu(_tlin(h, h1_w, h1_s), approximate=False)
        h = jax.nn.gelu(_tlin(h, h2_w, h2_s), approximate=False)
        return _tlin(h, w3_w, w3_s)
    x = L0_attn_x
    x = x + _L0_attn_ref(_layernorm(x, axis=-1), L0_attn_ln1_g, L0_attn_ln1_b, L0_attn_in_proj_w, L0_attn_conv_w, L0_attn_conv_b, L0_attn_x_proj_w, L0_attn_dt_proj_w, L0_attn_dt_proj_b, L0_attn_A_log, L0_attn_D, L0_attn_out_proj_w, L0_attn_ln2_g, L0_attn_ln2_b, L0_attn_ffn_w1, L0_attn_ffn_b1, L0_attn_ffn_w2, L0_attn_ffn_b2)
    x = x + _L0_ffn_ref(_layernorm(x, axis=-1), L0_ffn_gate_w, L0_ffn_gate_b, L0_ffn_w1, L0_ffn_b1, L0_ffn_w2, L0_ffn_b2)
    x = x + _L1_attn_ref(_layernorm(x, axis=-1), L1_attn_Wq, L1_attn_bq, L1_attn_Wk, L1_attn_bk, L1_attn_Wv, L1_attn_bv, L1_attn_gamma)
    x = x + _L1_ffn_ref(_layernorm(x, axis=-1), L1_ffn_router_w, L1_ffn_w_gate, L1_ffn_w_up, L1_ffn_w_down)
    x = x + _L2_attn_ref(_layernorm(x, axis=-1), L2_attn_Wq, L2_attn_bq, L2_attn_Wk, L2_attn_bk, L2_attn_Wv, L2_attn_bv, L2_attn_Wo, L2_attn_bo)
    x = x + _L2_ffn_ref(_layernorm(x, axis=-1), L2_ffn_gate_w, L2_ffn_gate_b, L2_ffn_w1, L2_ffn_b1, L2_ffn_w2, L2_ffn_b2, L2_ffn_w3, L2_ffn_b3)
    x = x + _L3_attn_ref(_layernorm(x, axis=-1), L3_attn_w_qkv, L3_attn_w_o)
    x = x + _L3_ffn_ref(_layernorm(x, axis=-1), L3_ffn_w1_w, L3_ffn_w1_s, L3_ffn_w2_w, L3_ffn_w2_s, L3_ffn_h1_w, L3_ffn_h1_s, L3_ffn_h2_w, L3_ffn_h2_s, L3_ffn_w3_w, L3_ffn_w3_s)
    return x

_drawn_inputs = setup_inputs


def setup_inputs(seed=0):
    import zlib

    import numpy as np

    out = dict(_drawn_inputs(seed))
    spreads = {'L0_attn_ln1_g': (1.0, 0.2),
     'L0_attn_ln1_b': (0.0, 0.1),
     'L0_attn_conv_b': (0.0, 0.1),
     'L0_attn_D': (1.0, 0.2),
     'L0_attn_ln2_g': (1.0, 0.2),
     'L0_attn_ln2_b': (0.0, 0.1),
     'L0_attn_ffn_b1': (0.0, 0.1),
     'L0_attn_ffn_b2': (0.0, 0.1),
     'L0_ffn_gate_b': (0.0, 0.1),
     'L0_ffn_b1': (0.0, 0.1),
     'L0_ffn_b2': (0.0, 0.1),
     'L1_attn_bq': (0.0, 0.1),
     'L1_attn_bk': (0.0, 0.1),
     'L1_attn_bv': (0.0, 0.1)}
    factors = {}
    for name, (base, spread) in spreads.items():
        noise = np.random.default_rng([zlib.crc32(name.encode()), seed]).standard_normal(out[name].shape)
        drawn = base * np.exp(spread * noise) if base else spread * noise
        out[name] = jnp.asarray(drawn.astype(out[name].dtype))
    for name, factor in factors.items():
        out[name] = (out[name] * factor).astype(out[name].dtype)
    return out
```

```python
from contextlib import ExitStack

import concourse.bass as bass
from concourse import mybir

F32 = mybir.dt.float32
BF16 = mybir.dt.bfloat16
U32 = mybir.dt.uint32
ALU = mybir.AluOpType
ACT = mybir.ActivationFunctionType
AX = mybir.AxisListType

P = 128
CT = 4
CW = CT * P
EPS = 1e-5
MASKED = -1.0e30
PARTS = ("mamba", "moe0", "linear", "moe1", "decay", "deep", "window", "ffn3")


class Core:

    def __init__(self, nc, ctx, t):
        self.nc, self.ctx, self.t = nc, ctx, t
        self.N = t["x"].shape[0]
        self.T = self.N // P
        self.C = self.T // CT
        self.E = t["moe0_gate_w"].shape[1]
        self.L = 0
        self.bank = [ctx.enter_context(nc.psum_tensor(f"bank{i}", [P, 512], F32)) for i in range(8)]
        self.X = self.sb("X", [P, self.T, P])
        self.xnT = self.sb("xnT", [P, self.N])
        self.stats = self.sb("stats", [P, CT, 6])
        self.meanvar = self.sb("meanvar", [P, CT, 2])
        self.veps = self.sb("veps", [P, CT])
        self.rstd = self.sb("rstd", [P, CT])
        self.xn = self.sb("xn", [P, CT, P])
        self.ident = self.sb("ident", [P, P])
        self.identb = self.sb("identb", [P, P], BF16)
        self.ones = self.sb("ones", [P, P])
        self.mhalf = self.sb("mhalf", [P, 32])
        self.part_sems = []
        self.passed = self.sem("passed")
        self.ln_st = self.sem("ln_st")
        self.ln_mv = self.sem("ln_mv")
        self.ln_ve = self.sem("ln_ve")
        self.ln_rs = self.sem("ln_rs")
        self.ln_xn = self.sem("ln_xn")
        self.ln_tr = self.sem("ln_tr")
        self.ln_ev = self.sem("ln_ev")
        self.part_sems = []

    def sb(self, name, shape, dt=F32, ctx=None):
        return (ctx or self.ctx).enter_context(self.nc.sbuf_tensor(name, shape, dt))

    def sem(self, name):
        handle = self.nc.alloc_semaphore(name=name)
        self.part_sems.append(handle)
        return handle

    def end_part(self):
        self.nc.clear_and_free_semaphores(self.part_sems)
        self.nc.all_engine_barrier()
        self.part_sems = []

    def wait_alone(self, engine, sem, value):
        engine.wait_ge(sem, value)
        engine.sem_inc(self.passed, 1)

    def norm_vector(self, L, c):
        nc, v = self.nc, self.nc.vector
        tile = lambda i: self.X[:, bass.ds(c * CT + i, 1), :]
        for i in range(CT):
            last = v.bn_stats(self.stats[:, i, :], tile(i))
        last.then_inc(self.ln_st, 1)
        self.wait_alone(v, self.ln_st, L + 1)
        for i in range(CT):
            last = v.bn_aggr(self.meanvar[:, i, :], self.stats[:, i, :])
        last.then_inc(self.ln_mv, 1)
        v.wait_ge(self.ln_mv, L + 1)
        v.tensor_scalar(self.veps[:], self.meanvar[:, :, 1], EPS, None, ALU.add).then_inc(self.ln_ve, 1)
        v.wait_ge(self.ln_rs, L + 1)
        if not isinstance(L, int) or L > 0:
            v.wait_ge(self.ln_tr, L)
        for i in range(CT):
            last = v.tensor_scalar(self.xn[:, i, :], tile(i), self.meanvar[:, i, 0:1], self.rstd[:, i:i + 1],
                                   ALU.subtract, ALU.mult)
        last.then_inc(self.ln_xn, 1)

    def norm_pool(self, L):
        self.nc.gpsimd.wait_ge(self.ln_ve, L + 1)
        self.nc.gpsimd.tensor_tensor(self.rstd[:], self.veps[:], self.mhalf[:, 0:CT], ALU.pow)\
            .then_inc(self.ln_rs, 1)

    def norm_tensor(self, L):
        pe = self.nc.tensor
        pe.wait_ge(self.ln_xn, L + 1)
        if not isinstance(L, int) or L > 0:
            pe.wait_ge(self.ln_ev, L)
        for i in range(CT):
            last = pe.transpose(self.bank[7][:, i * P:(i + 1) * P], self.xn[:, i, :], self.ident[:])
        last.then_inc(self.ln_tr, 1)

    def norm_scalar(self, L, dst):
        self.nc.scalar.wait_ge(self.ln_tr, L + 1)
        self.nc.scalar.activation(dst, self.bank[7][:], ACT.Copy).then_inc(self.ln_ev, 1)


def constants(k):
    nc = k.nc
    loaded, zeroed, made = k.sem("x_loaded"), k.sem("const_zeroed"), k.sem("const_made")
    with nc.Block() as block:
        @block.sync
        def _(sp):
            sp.dma_start(k.X[:], k.t["x"].rearrange("(t p) d -> p t d", p=P)).then_inc(loaded, 16)
            sp.wait_ge(loaded, 16)

        @block.gpsimd
        def _(pool):
            nc.gpsimd.memset(k.ident[:], 0.0)
            nc.gpsimd.memset(k.ones[:], 1.0)
            nc.gpsimd.memset(k.mhalf[:], -0.5).then_inc(zeroed, 1)
            pool.wait_ge(zeroed, 1)
            nc.gpsimd.affine_select(out=k.ident[:], in_=k.ident[:], compare_op=ALU.not_equal, fill=1.0, base=0,
                                    pattern=[[-1, P]], channel_multiplier=1).then_inc(made, 1)

        @block.vector
        def _(dve):
            dve.wait_ge(made, 1)
            nc.vector.tensor_copy(k.identb[:], k.ident[:])


def mamba(k):
    nc, t, N, C = k.nc, k.t, k.N, k.C
    DI = t["in_proj_w"].shape[1] // 2
    H = DI // P
    NS = t["A_log"].shape[1]
    R = t["dt_proj_w"].shape[0]
    FB = t["ffn_w1"].shape[1] // P
    KC = t["conv_w"].shape[1]
    PAD = KC - 1
    L0 = k.L
    bank = k.bank
    tmp = ExitStack()
    sb = lambda name, shape, dt=F32: k.sb(name, shape, dt, tmp)
    with tmp:
        inw = sb("inw", [P, 2 * DI])
        g1 = sb("g1", [P, 1])
        b1 = sb("b1", [P, 1])
        g2 = sb("g2", [P, 1])
        b2 = sb("b2", [P, 1])
        cw = sb("cw", [P, H, KC])
        cb = sb("cb", [P, H])
        xpw = sb("xpw", [P, H, R + 2 * NS])
        xpw3 = sb("xpw3", [P, H, 3, 2 * NS])
        dtw = sb("dtw", [R, DI])
        dtb = sb("dtb", [P, H])
        A = sb("A", [P, H, NS])
        Dp = sb("Dp", [P, H])
        outw = sb("outw", [P, H, P])
        w1 = sb("m_w1", [P, FB * P])
        w1b = sb("m_w1b", [P, FB])
        w2 = sb("m_w2", [P, FB, P])
        w2b = sb("m_w2b", [1, P])
        xo = sb("xo", [P, k.T, P])
        xi = sb("xi", [P, H, PAD + N])
        sz = sb("sz", [P, H, N])
        xc = sb("xc", [P, H, N])
        dt = sb("dt", [P, H, N])
        dtx = sb("dtx", [P, H, N])
        BC3 = sb("BC3", [96, N], BF16)
        sel = sb("sel", [96, 2 * NS, P], BF16)
        rt1 = sb("rt1", [96, CW])
        rt2 = sb("rt2", [96, CW])
        hib = sb("hib", [96, CW], BF16)
        midb = sb("midb", [96, CW], BF16)
        lr = sb("lr", [R, CW])
        dA = sb("dA", [P, 2, H, CW])
        dBx = sb("dBx", [P, 2, H, CW])
        h = sb("h", [P, 2, H, CW])
        hC = sb("hC", [P, 2, H, CW])
        Cs = sb("Cs", [P, 2, CW])
        state = sb("state", [P, NS, H])
        r2 = sb("r2", [P, CT])

        wl, sel0, selm = k.sem("m_weights"), k.sem("m_sel_zeroed"), k.sem("m_sel_made")
        s_r2 = k.sem("m_r2")
        s_ve2 = k.sem("m_ve2")
        s_xo = k.sem("m_xo")
        s_un = k.sem("m_un")
        s_in = k.sem("m_in")
        s_inev = k.sem("m_inev")
        s_cv = k.sem("m_conv")
        s_xc = k.sem("m_xc")
        s_xd = k.sem("m_xd")
        s_xde = k.sem("m_xde")
        s_bc = k.sem("m_bc")
        s_dtm = k.sem("m_dtm")
        s_dta = k.sem("m_dta")
        s_sp = k.sem("m_softplus")
        s_dt = k.sem("m_dt")
        s_dtx = k.sem("m_dtx")
        s_A = k.sem("m_A")

        wloads = [
            (inw[:], t["in_proj_w"]), (g1[:], t["ln1_g"].rearrange("(p o) -> p o", o=1)),
            (b1[:], t["ln1_b"].rearrange("(p o) -> p o", o=1)), (g2[:], t["ln2_g"].rearrange("(p o) -> p o", o=1)),
            (b2[:], t["ln2_b"].rearrange("(p o) -> p o", o=1)),
            (cw[:], t["conv_w"].rearrange("(h p) k -> p h k", p=P)),
            (cb[:], t["conv_b"].rearrange("(h p) -> p h", p=P)),
            (xpw[:], t["x_proj_w"].rearrange("(h p) k -> p h k", p=P)),
            (dtw[:], t["dt_proj_w"]), (dtb[:], t["dt_proj_b"].rearrange("(h p) -> p h", p=P)),
            (A[:], t["A_log"].rearrange("(h p) n -> p h n", p=P)), (Dp[:], t["D"].rearrange("(h p) -> p h", p=P)),
            (outw[:], t["out_proj_w"].rearrange("(h p) d -> p h d", p=P)),
            (w1[:], t["ffn_w1"]), (w1b[:], t["ffn_b1"].rearrange("(f p) -> p f", p=P)),
            (w2[:], t["ffn_w2"].rearrange("(f p) d -> p f d", p=P)),
            (w2b[:], t["ffn_b2"].rearrange("(o d) -> o d", o=1)),
        ]

        with nc.Block() as block:
            @block.sync
            def _(sp):
                with nc.allow_non_contiguous_dma(reason="small weights"):
                    for dst, src in wloads:
                        sp.dma_start(dst, src).then_inc(wl, 16)

            @block.gpsimd
            def _(pool):
                nc.gpsimd.memset(sel[:], 0.0)
                nc.gpsimd.memset(state[:], 0.0)
                nc.gpsimd.memset(xi[:, :, 0:PAD], 0.0).then_inc(sel0, 1)
                pool.wait_ge(sel0, 1)
                for part in range(3):
                    last = nc.gpsimd.affine_select(out=sel[:], in_=sel[:], compare_op=ALU.not_equal, fill=1.0,
                                                   base=-32 * part, pattern=[[-1, 2 * NS], [0, P]],
                                                   channel_multiplier=1)
                    last.then_inc(selm, 1)
                    pool.wait_ge(selm, part + 1)
                for c in range(C):
                    k.norm_pool(L0 + c)
                    pool.wait_ge(s_ve2, c + 1)
                    nc.gpsimd.tensor_tensor(r2[:], r2[:], k.mhalf[:, 0:CT], ALU.pow).then_inc(s_r2, 1)

            @block.vector
            def _(dve):
                dve.wait_ge(wl, 16 * len(wloads))
                for p in range(3):
                    last = nc.vector.tensor_copy(xpw3[:, :, p, :], xpw[:, :, R:R + 2 * NS])
                last.then_inc(s_A, 1)

                def norm(c):
                    L = L0 + c
                    v = nc.vector
                    tile = lambda i: k.X[:, c * CT + i, :]
                    for i in range(CT):
                        last = v.bn_stats(k.stats[:, i, :], tile(i))
                    last.then_inc(k.ln_st, 1)
                    v.wait_ge(k.ln_st, L + 1)
                    for i in range(CT):
                        last = v.bn_aggr(k.meanvar[:, i, :], k.stats[:, i, :])
                    last.then_inc(k.ln_mv, 1)
                    v.wait_ge(k.ln_mv, L + 1)
                    v.tensor_scalar(k.veps[:], k.meanvar[:, :, 1], EPS, None, ALU.add).then_inc(k.ln_ve, 1)
                    v.wait_ge(k.ln_rs, L + 1)
                    for i in range(CT):
                        last = v.tensor_scalar(xo[:, c * CT + i, :], tile(i), k.meanvar[:, i, 0:1],
                                               k.rstd[:, i:i + 1], ALU.subtract, ALU.mult)
                    last.then_inc(s_xo, 1)
                    v.tensor_tensor(r2[:], k.meanvar[:, :, 1], k.rstd[:], ALU.mult).then_inc(s_un, 1)
                    v.wait_ge(s_un, 3 * c + 1)
                    v.tensor_tensor(r2[:], r2[:], k.rstd[:], ALU.mult).then_inc(s_un, 1)
                    v.wait_ge(s_un, 3 * c + 2)
                    v.tensor_scalar(r2[:], r2[:], EPS, None, ALU.add).then_inc(s_ve2, 1)
                    v.wait_ge(s_r2, c + 1)
                    v.wait_ge(s_xo, c + 1)
                    if c:
                        v.wait_ge(k.ln_tr, L)
                    for i in range(CT):
                        last = v.tensor_scalar(k.xn[:, i, :], xo[:, c * CT + i, :], r2[:, i:i + 1], None, ALU.mult)
                    last.then_inc(k.ln_xn, 1)
                    v.nop().then_inc(s_un, 1)

                def conv(c):
                    a = PAD + c * CW
                    for hh in range(H):
                        acc = xc[:, hh, c * CW:(c + 1) * CW]
                        dve.wait_ge(s_inev, 2 * H * c + hh + 1)
                        n0 = KC * (c * H + hh)
                        nc.vector.tensor_scalar(acc, xi[:, hh, a - PAD:a - PAD + CW], cw[:, hh, 0:1],
                                                cb[:, hh:hh + 1], ALU.mult, ALU.add).then_inc(s_cv, 1)
                        for j in range(1, KC):
                            dve.wait_ge(s_cv, n0 + j)
                            nc.vector.scalar_tensor_tensor(
                                out=acc, in0=xi[:, hh, a - PAD + j:a - PAD + j + CW], scalar=cw[:, hh, j:j + 1],
                                in1=acc, op0=ALU.mult, op1=ALU.add).then_inc(s_cv, 1)

                def split(c):
                    cs = slice(c * CW, (c + 1) * CW)
                    v = nc.vector
                    dve.wait_ge(s_xd, 2 * c + 1)
                    n0 = 8 * c
                    v.tensor_copy(hib[:], bank[4][0:96, :]).then_inc(s_bc, 1)
                    dve.wait_ge(s_bc, n0 + 1)
                    v.tensor_tensor(rt1[:], bank[4][0:96, :], hib[:], ALU.subtract).then_inc(s_bc, 1)
                    v.tensor_copy(BC3[0:32, cs], hib[0:32, :]).then_inc(s_bc, 1)
                    dve.wait_ge(s_bc, n0 + 2)
                    v.tensor_copy(midb[:], rt1[:]).then_inc(s_bc, 1)
                    dve.wait_ge(s_bc, n0 + 4)
                    v.tensor_tensor(rt2[:], rt1[:], midb[:], ALU.subtract).then_inc(s_bc, 1)
                    v.tensor_copy(BC3[32:64, cs], midb[32:64, :]).then_inc(s_bc, 1)
                    dve.wait_ge(s_bc, n0 + 5)
                    v.tensor_copy(BC3[64:96, cs], rt2[64:96, :]).then_inc(s_bc, 1)
                    dve.wait_ge(s_xd, 2 * c + 2)
                    v.tensor_copy(lr[:], bank[5][0:R, :]).then_inc(s_bc, 1)

                for c in range(C):
                    norm(c)
                    conv(c)
                    split(c)
                for c in range(C):
                    cs = slice(c * CW, (c + 1) * CW)
                    dve.wait_ge(s_sp, 2)
                    nc.vector.tensor_tensor(dt[:, :, cs], dt[:, :, cs], dtx[:, :, cs], ALU.add).then_inc(s_dt, 1)
                    dve.wait_ge(s_dt, c + 1)
                    nc.vector.tensor_tensor(dtx[:, :, cs], dt[:, :, cs], xc[:, :, cs], ALU.mult)

            @block.tensor
            def _(pe):
                pe.wait_ge(wl, 16 * len(wloads))
                pe.wait_ge(s_A, 1)
                for c in range(C):
                    cs = slice(c * CW, (c + 1) * CW)
                    k.norm_tensor(L0 + c)
                    pe.wait_ge(k.ln_ev, L0 + c + 1)
                    if c:
                        pe.wait_ge(s_inev, 2 * H * c)
                    for b in range(2 * H):
                        nc.tensor.matmul(bank[b][:], inw[:, b * P:(b + 1) * P], k.xnT[:, cs], start=True, stop=True)\
                            .then_inc(s_in, 1)
                    pe.wait_ge(s_xc, c + 1)
                    if c:
                        pe.wait_ge(s_bc, 8 * c)
                        pe.wait_ge(s_dta, 2 * H * c)
                    for hh in range(H):
                        last = nc.tensor.matmul(bank[4][0:96, :], xpw3[:, hh].rearrange("p a b -> p (a b)"),
                                                xc[:, hh, cs], start=(hh == 0), stop=(hh == H - 1))
                    last.then_inc(s_xd, 1)
                    for hh in range(H):
                        last = nc.tensor.matmul(bank[5][0:R, :], xpw[:, hh, 0:R], xc[:, hh, cs],
                                                start=(hh == 0), stop=(hh == H - 1))
                    last.then_inc(s_xd, 1)
                    pe.wait_ge(s_bc, 8 * c + 8)
                    for hh in range(H):
                        if hh or c:
                            pe.wait_ge(s_dta, 2 * (c * H + hh))
                        nc.tensor.matmul(bank[6][:], dtw[:, hh * P:(hh + 1) * P], lr[:], start=True, stop=True)\
                            .then_inc(s_dtm, 1)

            @block.scalar
            def _(act):
                act.wait_ge(wl, 16 * len(wloads))
                act.wait_ge(sel0, 1)
                for c in range(C):
                    cs = slice(c * CW, (c + 1) * CW)
                    act.wait_ge(k.ln_tr, L0 + c + 1)
                    nc.scalar.activation(k.xnT[:, cs], bank[7][:], ACT.Identity, bias=b1[:], scale=g1[:])\
                        .then_inc(k.ln_ev, 1)
                    for b in range(2 * H):
                        act.wait_ge(s_in, 2 * H * c + b + 1)
                        if b < H:
                            nc.scalar.activation(xi[:, b, PAD + c * CW:PAD + (c + 1) * CW], bank[b][:], ACT.Copy)\
                                .then_inc(s_inev, 1)
                        else:
                            nc.scalar.activation(sz[:, b - H, cs], bank[b][:], ACT.Silu).then_inc(s_inev, 1)
                    act.wait_ge(s_cv, KC * H * (c + 1))
                    nc.scalar.activation(xc[:, :, cs], xc[:, :, cs], ACT.Silu).then_inc(s_xc, 1)
                    for hh in range(H):
                        act.wait_ge(s_dtm, c * H + hh + 1)
                        nc.scalar.activation(dt[:, hh, cs], bank[6][:], ACT.Relu, bias=dtb[:, hh:hh + 1])\
                            .then_inc(s_dta, 1)
                        nc.scalar.activation(dtx[:, hh, cs], bank[6][:], ACT.Abs, bias=dtb[:, hh:hh + 1])\
                            .then_inc(s_dta, 1)
                act.wait_ge(s_dta, 2 * H * C)
                nc.scalar.activation(dtx[:], dtx[:], ACT.Exp, scale=-1.0).then_inc(s_sp, 1)
                nc.scalar.activation(A[:], A[:], ACT.Exp).then_inc(s_A, 1)
                act.wait_ge(s_sp, 1)
                nc.scalar.activation(dtx[:], dtx[:], ACT.Ln, bias=1.0).then_inc(s_sp, 1)
                act.wait_ge(s_A, 2)
                nc.scalar.mul(A[:], A[:], -1.0)
        k.L += C

        q_bc = k.sem("q_bc")
        q_dA = k.sem("q_dA")
        q_cs = k.sem("q_cs")
        q_dBx = k.sem("q_dBx")
        q_h = k.sem("q_h")
        q_hC = k.sem("q_hC")
        q_st = k.sem("q_st")
        q_y = k.sem("q_y")
        q_yc = k.sem("q_yc")
        q_yg = k.sem("q_yg")
        yT = sb("yT", [P, H, CW])
        o_mm = k.sem("o_mm")
        o_x1 = k.sem("o_x1")
        x1 = xo
        assert H == 2
        with nc.Block() as block:
            def y_sum(pe, c, n):
                pe.wait_ge(q_hC, c * NS + n + 1)
                for hh in range(H):
                    last = nc.tensor.matmul(bank[4 + hh][:], k.ident[:], hC[:, n % 2, hh, :],
                                            start=(n == 0), stop=(n == NS - 1))
                last.then_inc(q_y, 1)

            @block.tensor
            def _(pe):
                nc.tensor.sem_inc(q_bc, 4)
                nc.tensor.sem_inc(q_y, 1)
                with pe.Fori(0, C) as c:
                    for n in range(NS):
                        u = c * NS + n
                        if n >= 2:
                            pe.wait_ge(q_dBx, u - 1)
                            pe.wait_ge(q_cs, u - 1)
                        for j in range(2):
                            nc.tensor.matmul(bank[2 * j + n % 2][:], sel[:, j * NS + n, :],
                                             BC3[:, bass.ds(c * CW, CW)], start=True, stop=True).then_inc(q_bc, 1)
                        if n >= 1:
                            y_sum(pe, c, n - 1)
                    y_sum(pe, c, NS - 1)
                    pe.wait_ge(q_yg, c + 1)
                    for i in range(CT):
                        for hh in range(H):
                            last = nc.tensor.matmul(bank[6][:, i * P:(i + 1) * P], yT[:, hh, i * P:(i + 1) * P],
                                                    outw[:, hh, :], start=(hh == 0), stop=(hh == H - 1))
                    last.then_inc(o_mm, 1)
                    pe.wait_ge(o_x1, c + 1)

            @block.scalar
            def _(act):
                with act.Fori(0, C) as c:
                    for n in range(NS):
                        u = c * NS + n
                        if n >= 2:
                            k.wait_alone(act, q_h, 2 * u - 2)
                        for hh in range(H):
                            nc.scalar.activation(dA[:, n % 2, hh, :], dt[:, hh, bass.ds(c * CW, CW)], ACT.Exp,
                                                 scale=A[:, hh, n:n + 1]).then_inc(q_dA, 1)
                        act.wait_ge(q_bc, 2 * u + 2 + 4)
                        if n >= 2:
                            act.wait_ge(q_hC, u - 1)
                        nc.scalar.activation(Cs[:, n % 2, :], bank[2 + n % 2][:], ACT.Copy).then_inc(q_cs, 1)
                    act.wait_ge(q_hC, c * NS + NS)

            @block.vector
            def _(dve):
                with dve.Fori(0, C) as c:
                    for n in range(NS):
                        u = c * NS + n
                        dve.wait_ge(q_bc, 2 * u + 1 + 4)
                        nc.vector.tensor_tensor(dBx[:, n % 2], dtx[:, :, bass.ds(c * CW, CW)],
                                                bank[n % 2][:, None, :].to_broadcast([P, H, CW]), ALU.mult)\
                            .then_inc(q_dBx, 1)
                        dve.wait_ge(q_dBx, u + 1)
                        dve.wait_ge(q_dA, 2 * u + 2)
                        if n >= 2:
                            dve.wait_ge(q_hC, u - 1)
                            dve.wait_ge(q_st, u - 1)
                        for hh in range(H):
                            nc.vector.tensor_tensor_scan(h[:, n % 2, hh, :], dA[:, n % 2, hh, :], dBx[:, n % 2, hh, :],
                                                         state[:, n, hh:hh + 1], ALU.mult, ALU.add).then_inc(q_h, 1)
                    dve.wait_ge(q_y, c * NS + NS + 1)
                    for hh in range(H):
                        nc.vector.scalar_tensor_tensor(out=yT[:, hh, :], in0=xc[:, hh, bass.ds(c * CW, CW)],
                                                       scalar=Dp[:, hh:hh + 1], in1=bank[4 + hh][:],
                                                       op0=ALU.mult, op1=ALU.add).then_inc(q_yc, 1)
                    dve.wait_ge(q_yc, 2 * c + 2)
                    nc.vector.tensor_tensor(yT[:], yT[:], sz[:, :, bass.ds(c * CW, CW)], ALU.mult).then_inc(q_yg, 1)
                    dve.wait_ge(o_mm, c + 1)
                    xt = x1[:, bass.ds(c * CT, CT), :]
                    nc.vector.tensor_tensor(xt, bank[6][:].rearrange("p (i d) -> p i d", i=CT), xt, ALU.add)\
                        .then_inc(o_x1, 1)
                    dve.wait_ge(q_st, c * NS + NS)

            @block.gpsimd
            def _(pool):
                with pool.Fori(0, C) as c:
                    for n in range(NS):
                        u = c * NS + n
                        pool.wait_ge(q_h, 2 * u + 2)
                        pool.wait_ge(q_cs, u + 1)
                        if n >= 2:
                            pool.wait_ge(q_y, u - 1 + 1)
                        nc.gpsimd.tensor_tensor(hC[:, n % 2], h[:, n % 2],
                                                Cs[:, n % 2, None, :].to_broadcast([P, H, CW]), ALU.mult)\
                            .then_inc(q_hC, 1)
                        nc.gpsimd.tensor_copy(state[:, n, :], h[:, n % 2, :, CW - 1]).then_inc(q_st, 1)
                    pool.wait_ge(q_y, c * NS + NS + 1)

        hT = [dtx[:].rearrange("p h n -> p (h n)")[:, b * FB * CW:(b + 1) * FB * CW].rearrange("p (f w) -> p f w", f=FB)
              for b in range(2)]
        f_x = k.sem("f_x")
        f_cp = k.sem("f_cp")
        f_h = k.sem("f_h")
        f_ev = k.sem("f_ev")
        f_y = k.sem("f_y")
        L1 = k.L
        with nc.Block() as block:
            @block.gpsimd
            def _(pool):
                for c in range(C):
                    k.norm_pool(L1 + c)

            @block.vector
            def _(dve):
                for c in range(C):
                    xt = k.X[:, c * CT:(c + 1) * CT, :]
                    nc.vector.tensor_tensor(xt, xt, x1[:, c * CT:(c + 1) * CT, :], ALU.add).then_inc(f_x, 1)
                keep, k.X = k.X, x1
                for c in range(C):
                    k.norm_vector(L1 + c, c)
                k.X = keep
                for c in range(C):
                    dve.wait_ge(f_x, c + 1)
                    dve.wait_ge(f_y, c + 1)
                    xt = k.X[:, c * CT:(c + 1) * CT, :]
                    nc.vector.tensor_tensor(xt, bank[4 + c % 2][:].rearrange("p (i d) -> p i d", i=CT), xt, ALU.add)\
                        .then_inc(f_cp, 1)

            @block.tensor
            def _(pe):
                for c in range(C):
                    k.norm_tensor(L1 + c)
                    pe.wait_ge(k.ln_ev, L1 + c + 1)
                    for f in range(FB):
                        if c:
                            pe.wait_ge(f_ev, (c - 1) * FB + f + 1)
                        nc.tensor.matmul(bank[f][:], w1[:, f * P:(f + 1) * P], k.xnT[:, c * CW:(c + 1) * CW],
                                         start=True, stop=True).then_inc(f_h, 1)
                    if c >= 2:
                        pe.wait_ge(f_cp, c - 1)
                    pe.wait_ge(f_ev, c * FB + FB)
                    for i in range(CT):
                        dst = bank[4 + c % 2][:, i * P:(i + 1) * P]
                        nc.tensor.matmul(dst, k.ones[0:1, :], w2b[:], start=True, stop=False)
                        for f in range(FB):
                            last = nc.tensor.matmul(dst, hT[c % 2][:, f, i * P:(i + 1) * P], w2[:, f, :],
                                                    start=False, stop=(f == FB - 1))
                    last.then_inc(f_y, 1)

            @block.scalar
            def _(act):
                for c in range(C):
                    act.wait_ge(k.ln_tr, L1 + c + 1)
                    nc.scalar.activation(k.xnT[:, c * CW:(c + 1) * CW], bank[7][:], ACT.Identity, bias=b2[:],
                                         scale=g2[:]).then_inc(k.ln_ev, 1)
                    for f in range(FB):
                        act.wait_ge(f_h, c * FB + f + 1)
                        if c >= 2:
                            act.wait_ge(f_y, c - 1)
                        nc.scalar.activation(hT[c % 2][:, f, :], bank[f][:], ACT.Gelu_apprx_tanh,
                                             bias=w1b[:, f:f + 1]).then_inc(f_ev, 1)
        k.L += C


def top_two(k, dve, act_sem, src, top, ti, tf, s):
    nc = k.nc
    for i in range(k.T):
        last = nc.vector.max(top[:, i, :], src[:, i, :])
    last.then_inc(s, 1)
    dve.wait_ge(s, act_sem + 1)
    for i in range(k.T):
        last = nc.vector.max_index(ti[:, i, :], top[:, i, :], src[:, i, :])
    last.then_inc(s, 1)
    dve.wait_ge(s, act_sem + 2)
    nc.vector.tensor_copy(tf[:], ti[:, :, 0:2]).then_inc(s, 1)


def experts(k, name, gated):
    nc, t, C, T, E = k.nc, k.t, k.C, k.T, k.E
    L0, bank, pre = k.L, k.bank, name
    FB = t[pre + "_w1"].shape[2] // P
    tmp = ExitStack()
    sb = lambda n, shape, dt=F32: k.sb(f"{name}_{n}", shape, dt, tmp)
    sem = lambda n: k.sem(f"{name}_{n}")
    with tmp:
        gw = sb("gw", [P, E])
        gb = sb("gb", [1, E])
        lg = sb("lg", [P, T, E])
        top = sb("top", [P, T, E])
        ti = sb("ti", [P, T, E], U32)
        tf = sb("tf", [P, T, 2])
        ex = sb("ex", [P, T])
        den = sb("den", [P, T])
        wt = sb("wt", [P, 2, T])
        pick = sb("pick", [P, 2, T])
        comb = sb("comb", [P, E, T])
        wa = [sb(f"wa{u}", [P, FB * P]) for u in range(2)]
        wu = [sb(f"wu{u}", [P, FB * P]) for u in range(2)] if gated else None
        wd = [sb(f"wd{u}", [P, FB, P]) for u in range(2)]
        ba = None if gated else [sb(f"ba{u}", [P, FB]) for u in range(2)]
        bd = None if gated else [sb(f"bd{u}", [1, P]) for u in range(2)]
        sg = sb("sg", [P, 2, CW]) if gated else None
        hT = [sb(f"hT{b}", [P, FB, CW]) for b in range(2)]
        NH = 2 if gated else 4
        ND = 3 if gated else 4

        g_w, g_mm, g_top, g_ex, g_cb = sem("gate_w"), sem("gate_mm"), sem("gate_top"), sem("gate_ex"), sem("gate_cb")
        w_ready = [sem(f"w_ready{u}") for u in range(2)]
        s_h, s_sg, s_hev, s_y, s_x, s_e = (sem(n) for n in ("h", "sg", "hev", "y", "x", "e_done"))

        with nc.Block() as block:
            @block.sync
            def _(sp):
                sp.dma_start(gw[:], t[pre + "_gate_w"]).then_inc(g_w, 16)
                if not gated:
                    sp.dma_start(gb[:], t[pre + "_gate_b"].rearrange("(o e) -> o e", o=1)).then_inc(g_w, 16)

            @block.gpsimd
            def _(pool):
                for c in range(C):
                    k.norm_pool(L0 + c)

            @block.scalar
            def _(act):
                for c in range(C):
                    k.norm_scalar(L0 + c, k.xnT[:, c * CW:(c + 1) * CW])
                act.wait_ge(g_cb, 2)
                nc.scalar.activation(ex[:], den[:], ACT.Exp).then_inc(g_ex, 1)

            @block.tensor
            def _(pe):
                pe.wait_ge(g_w, 16 if gated else 32)
                for c in range(C):
                    k.norm_tensor(L0 + c)
                    pe.wait_ge(k.ln_ev, L0 + c + 1)
                    for i in range(c * CT, (c + 1) * CT):
                        dst = bank[6][:, i * E:(i + 1) * E]
                        last = nc.tensor.matmul(dst, k.xnT[:, i * P:(i + 1) * P], gw[:], start=True, stop=gated)
                        if not gated:
                            last = nc.tensor.matmul(dst, k.ones[0:1, :], gb[:], start=False, stop=True)
                last.then_inc(g_mm, 1)

            @block.vector
            def _(dve):
                for c in range(C):
                    k.norm_vector(L0 + c, c)
                dve.wait_ge(g_mm, 1)
                nc.vector.tensor_copy(lg[:], bank[6][:, 0:T * E].rearrange("p (t e) -> p t e", t=T)).then_inc(g_cb, 1)
                dve.wait_ge(g_cb, 1)
                top_two(k, dve, 0, lg, top, ti, tf, g_top)
                nc.vector.tensor_tensor(den[:], top[:, :, 1], top[:, :, 0], ALU.subtract).then_inc(g_cb, 1)
                dve.wait_ge(g_ex, 1)
                nc.vector.tensor_scalar(den[:], ex[:], 1.0, None, ALU.add).then_inc(g_cb, 1)
                dve.wait_ge(g_cb, 3)
                nc.vector.reciprocal(wt[:, 0, :], den[:]).then_inc(g_cb, 1)
                dve.wait_ge(g_cb, 4)
                nc.vector.tensor_tensor(wt[:, 1, :], ex[:], wt[:, 0, :], ALU.mult).then_inc(g_cb, 1)
                dve.wait_ge(g_cb, 5)
                dve.wait_ge(g_top, 3)
                for e in range(E):
                    if e:
                        dve.wait_ge(g_cb, 5 + 2 * e)
                    for j in range(2):
                        last = nc.vector.scalar_tensor_tensor(out=pick[:, j, :], in0=tf[:, :, j], scalar=float(e),
                                                              in1=wt[:, j, :], op0=ALU.is_equal, op1=ALU.mult)
                    last.then_inc(g_cb, 1)
                    dve.wait_ge(g_cb, 6 + 2 * e)
                    nc.vector.tensor_tensor(comb[:, e, :], pick[:, 0, :], pick[:, 1, :], ALU.add).then_inc(g_cb, 1)
        k.L += C

        with nc.Block() as block:
            @block.sync
            def _(sp):
                with nc.allow_non_contiguous_dma(reason="bias columns"):
                    with sp.Fori(0, E // 2) as ep:
                        for u in range(2):
                            e = ep * 2 + u
                            sp.wait_ge(s_e, e + 1)
                            one = lambda n: t[pre + n][bass.ds(e, 1)]
                            loads = [(wa[u][:], one("_w1").rearrange("o p f -> (o p) f")),
                                     (wd[u][:], one("_w2").rearrange("o (f p) d -> (o p) f d", p=P))]
                            if gated:
                                loads.append((wu[u][:], one("_wu").rearrange("o p f -> (o p) f")))
                            else:
                                loads.append((ba[u][:], one("_b1").rearrange("o (f p) -> (o p) f", p=P)))
                                loads.append((bd[u][:], one("_b2")))
                            for dst, src in loads:
                                sp.dma_start(dst, src).then_inc(w_ready[u], 16)

            @block.tensor
            def _(pe):
                nc.tensor.sem_inc(s_e, 2)
                nc.tensor.sem_inc(s_y, 2)

                def hidden(ep, u, c):
                    q = (ep * 2 + u) * C + c
                    if c == 0:
                        pe.wait_ge(w_ready[u], (ep + 1) * (16 * ND))
                    for f in range(FB):
                        pe.wait_ge(s_hev, q * FB + f + 1)
                        xc = k.xnT[:, c * CW:(c + 1) * CW]
                        last = nc.tensor.matmul(bank[f % NH][:], wa[u][:, f * P:(f + 1) * P], xc, start=True, stop=True)
                        if gated:
                            last.then_inc(s_h, 1)
                            last = nc.tensor.matmul(bank[2 + f % 2][:], wu[u][:, f * P:(f + 1) * P], xc,
                                                    start=True, stop=True)
                        last.then_inc(s_h, 1)

                def down(ep, u, c):
                    q = (ep * 2 + u) * C + c
                    pe.wait_ge(s_hev, q * FB + FB + NH)
                    pe.wait_ge(s_x, q + 1)
                    for i in range(CT):
                        dst = bank[4 + c % 2][:, i * P:(i + 1) * P]
                        if not gated:
                            nc.tensor.matmul(dst, k.ones[0:1, :], bd[u][:], start=True, stop=False)
                        for f in range(FB):
                            last = nc.tensor.matmul(dst, hT[c % 2][:, f, i * P:(i + 1) * P], wd[u][:, f, :],
                                                    start=(gated and f == 0), stop=(f == FB - 1))
                    last.then_inc(s_y, 1)

                with pe.Fori(0, E // 2) as ep:
                    units = [(u, c) for u in range(2) for c in range(C)]
                    hidden(ep, *units[0])
                    for n, unit in enumerate(units):
                        if n + 1 < len(units):
                            hidden(ep, *units[n + 1])
                        down(ep, *unit)
                        if unit[1] == C - 1:
                            nc.tensor.drain().then_inc(s_e, 1)

            @block.scalar
            def _(act):
                if not gated:
                    nc.scalar.sem_inc(s_hev, NH)
                with act.Fori(0, E // 2) as ep:
                    for u in range(2):
                        for c in range(C):
                            q = (ep * 2 + u) * C + c
                            for f in range(FB):
                                b = q * FB + f
                                if gated:
                                    act.wait_ge(s_hev, b + 1)
                                    act.wait_ge(s_h, 2 * b + 1)
                                    nc.scalar.activation(sg[:, f % 2, :], bank[f % 2][:], ACT.Silu).then_inc(s_sg, 1)
                                else:
                                    if f == 0:
                                        act.wait_ge(s_y, q + 1)
                                    act.wait_ge(s_h, b + 1)
                                    nc.scalar.activation(hT[c % 2][:, f, :], bank[f][:], ACT.Relu,
                                                         bias=ba[u][:, f:f + 1]).then_inc(s_hev, 1)

            @block.vector
            def _(dve):
                nc.vector.sem_inc(s_x, 2)
                if gated:
                    nc.vector.sem_inc(s_hev, NH)

                def up(ep, u, c):
                    q = (ep * 2 + u) * C + c
                    for f in range(FB):
                        b = q * FB + f
                        if f == 0:
                            dve.wait_ge(s_y, q + 1)
                        dve.wait_ge(s_h, 2 * b + 2)
                        dve.wait_ge(s_sg, b + 1)
                        nc.vector.tensor_tensor(hT[c % 2][:, f, :], bank[2 + f % 2][:], sg[:, f % 2, :], ALU.mult)\
                            .then_inc(s_hev, 1)

                def add(ep, u, c):
                    e = ep * 2 + u
                    q = e * C + c
                    dve.wait_ge(s_x, q + 1)
                    dve.wait_ge(s_y, q + 1 + 2)
                    for i in range(CT):
                        xt = k.X[:, c * CT + i, :]
                        last = nc.vector.scalar_tensor_tensor(
                            out=xt, in0=bank[4 + c % 2][:, i * P:(i + 1) * P],
                            scalar=comb[:, bass.ds(e, 1), c * CT + i], in1=xt, op0=ALU.mult, op1=ALU.add)
                    last.then_inc(s_x, 1)

                with dve.Fori(0, E // 2) as ep:
                    units = [(u, c) for u in range(2) for c in range(C)]
                    if gated:
                        up(ep, *units[0])
                    for n, unit in enumerate(units):
                        if gated and n + 1 < len(units):
                            up(ep, *units[n + 1])
                        add(ep, *unit)


def linear(k):
    nc, t, C, T = k.nc, k.t, k.C, k.T
    L0, bank = k.L, k.bank
    EPSA = 1e-6
    tmp = ExitStack()
    sb = lambda n, shape, dt=F32: k.sb("lin_" + n, shape, dt, tmp)
    sem = lambda n: k.sem("lin_" + n)
    with tmp:
        wqk, bqk, wv = sb("wqk", [P, 2 * P]), sb("bqk", [1, 2 * P]), sb("wv", [P, P])
        bv, gam = sb("bv", [P, 1]), sb("gam", [P, 1])
        qk, sq = sb("qk", [P, 2, 2 * P]), sb("sq", [P, 2, 2 * P])
        half = sb("half", [P, P])
        sums = sb("sums", [P, 2 * P])
        nk = sb("nk", [P, 1])
        Gn, tl, H, M = (sb(n, [P, P]) for n in ("Gn", "tl", "H", "M"))
        rrow = sb("rrow", [1, P])
        lw, s_qk, s_ev, s_g, s_p, s_v, s_m, s_h = (sem(n) for n in ("w", "qk", "ev", "g", "pow", "v", "m", "half"))
        s_o, s_x = sem("o"), sem("x")
        with nc.Block() as block:
            @block.sync
            def _(sp):
                with nc.allow_non_contiguous_dma(reason="small weights"):
                    for dst, src in ((wqk[:, 0:P], t["lin_wqT"]), (wqk[:, P:2 * P], t["lin_wkT"]), (wv[:], t["lin_wv"]),
                                     (bqk[:, 0:P], t["lin_bq"].rearrange("(o d) -> o d", o=1)),
                                     (bqk[:, P:2 * P], t["lin_bk"].rearrange("(o d) -> o d", o=1)),
                                     (bv[:], t["lin_bv"].rearrange("(d o) -> d o", o=1)),
                                     (gam[:], t["lin_gamma"].partition_broadcast(P))):
                        sp.dma_start(dst, src).then_inc(lw, 16)

            @block.gpsimd
            def _(pool):
                nc.gpsimd.memset(half[:], -0.5).then_inc(s_h, 1)
                for c in range(C):
                    k.norm_pool(L0 + c)
                pool.wait_ge(s_h, 1)
                pool.wait_ge(s_v, 2)
                nc.gpsimd.tensor_tensor(sums[:, P:2 * P], sums[:, P:2 * P], half[:], ALU.pow).then_inc(s_p, 1)
                nc.gpsimd.tensor_tensor(nk[:], nk[:], half[:, 0:1], ALU.pow).then_inc(s_p, 1)

            @block.scalar
            def _(act):
                for c in range(C):
                    k.norm_scalar(L0 + c, k.xnT[:, c * CW:(c + 1) * CW])
                    for i in range(c * CT, (c + 1) * CT):
                        act.wait_ge(s_qk, i + 1)
                        if i >= 2:
                            act.wait_ge(s_g, i - 1)
                        nc.scalar.activation(qk[:, i % 2, :], bank[i % 2][:, 0:2 * P], ACT.Copy).then_inc(s_ev, 1)
                        nc.scalar.activation(sq[:, i % 2, :], bank[i % 2][:, 0:2 * P], ACT.Square).then_inc(s_ev, 1)

            @block.tensor
            def _(pe):
                pe.wait_ge(lw, 16 * 7)

                def gram(i):
                    pe.wait_ge(s_ev, 2 * i + 2)
                    q, kk, q2, k2 = (a[:, i % 2, b * P:(b + 1) * P] for a in (qk, sq) for b in range(2))
                    f, z = i == 0, i == T - 1
                    nc.tensor.matmul(bank[2][:, 0:P], kk, q, start=f, stop=z)
                    nc.tensor.matmul(bank[3][:, 0:P], k.ones[:], q, start=f, stop=z)
                    nc.tensor.matmul(bank[4][:, 0:P], k.ones[:], q2, start=f, stop=z)
                    nc.tensor.matmul(bank[5][:, 0:1], k2, k.ones[:, 0:1], start=f, stop=z).then_inc(s_g, 1)

                for c in range(C):
                    k.norm_tensor(L0 + c)
                    pe.wait_ge(k.ln_ev, L0 + c + 1)
                    for i in range(c * CT, (c + 1) * CT):
                        if i >= 2:
                            pe.wait_ge(s_ev, 2 * i - 2)
                        nc.tensor.matmul(bank[i % 2][:, 0:2 * P], k.xnT[:, i * P:(i + 1) * P], wqk[:], start=True, stop=False)
                        nc.tensor.matmul(bank[i % 2][:, 0:2 * P], k.ones[0:1, :], bqk[:], start=False, stop=True)\
                            .then_inc(s_qk, 1)
                        if i:
                            gram(i - 1)
                gram(T - 1)
                pe.wait_ge(s_v, 3)
                nc.tensor.matmul(bank[3][:, 0:P], k.ones[:], Gn[:], start=True, stop=True).then_inc(s_m, 1)
                pe.wait_ge(s_v, 8)
                nc.tensor.matmul(bank[4][:, 0:P], wv[:], H[:], start=True, stop=True)
                nc.tensor.matmul(bank[5][0:1, 0:P], bv[:], H[:], start=True, stop=True).then_inc(s_m, 1)

            @block.vector
            def _(dve):
                v = nc.vector
                for c in range(C):
                    k.norm_vector(L0 + c, c)
                dve.wait_ge(lw, 16 * 7)
                dve.wait_ge(s_g, T)
                v.tensor_copy(sums[:, 0:P], bank[3][:, 0:P])
                v.tensor_copy(sums[:, P:2 * P], bank[4][:, 0:P]).then_inc(s_v, 1)
                v.tensor_copy(nk[:], bank[5][:, 0:1]).then_inc(s_v, 1)
                dve.wait_ge(s_p, 2)
                v.scalar_tensor_tensor(out=Gn[:], in0=bank[2][:, 0:P], scalar=nk[:], in1=sums[:, P:2 * P],
                                       op0=ALU.mult, op1=ALU.mult).then_inc(s_v, 1)
                dve.wait_ge(s_v, 3)
                v.scalar_tensor_tensor(out=tl[:], in0=sums[:, 0:P], scalar=EPSA, in1=sums[:, P:2 * P],
                                       op0=ALU.mult, op1=ALU.mult).then_inc(s_v, 1)
                dve.wait_ge(s_v, 4)
                dve.wait_ge(s_m, 1)
                v.scalar_tensor_tensor(out=tl[:], in0=tl[:], scalar=float(P), in1=bank[3][:, 0:P],
                                       op0=ALU.add, op1=ALU.add).then_inc(s_v, 1)
                dve.wait_ge(s_v, 5)
                v.reciprocal(tl[:], tl[:]).then_inc(s_v, 1)
                dve.wait_ge(s_v, 6)
                v.scalar_tensor_tensor(out=H[:], in0=Gn[:], scalar=1.0, in1=tl[:], op0=ALU.add, op1=ALU.mult)\
                    .then_inc(s_v, 1)
                dve.wait_ge(s_v, 7)
                v.tensor_scalar(H[:], H[:], gam[:], None, ALU.mult).then_inc(s_v, 1)
                dve.wait_ge(s_m, 2)
                v.tensor_tensor(M[:], bank[4][:, 0:P], k.ident[:], ALU.add)
                v.tensor_copy(rrow[:], bank[5][0:1, 0:P])
        k.L += C
        with nc.Block() as block:
            @block.tensor
            def _(pe):
                for c in range(C):
                    if c >= 2:
                        pe.wait_ge(s_x, c - 1)
                    for i in range(CT):
                        dst = bank[c % 2][:, i * P:(i + 1) * P]
                        a = (c * CT + i) * P
                        nc.tensor.matmul(dst, k.xnT[:, a:a + P], M[:], start=True, stop=False)
                        last = nc.tensor.matmul(dst, k.ones[0:1, :], rrow[:], start=False, stop=True)
                    last.then_inc(s_o, 1)

            @block.vector
            def _(dve):
                for c in range(C):
                    dve.wait_ge(s_o, c + 1)
                    xt = k.X[:, c * CT:(c + 1) * CT, :]
                    nc.vector.tensor_tensor(xt, bank[c % 2][:].rearrange("p (i d) -> p i d", i=CT), xt, ALU.add)\
                        .then_inc(s_x, 1)


def deep(k):
    nc, t, C, T, E = k.nc, k.t, k.C, k.T, k.E
    L0, bank = k.L, k.bank
    tmp = ExitStack()
    sb = lambda n, shape, dt=F32: k.sb("deep_" + n, shape, dt, tmp)
    sem = lambda n: k.sem("deep_" + n)
    with tmp:
        gw, gb = sb("gw", [P, E]), sb("gb", [E, 1])
        w1, w2, w3 = (sb(n, [P, E, P]) for n in ("w1", "w2", "w3"))
        c1, c2, r3 = sb("c1", [P, E]), sb("c2", [P, E]), sb("r3", [1, E, P])
        W = [sb(f"W{i}", [P, 3, P]) for i in range(2)]
        lg = sb("lg", [E, k.N])
        mx, sm = sb("mx", [E, 1]), sb("sm", [E, 1])
        pr, top, ti = sb("pr", [P, T, E]), sb("top", [P, T, E]), sb("ti", [P, T, E], U32)
        tf = sb("tf", [P, T, 2])
        pick = sb("pick", [P, 4, T])
        comb, ind = sb("comb", [P, E, T]), sb("ind", [P, T, E])
        h1 = [sb(f"h1{b}", [P, CW]) for b in range(2)]
        h2 = [sb(f"h2{b}", [P, CW]) for b in range(2)]
        ry = [sb(f"ry{b}", [P, CW]) for b in range(2)]
        vrow, vE = sb("vrow", [1, E, P]), sb("vE", [E, P])
        indT = sb("indT", [E, T, P])
        lw, s_lg, s_lge, s_sm, s_ex, s_pt, s_pc, s_top, s_cb = (
            sem(n) for n in ("w", "lg", "lge", "sm", "ex", "pt", "pc", "top", "cb"))
        with nc.Block() as block:
            @block.sync
            def _(sp):
                with nc.allow_non_contiguous_dma(reason="small weights"):
                    for dst, src in ((gw[:], t["deep_gate_w"]), (gb[:], t["deep_gate_b"].rearrange("(e o) -> e o", o=1)),
                                     (w1[:], t["deep_w1"].rearrange("e p o -> p e o")),
                                     (w2[:], t["deep_w2"].rearrange("e p o -> p e o")),
                                     (w3[:], t["deep_w3"].rearrange("e p o -> p e o")),
                                     (c1[:], t["deep_b1"].rearrange("e p -> p e")),
                                     (c2[:], t["deep_b2"].rearrange("e p -> p e")),
                                     (r3[:], t["deep_b3"].rearrange("(o e) p -> o e p", o=1))):
                        sp.dma_start(dst, src).then_inc(lw, 16)

            @block.gpsimd
            def _(pool):
                for c in range(C):
                    k.norm_pool(L0 + c)

            @block.scalar
            def _(act):
                act.wait_ge(lw, 16 * 8)
                for c in range(C):
                    k.norm_scalar(L0 + c, k.xnT[:, c * CW:(c + 1) * CW])
                    act.wait_ge(s_lg, c + 1)
                    nc.scalar.activation(lg[:, c * CW:(c + 1) * CW], bank[c % 2][0:E, :], ACT.Identity, bias=gb[:])\
                        .then_inc(s_lge, 1)
                act.wait_ge(s_sm, 1)
                nc.scalar.activation(lg[:], lg[:], ACT.Exp, bias=mx[:], accum_out=sm[:]).then_inc(s_ex, 1)

            @block.tensor
            def _(pe):
                pe.wait_ge(lw, 16 * 8)
                for c in range(C):
                    k.norm_tensor(L0 + c)
                    pe.wait_ge(k.ln_ev, L0 + c + 1)
                    if c >= 2:
                        pe.wait_ge(s_lge, c - 1)
                    nc.tensor.matmul(bank[c % 2][0:E, :], gw[:], k.xnT[:, c * CW:(c + 1) * CW], start=True, stop=True)\
                        .then_inc(s_lg, 1)
                pe.wait_ge(s_sm, 3)
                for i in range(T):
                    last = nc.tensor.transpose(bank[2][:, i * E:(i + 1) * E], lg[:, i * P:(i + 1) * P], k.ident[0:E, 0:E])
                last.then_inc(s_pt, 1)
                pe.wait_ge(s_cb, 1 + E)
                for h in range(T // CT):
                    for i in range(CT):
                        last = nc.tensor.transpose(bank[3 + h][0:E, i * P:(i + 1) * P], ind[:, h * CT + i, :], k.ident[:])
                    last.then_inc(s_pt, 1)

            @block.vector
            def _(dve):
                v = nc.vector
                for c in range(C):
                    k.norm_vector(L0 + c, c)
                dve.wait_ge(s_lge, C)
                v.tensor_reduce(mx[:], lg[:], AX.X, ALU.max, negate=True).then_inc(s_sm, 1)
                dve.wait_ge(s_ex, 1)
                v.reciprocal(sm[:], sm[:]).then_inc(s_sm, 1)
                dve.wait_ge(s_sm, 2)
                v.tensor_scalar(lg[:], lg[:], sm[:], None, ALU.mult).then_inc(s_sm, 1)
                dve.wait_ge(s_pt, 1)
                v.tensor_copy(pr[:], bank[2][:, 0:T * E].rearrange("p (t e) -> p t e", t=T)).then_inc(s_cb, 1)
                dve.wait_ge(s_cb, 1)
                top_two(k, dve, 0, pr, top, ti, tf, s_top)
                dve.wait_ge(s_top, 3)
                for e in range(E):
                    if e:
                        dve.wait_ge(s_cb, 1 + e)
                    for j in range(2):
                        v.scalar_tensor_tensor(out=pick[:, j, :], in0=tf[:, :, j], scalar=float(e),
                                               in1=top[:, :, j], op0=ALU.is_equal, op1=ALU.mult)
                        last = v.tensor_scalar(pick[:, 2 + j, :], tf[:, :, j], float(e), None, ALU.is_equal)
                    last.then_inc(s_pc, 1)
                    dve.wait_ge(s_pc, e + 1)
                    v.tensor_tensor(comb[:, e, :], pick[:, 0, :], pick[:, 1, :], ALU.add)
                    v.tensor_tensor(ind[:, :, e], pick[:, 2, :], pick[:, 3, :], ALU.add).then_inc(s_cb, 1)
                for h in range(T // CT):
                    dve.wait_ge(s_pt, 2 + h)
                    v.tensor_copy(indT[:, h * CT:(h + 1) * CT, :],
                                  bank[3 + h][0:E, :].rearrange("p (i q) -> p i q", i=CT))
        k.L += C

        s_W, s_a, s_ae, s_b, s_be, s_y, s_ye, s_v, s_ve, s_e, s_dma, s_o, s_x = (
            sem(n) for n in ("W", "a", "ae", "b", "be", "y", "ye", "v", "ve", "e", "dma", "o", "x"))
        with nc.Block() as block:
            @block.sync
            def _(sp):
                sp.wait_ge(s_ve, E)
                sp.dma_start(vE[:], vrow[:]).then_inc(s_dma, 16)

            @block.gpsimd
            def _(pool):
                for e in range(E):
                    if e >= 2:
                        pool.wait_ge(s_e, e - 1)
                    for n, w in enumerate((w1, w2, w3)):
                        last = nc.gpsimd.tensor_copy(W[e % 2][:, n, :], w[:, e, :])
                    last.then_inc(s_W, 1)

            @block.scalar
            def _(act):
                for e in range(E):
                    for c in range(C):
                        q = e * C + c
                        act.wait_ge(s_a, q + 1)
                        if q >= 2:
                            act.wait_ge(s_b, q - 1)
                        nc.scalar.activation(h1[c % 2][:], bank[c % 2][:], ACT.Relu, bias=c1[:, e:e + 1]).then_inc(s_ae, 1)
                        act.wait_ge(s_b, q + 1)
                        if q >= 2:
                            act.wait_ge(s_y, q - 1)
                        nc.scalar.activation(h2[c % 2][:], bank[2 + c % 2][:], ACT.Relu, bias=c2[:, e:e + 1])\
                            .then_inc(s_be, 1)

            @block.tensor
            def _(pe):
                def first(e, c):
                    q = e * C + c
                    if c == 0:
                        pe.wait_ge(s_W, e + 1)
                    if q >= 2:
                        pe.wait_ge(s_ae, q - 1)
                    nc.tensor.matmul(bank[c % 2][:], W[e % 2][:, 0, :], k.xnT[:, c * CW:(c + 1) * CW],
                                     start=True, stop=True).then_inc(s_a, 1)

                def second(e, c):
                    q = e * C + c
                    pe.wait_ge(s_ae, q + 1)
                    if q >= 2:
                        pe.wait_ge(s_be, q - 1)
                    nc.tensor.matmul(bank[2 + c % 2][:], W[e % 2][:, 1, :], h1[c % 2][:], start=True, stop=True)\
                        .then_inc(s_b, 1)

                def third(e, c):
                    q = e * C + c
                    pe.wait_ge(s_be, q + 1)
                    if q >= 2:
                        pe.wait_ge(s_ye, q - 1)
                    for i in range(CT):
                        dst = bank[4 + c % 2][:, i * P:(i + 1) * P]
                        nc.tensor.matmul(dst, h2[c % 2][:, i * P:(i + 1) * P], W[e % 2][:, 2, :], start=True, stop=False)
                        last = nc.tensor.matmul(dst, k.ones[0:1, :], r3[:, e, :], start=False, stop=True)
                    last.then_inc(s_y, 1)

                def total(e, c):
                    q = e * C + c
                    pe.wait_ge(s_ye, q + 1)
                    if c == 0 and e:
                        pe.wait_ge(s_ve, e)
                    nc.tensor.matmul(bank[6][0:1, :], k.ones[:, 0:1], ry[c % 2][:], start=(c == 0), stop=(c == C - 1))\
                        .then_inc(s_v, 1)

                units = [(e, c) for e in range(E) for c in range(C)]
                for n in range(len(units) + 3):
                    if n < len(units):
                        first(*units[n])
                    if 0 <= n - 1 < len(units):
                        second(*units[n - 1])
                    if 0 <= n - 2 < len(units):
                        third(*units[n - 2])
                        if units[n - 2][1] == C - 1:
                            nc.tensor.drain().then_inc(s_e, 1)
                    if 0 <= n - 3 < len(units):
                        total(*units[n - 3])
                pe.wait_ge(s_dma, 16)
                for c in range(C):
                    if c >= 2:
                        pe.wait_ge(s_x, c - 1)
                    for i in range(CT):
                        last = nc.tensor.matmul(bank[c % 2][:, i * P:(i + 1) * P], indT[:, c * CT + i, :], vE[:],
                                                start=True, stop=True)
                    last.then_inc(s_o, 1)

            def flush(dve, e):
                dve.wait_ge(s_v, C * (e + 1))
                nc.vector.tensor_reduce(vrow[:, e, :], bank[6][0:1, :].rearrange("p (i o) -> p o i", i=CT), AX.X, ALU.add)\
                    .then_inc(s_ve, 1)

            @block.vector
            def _(dve):
                v = nc.vector
                for e in range(E):
                    for c in range(C):
                        q = e * C + c
                        dve.wait_ge(s_y, q + 1)
                        if q >= 2:
                            dve.wait_ge(s_v, q - 1)
                        for i in range(CT):
                            last = v.tensor_scalar(ry[c % 2][:, i * P:(i + 1) * P], bank[4 + c % 2][:, i * P:(i + 1) * P],
                                                   0.0, comb[:, e, c * CT + i:c * CT + i + 1], ALU.max, ALU.mult)
                        last.then_inc(s_ye, 1)
                        if c == 0 and e:
                            flush(dve, e - 1)
                flush(dve, E - 1)
                for c in range(C):
                    dve.wait_ge(s_o, c + 1)
                    xt = k.X[:, c * CT:(c + 1) * CT, :]
                    v.tensor_tensor(xt, bank[c % 2][:].rearrange("p (i d) -> p i d", i=CT), xt, ALU.add).then_inc(s_x, 1)


def softmax_mixer(k, name, windowed):
    nc, t, C, T = k.nc, k.t, k.C, k.T
    bank = k.bank
    HEADS, HD = 16, P // 16
    G, U = HEADS // 4, 4
    S = CT + 1
    WINDOW = 64
    SCALE = float(HD) ** -0.5
    NW = HEADS // 2
    tmp = ExitStack()
    sb = lambda n, shape, dt=F32: k.sb(f"{name}_{n}", shape, dt, tmp)
    sem = lambda n: k.sem(f"{name}_{n}")
    with tmp:
        wqkv, bqkv = sb("wqkv", [P, 3 * P]), sb("bqkv", [1, 3 * P])
        wo, bo = sb("wo", [P, P]), sb("bo", [1, P])
        biasf = sb("biasf", [P, 2, 2, P])
        q_bias = sb("q_bias", [P, C, 4 * P], BF16)
        k_bias = sb("k_bias", [P, C, 4 * P], BF16)
        o_bias = sb("o_bias", [P, 2, 4 * P], BF16)
        raw = sb("raw", [P, 2, HEADS, HD // 2, 2]) if windowed else None
        rot = sb("rot", [P, 4, 2 * HEADS, HD // 2]) if windowed else None
        cs = sb("cs", [P, T, 2, HD // 2]) if windowed else None
        qp, kp, mp = (sb(n, [P, G, U, 32]) for n in ("qp", "kp", "mp"))
        V = sb("V", [P, S, HEADS, HD + 1])
        kT = sb("kT", [P, G, S * P])
        qT = sb("qT", [P, CT, G, P])
        q2 = sb("q2", [P, G, P])
        pb = sb("pb", [P, 2, 4 * P])
        rec = sb("rec", [P, HEADS])
        AO = sb("AO", [P, T, P])
        aoT = sb("aoT", [P, CW])

        lw, s_bi, s_z = sem("w"), sem("bias"), sem("zero")
        s_qkv, s_raw, s_rot, s_pad, s_kt, s_kev, s_qt, s_qev = (
            sem(n) for n in ("qkv", "raw", "rot", "pad", "kt", "kev", "qt", "qev"))
        s_s, s_mx, s_mt, s_q2, s_t, s_ex, s_pv, s_rec, s_o = (
            sem(n) for n in ("s", "mx", "mt", "q2", "t", "ex", "pv", "rec", "o"))
        s_at, s_ae, s_pr, s_x = (sem(n) for n in ("at", "ae", "proj", "x"))
        loads = [(wo[:], t[name + "_wo"])]
        if windowed:
            loads += [(wqkv[:], t[name + "_wqkv"]), (cs[:], t["rotary"].rearrange("(t p) a d -> p t a d", p=P))]
        else:
            row = lambda n: t[f"{name}_{n}"].rearrange("(o d) -> o d", o=1)
            for a, n in enumerate("qkv"):
                loads += [(wqkv[:, a * P:(a + 1) * P], t[f"{name}_w{n}"]), (bqkv[:, a * P:(a + 1) * P], row(f"b{n}"))]
            loads.append((bo[:], row("bo")))

        with nc.Block() as block:
            @block.sync
            def _(sp):
                for dst, src in loads:
                    sp.dma_start(dst, src).then_inc(lw, 16)

            @block.gpsimd
            def _(pool):
                n = 0

                def step(ins):
                    nonlocal n
                    n += 1
                    ins.then_inc(s_bi, 1)
                    pool.wait_ge(s_bi, n)

                flat = biasf[:].rearrange("p a b c -> p (a b c)")
                for dst, d, first, tilecols in (
                        (q_bias, (P, 1, [[0, 2], [-P, 2], [-1, P]]), ((-1, 0), [[0, 2], [P, 2], [0, P]]), 0),
                        (k_bias, (P, -1, [[0, 2], [-P, 2], [1, P]]), ((-1, 0), [[0, 2], [P, 2], [0, P]]), 1)):
                    base, chan, pat = d
                    neg = [[-a, b] for a, b in pat]
                    if windowed:
                        step(nc.gpsimd.memset(biasf[:], 0.0))
                    else:
                        step(nc.gpsimd.iota(biasf[:], pattern=neg, base=-base, channel_multiplier=-chan,
                                            allow_small_or_imprecise_dtypes=True))
                    step(nc.gpsimd.affine_select(out=biasf[:], in_=biasf[:], compare_op=ALU.is_ge, fill=MASKED,
                                                 base=base, pattern=pat, channel_multiplier=chan))
                    if windowed:
                        step(nc.gpsimd.affine_select(out=biasf[:], in_=biasf[:], compare_op=ALU.is_ge, fill=MASKED,
                                                     base=WINDOW - base, pattern=neg, channel_multiplier=-chan))
                    for c in range(1, C):
                        step(nc.gpsimd.tensor_copy(dst[:, c, :], flat))
                    step(nc.gpsimd.tensor_copy(o_bias[:, tilecols, :], flat))
                    step(nc.gpsimd.affine_select(out=biasf[:], in_=biasf[:], compare_op=ALU.is_ge, fill=MASKED,
                                                 base=-1, pattern=first[1], channel_multiplier=0))
                    step(nc.gpsimd.tensor_copy(dst[:, 0, :], flat))
                for a in (qp, mp, V, kT):
                    nc.gpsimd.memset(a[:], 0.0)
                step(nc.gpsimd.memset(kp[:], 0.0))
                nc.gpsimd.memset(kp[:, :, :, HD], 1.0)
                step(nc.gpsimd.memset(V[:, :, :, HD], 1.0))

        L0 = k.L
        with nc.Block() as block:
            def rotate(pool, tile):
                k.wait_alone(pool, s_raw, tile + 1)
                even, odd = (raw[:, :, :, :, a].rearrange("p a h d -> p (a h) d") for a in range(2))
                for n, (x, a) in enumerate(((even, 0), (odd, 1), (odd, 0), (even, 1))):
                    f = cs[:, bass.ds(tile, 1), a, :].to_broadcast([P, 2 * HEADS, HD // 2])
                    last = nc.gpsimd.tensor_tensor(rot[:, n], x, f, ALU.mult)
                last.then_inc(s_rot, 1)
                pool.wait_ge(s_rot, tile * 2 + 1)
                for a, dst in enumerate((qp, kp)):
                    to = dst[:, :, :, 0:HD].rearrange("p g u (d two) -> p two (g u) d", two=2)
                    h = slice(a * HEADS, (a + 1) * HEADS)
                    nc.gpsimd.tensor_tensor(to[:, 0], rot[:, 0, h], rot[:, 1, h], ALU.subtract)
                    last = nc.gpsimd.tensor_tensor(to[:, 1], rot[:, 2, h], rot[:, 3, h], ALU.add)
                last.then_inc(s_rot, 1)

            @block.gpsimd
            def _(pool):
                with pool.Fori(0, C) as c:
                    k.norm_pool(c + L0)
                    if windowed:
                        for i in range(CT):
                            rotate(pool, c * CT + i)

            def scores(pe, c, i, w):
                r, u = w // U, w % U
                pe.wait_ge(s_ex, (c * CT + i) * NW + w + 1)
                out = bank[2 + w % 2]
                bias = k_bias[:, bass.ds(c, 1), :] if i == 0 else o_bias[:, 1, :]
                nc.tensor.matmul(out[:], k.identb[:], bias, start=True, stop=False, skip_group_check=True)
                rows = slice(32 * u, 32 * u + HD + 1)
                for j in range(2):
                    for s in range(2):
                        last = nc.tensor.matmul(out[:, (2 * j + s) * P:(2 * j + s + 1) * P],
                                                kT[rows, 2 * r + j, (i + s) * P:(i + s + 1) * P],
                                                q2[rows, 2 * r + j, :], start=False, stop=(j == 1 and s == 1),
                                                skip_group_check=True)
                last.then_inc(s_t, 1)

            def values(pe, c, i, w):
                r, u = w // U, w % U
                tile = c * CT + i
                if w == 0:
                    pe.wait_ge(s_o, tile + 1)
                pe.wait_ge(s_ex, tile * NW + w + 3)
                for j in range(2):
                    h = 4 * (2 * r + j) + u
                    for s in range(2):
                        last = nc.tensor.matmul(bank[4][:, h * (HD + 1):(h + 1) * (HD + 1)],
                                                pb[:, w % 2, (2 * j + s) * P:(2 * j + s + 1) * P], V[:, i + s, h, :],
                                                start=(w == 0 and j == 0 and s == 0),
                                                stop=(w == NW - 1 and j == 1 and s == 1), skip_group_check=True)
                last.then_inc(s_pv, 1)

            @block.tensor
            def _(pe):
                nc.tensor.sem_inc(s_t, 2)
                nc.tensor.sem_inc(s_pv, 2)
                pe.wait_ge(lw, 16 * len(loads))
                with pe.Fori(0, C) as c:
                    k.norm_tensor(c + L0)
                    pe.wait_ge(k.ln_ev, c + L0 + 1)
                    for i in range(CT):
                        tile = c * CT + i
                        pe.wait_ge(s_qev, tile + 1)
                        dst = bank[6][:, 0:3 * P]
                        last = nc.tensor.matmul(dst, k.xnT[:, i * P:(i + 1) * P], wqkv[:], start=True, stop=windowed)
                        if not windowed:
                            last = nc.tensor.matmul(dst, k.ones[0:1, :], bqkv[:], start=False, stop=True)
                        last.then_inc(s_qkv, 1)
                        pe.wait_ge(s_pad, tile + 1)
                        if windowed:
                            pe.wait_ge(s_rot, tile * 2 + 2)
                        for src, done in ((kp, s_kt), (qp, s_qt)):
                            if src is qp:
                                pe.wait_ge(s_kev, tile + 2)
                            for g in range(G):
                                last = nc.tensor.transpose(bank[6][:, g * P:(g + 1) * P],
                                                           src[:, g].rearrange("p u d -> p (u d)"), k.ident[:])
                            last.then_inc(done, 1)
                    pe.wait_ge(s_qev, c * CT + CT + 1)
                    for i in range(CT):
                        tile = c * CT + i
                        for w in range(NW):
                            r, u = w // U, w % U
                            pe.wait_ge(s_mx, tile * NW + w + 1)
                            out = bank[w % 2]
                            bias = q_bias[:, bass.ds(c, 1), :] if i == 0 else o_bias[:, 0, :]
                            nc.tensor.matmul(out[:], k.identb[:], bias, start=True, stop=False, skip_group_check=True)
                            rows = slice(32 * u, 32 * u + HD)
                            for j in range(2):
                                last = nc.tensor.matmul(out[:, j * 2 * P:(j + 1) * 2 * P], qT[rows, i, 2 * r + j, :],
                                                        kT[rows, 2 * r + j, i * P:(i + 2) * P], start=False,
                                                        stop=(j == 1), skip_group_check=True)
                            last.then_inc(s_s, 1)
                        pe.wait_ge(s_mx, tile * NW + NW + 2)
                        pe.wait_ge(s_q2, tile + 1)
                        for g in range(G):
                            last = nc.tensor.transpose(bank[5][:, g * P:(g + 1) * P],
                                                       mp[:, g].rearrange("p u d -> p (u d)"), k.ident[:])
                        last.then_inc(s_mt, 1)
                        pe.wait_ge(s_q2, tile + 2)
                        for w in range(NW + 1):
                            if w < NW:
                                scores(pe, c, i, w)
                            if w:
                                values(pe, c, i, w - 1)

            @block.scalar
            def _(act):
                nc.scalar.sem_inc(s_qev, 1)
                nc.scalar.sem_inc(s_kev, 1)
                nc.scalar.sem_inc(s_ex, 2)
                with act.Fori(0, C) as c:
                    k.norm_scalar(c + L0, k.xnT[:, 0:CW])
                    act.wait_ge(s_kev, c * CT + 1)
                    act.wait_ge(s_pv, c * (CT * NW) + 2)
                    nc.scalar.activation(kT[:, :, 0:P], kT[:, :, CT * P:(CT + 1) * P], ACT.Copy)
                    nc.scalar.activation(V[:, 0], V[:, CT], ACT.Copy)
                    for i in range(CT):
                        tile = c * CT + i
                        act.wait_ge(s_qkv, tile + 1)
                        part = lambda a: bank[6][:, a * P:(a + 1) * P]
                        if windowed:
                            flat = raw[:].rearrange("p a h d e -> p a (h d e)")
                            nc.scalar.activation(flat[:, 0], part(0), ACT.Copy, scale=SCALE)
                            nc.scalar.activation(flat[:, 1], part(1), ACT.Copy).then_inc(s_raw, 1)
                        else:
                            for a, dst, scale in ((0, qp, SCALE), (1, kp, 1.0)):
                                nc.scalar.activation(dst[:, :, :, 0:HD].rearrange("p g u d -> p (g u) d"),
                                                     part(a).rearrange("p (h d) -> p h d", d=HD), ACT.Copy, scale=scale)
                        nc.scalar.activation(V[:, i + 1, :, 0:HD], part(2).rearrange("p (h d) -> p h d", d=HD), ACT.Copy)\
                            .then_inc(s_pad, 1)
                        act.wait_ge(s_kt, tile + 1)
                        four = bank[6][:].rearrange("p (g q) -> p g q", g=G)
                        nc.scalar.activation(kT[:, :, (i + 1) * P:(i + 2) * P], four, ACT.Copy).then_inc(s_kev, 1)
                        act.wait_ge(s_qt, tile + 1)
                        nc.scalar.activation(qT[:, i], four, ACT.Copy).then_inc(s_qev, 1)
                    for i in range(CT):
                        for w in range(NW):
                            W = (c * CT + i) * NW + w
                            act.wait_ge(s_t, W + 3)
                            act.wait_ge(s_pv, W + 1)
                            nc.scalar.activation(pb[:, w % 2, :], bank[2 + w % 2][:], ACT.Exp).then_inc(s_ex, 1)

            @block.vector
            def _(dve):
                v = nc.vector
                v.sem_inc(s_mx, 2)
                v.sem_inc(s_q2, 1)
                v.sem_inc(s_o, 1)
                with dve.Fori(0, C) as c:
                    k.norm_vector(c + L0, c)
                    for i in range(CT):
                        tile = c * CT + i
                        for w in range(NW):
                            r, u = w // U, w % U
                            dve.wait_ge(s_s, tile * NW + w + 1)
                            v.tensor_reduce(mp[:, 2 * r:2 * r + 2, u, HD],
                                            bank[w % 2][:].rearrange("p (j q) -> p j q", j=2), AX.X, ALU.max,
                                            negate=True).then_inc(s_mx, 1)
                        dve.wait_ge(s_mt, tile + 1)
                        v.tensor_tensor(q2[:], qT[:, i], bank[5][:].rearrange("p (g q) -> p g q", g=G), ALU.add)\
                            .then_inc(s_q2, 1)
                        dve.wait_ge(s_pv, tile * NW + NW + 2)
                        o = bank[4][:, 0:HEADS * (HD + 1)].rearrange("p (h d) -> p h d", h=HEADS)
                        v.reciprocal(rec[:], o[:, :, HD]).then_inc(s_rec, 1)
                        dve.wait_ge(s_rec, tile + 1)
                        v.tensor_tensor(AO[:, bass.ds(tile, 1), :].rearrange("p o (h d) -> p (o h) d", h=HEADS),
                                        o[:, :, 0:HD], rec[:, :, None].to_broadcast([P, HEADS, HD]), ALU.mult)\
                            .then_inc(s_o, 1)
        k.L += C

        with nc.Block() as block:
            @block.tensor
            def _(pe):
                for c in range(C):
                    if c:
                        pe.wait_ge(s_ae, c)
                    for i in range(CT):
                        last = nc.tensor.transpose(bank[4][:, i * P:(i + 1) * P], AO[:, c * CT + i, :], k.ident[:])
                    last.then_inc(s_at, 1)
                    pe.wait_ge(s_ae, c + 1)
                    if c >= 2:
                        pe.wait_ge(s_x, c - 1)
                    for i in range(CT):
                        dst = bank[c % 2][:, i * P:(i + 1) * P]
                        last = nc.tensor.matmul(dst, aoT[:, i * P:(i + 1) * P], wo[:], start=True, stop=windowed)
                        if not windowed:
                            last = nc.tensor.matmul(dst, k.ones[0:1, :], bo[:], start=False, stop=True)
                    last.then_inc(s_pr, 1)

            @block.scalar
            def _(act):
                for c in range(C):
                    act.wait_ge(s_at, c + 1)
                    if c:
                        act.wait_ge(s_pr, c)
                    nc.scalar.activation(aoT[:], bank[4][:], ACT.Copy).then_inc(s_ae, 1)

            @block.vector
            def _(dve):
                for c in range(C):
                    dve.wait_ge(s_pr, c + 1)
                    xt = k.X[:, c * CT:(c + 1) * CT, :]
                    nc.vector.tensor_tensor(xt, bank[c % 2][:].rearrange("p (i d) -> p i d", i=CT), xt, ALU.add)\
                        .then_inc(s_x, 1)


def ffn3(k):
    nc, t, C = k.nc, k.t, k.C
    L0, bank = k.L, k.bank
    F = t["f3_w1"].shape[1]
    FB = F // P
    tmp = ExitStack()
    sb = lambda n, shape, dt=F32: k.sb("f3_" + n, shape, dt, tmp)
    sem = lambda n: k.sem("f3_" + n)
    with tmp:
        w1, w2 = sb("w1", [P, F]), sb("w2", [P, F])
        hw = [sb("h1w", [P, FB, F]), sb("h2w", [P, FB, F])]
        w3 = sb("w3", [P, FB, P])
        sc1, sc2, sch1, sch2 = (sb(n, [P, FB]) for n in ("sc1", "sc2", "sch1", "sch2"))
        s3 = sb("s3", [P, P])
        sg = sb("sg", [P, 2, CW])
        hA = [sb(f"hA{b}", [P, FB, CW]) for b in range(2)]
        hB = [sb(f"hB{b}", [P, FB, CW]) for b in range(2)]
        ys = sb("ys", [P, CT, P])
        lw, s_ab, s_sg, s_a, s_m, s_g, s_y, s_ys, s_x = (
            sem(n) for n in ("w", "ab", "sg", "a", "m", "g", "y", "ys", "x"))
        col = lambda n: t[n].rearrange("(f p) -> p f", p=P)
        mat = lambda n: t[n].rearrange("(f p) o -> p f o", p=P)
        loads = [(w1[:], t["f3_w1"]), (w2[:], t["f3_w2"]), (hw[0][:], mat("f3_h1")), (hw[1][:], mat("f3_h2")),
                 (w3[:], mat("f3_w3")), (sc1[:], col("f3_s1")), (sc2[:], col("f3_s2")), (sch1[:], col("f3_sh1")),
                 (sch2[:], col("f3_sh2")), (s3[:], t["f3_s3"].partition_broadcast(P))]
        with nc.Block() as block:
            @block.sync
            def _(sp):
                with nc.allow_non_contiguous_dma(reason="scale columns"):
                    for dst, src in loads:
                        sp.dma_start(dst, src).then_inc(lw, 16)

            @block.gpsimd
            def _(pool):
                for c in range(C):
                    k.norm_pool(L0 + c)

            @block.scalar
            def _(act):
                for c in range(C):
                    k.norm_scalar(L0 + c, k.xnT[:, c * CW:(c + 1) * CW])

            @block.tensor
            def _(pe):
                for c in range(C):
                    k.norm_tensor(L0 + c)
                pe.wait_ge(lw, 16 * len(loads))

            @block.vector
            def _(dve):
                for c in range(C):
                    k.norm_vector(L0 + c, c)
        k.L += C

        with nc.Block() as block:
            @block.tensor
            def _(pe):
                with pe.Fori(0, C // 2) as it:
                    for b in range(2):
                        if b == 0:
                            pe.wait_ge(s_ys, it * 2 + 2)
                        for f in range(FB):
                            pe.wait_ge(s_a, it * (2 * FB) + (b * FB + f) + 1)
                            for j, w in enumerate((w1, w2)):
                                nc.tensor.matmul(bank[2 * (f % 2) + j][:], w[:, f * P:(f + 1) * P],
                                                 k.xnT[:, bass.ds(it * (2 * CW) + b * CW, CW)], start=True, stop=True)\
                                    .then_inc(s_ab, 1)
                    for layer in range(2):
                        for b in range(2):
                            src = hA[b] if layer == 0 else hB[b]
                            if layer == 0:
                                pe.wait_ge(s_a, it * (2 * FB) + (b + 1) * FB + 2)
                            else:
                                pe.wait_ge(s_g, it * (4 * FB) + (b + 1) * FB + 4)
                            for f in range(FB):
                                m = (layer * 2 + b) * FB + f
                                pe.wait_ge(s_g, it * (4 * FB) + m + 1)
                                for i in range(FB):
                                    last = nc.tensor.matmul(bank[4 + m % 4][:], hw[layer][:, i, f * P:(f + 1) * P],
                                                            src[:, i, :], start=(i == 0), stop=(i == FB - 1))
                                last.then_inc(s_m, 1)
                    for b in range(2):
                        pe.wait_ge(s_g, it * (4 * FB) + (2 + b + 1) * FB + 4)
                        for i in range(CT):
                            for f in range(FB):
                                last = nc.tensor.matmul(bank[b][:, i * P:(i + 1) * P],
                                                        hA[b][:, f, i * P:(i + 1) * P], w3[:, f, :],
                                                        start=(f == 0), stop=(f == FB - 1))
                        last.then_inc(s_y, 1)

            @block.scalar
            def _(act):
                nc.scalar.sem_inc(s_g, 4)
                with act.Fori(0, C // 2) as it:
                    for b in range(2):
                        for f in range(FB):
                            n = it * (2 * FB) + (b * FB + f)
                            act.wait_ge(s_ab, n * 2 + 1)
                            act.wait_ge(s_a, n + 1)
                            nc.scalar.activation(sg[:, f % 2, :], bank[2 * (f % 2)][:], ACT.Silu, scale=sc1[:, f:f + 1])\
                                .then_inc(s_sg, 1)
                    for layer, (dst, sc) in enumerate(((hB, sch1), (hA, sch2))):
                        for b in range(2):
                            for f in range(FB):
                                m = (layer * 2 + b) * FB + f
                                act.wait_ge(s_m, it * (4 * FB) + m + 1)
                                nc.scalar.activation(dst[b][:, f, :], bank[4 + m % 4][:], ACT.Gelu, scale=sc[:, f:f + 1])\
                                    .then_inc(s_g, 1)

            @block.vector
            def _(dve):
                v = nc.vector
                v.sem_inc(s_a, 2)
                v.sem_inc(s_ys, 2)
                with dve.Fori(0, C // 2) as it:
                    for b in range(2):
                        for f in range(FB):
                            n = it * (2 * FB) + (b * FB + f)
                            dve.wait_ge(s_ab, n * 2 + 2)
                            dve.wait_ge(s_sg, n + 1)
                            v.scalar_tensor_tensor(out=hA[b][:, f, :], in0=bank[2 * (f % 2) + 1][:],
                                                   scalar=sc2[:, f:f + 1], in1=sg[:, f % 2, :], op0=ALU.mult,
                                                   op1=ALU.mult).then_inc(s_a, 1)
                    for b in range(2):
                        q = it * 2 + b
                        dve.wait_ge(s_y, q + 1)
                        v.tensor_tensor(ys[:], bank[b][:].rearrange("p (i d) -> p i d", i=CT),
                                        s3[:, None, :].to_broadcast([P, CT, P]), ALU.mult).then_inc(s_ys, 1)
                        dve.wait_ge(s_ys, q + 3)
                        xt = k.X[:, bass.ds(q * CT, CT), :]
                        v.tensor_tensor(xt, xt, ys[:], ALU.add).then_inc(s_x, 1)
                        dve.wait_ge(s_x, q + 1)


def store(k, out):
    stored = k.sem("stored")
    with k.nc.Block() as block:
        @block.sync
        def _(sp):
            sp.dma_start(out.rearrange("(t p) d -> p t d", p=P), k.X[:]).then_inc(stored, 16)
            sp.wait_ge(stored, 16)


def program(nc, t, out, parts=PARTS):
    with ExitStack() as ctx:
        k = Core(nc, ctx, t)
        constants(k)
        for part in parts:
            if part == "mamba":
                mamba(k)
            elif part in ("moe0", "moe1"):
                experts(k, part, gated=(part == "moe1"))
            elif part == "linear":
                linear(k)
            elif part in ("decay", "window"):
                softmax_mixer(k, part, windowed=(part == "window"))
            elif part == "deep":
                deep(k)
            elif part == "ffn3":
                ffn3(k)
            k.end_part()
        store(k, out)


NAMES = {
    "x": ("L0_attn_x", lambda a: a.reshape(a.shape[1:])),
    "ln1_g": ("L0_attn_ln1_g", None), "ln1_b": ("L0_attn_ln1_b", None),
    "in_proj_w": ("L0_attn_in_proj_w", None),
    "conv_w": ("L0_attn_conv_w", lambda a: a.reshape(a.shape[0], a.shape[2])),
    "conv_b": ("L0_attn_conv_b", None), "x_proj_w": ("L0_attn_x_proj_w", None),
    "dt_proj_w": ("L0_attn_dt_proj_w", None), "dt_proj_b": ("L0_attn_dt_proj_b", None),
    "A_log": ("L0_attn_A_log", None), "D": ("L0_attn_D", None), "out_proj_w": ("L0_attn_out_proj_w", None),
    "ln2_g": ("L0_attn_ln2_g", None), "ln2_b": ("L0_attn_ln2_b", None),
    "ffn_w1": ("L0_attn_ffn_w1", None), "ffn_b1": ("L0_attn_ffn_b1", None),
    "ffn_w2": ("L0_attn_ffn_w2", None), "ffn_b2": ("L0_attn_ffn_b2", None),
    "moe0_gate_w": ("L0_ffn_gate_w", None), "moe0_gate_b": ("L0_ffn_gate_b", None),
    "moe0_w1": ("L0_ffn_w1", None), "moe0_b1": ("L0_ffn_b1", None),
    "moe0_w2": ("L0_ffn_w2", None), "moe0_b2": ("L0_ffn_b2", None),
    "lin_wqT": ("L1_attn_Wq", lambda a: a.T), "lin_wkT": ("L1_attn_Wk", lambda a: a.T), "lin_wv": ("L1_attn_Wv", None),
    "lin_bq": ("L1_attn_bq", None), "lin_bk": ("L1_attn_bk", None), "lin_bv": ("L1_attn_bv", None),
    "lin_gamma": ("L1_attn_gamma", None),
    "moe1_gate_w": ("L1_ffn_router_w", lambda a: a.T), "moe1_w1": ("L1_ffn_w_gate", None),
    "moe1_wu": ("L1_ffn_w_up", None), "moe1_w2": ("L1_ffn_w_down", None),
    "decay_wq": ("L2_attn_Wq", lambda a: a.T), "decay_wk": ("L2_attn_Wk", lambda a: a.T),
    "decay_wv": ("L2_attn_Wv", lambda a: a.T), "decay_wo": ("L2_attn_Wo", lambda a: a.T),
    "decay_bq": ("L2_attn_bq", None), "decay_bk": ("L2_attn_bk", None), "decay_bv": ("L2_attn_bv", None),
    "decay_bo": ("L2_attn_bo", None),
    "deep_gate_w": ("L2_ffn_gate_w", None), "deep_gate_b": ("L2_ffn_gate_b", None),
    "deep_w1": ("L2_ffn_w1", None), "deep_b1": ("L2_ffn_b1", None), "deep_w2": ("L2_ffn_w2", None),
    "deep_b2": ("L2_ffn_b2", None), "deep_w3": ("L2_ffn_w3", None), "deep_b3": ("L2_ffn_b3", None),
    "window_wqkv": ("L3_attn_w_qkv", None), "window_wo": ("L3_attn_w_o", None),
    "f3_w1": ("L3_ffn_w1_w", lambda a: a.T), "f3_s1": ("L3_ffn_w1_s", None),
    "f3_w2": ("L3_ffn_w2_w", lambda a: a.T), "f3_s2": ("L3_ffn_w2_s", None),
    "f3_h1": ("L3_ffn_h1_w", lambda a: a.T), "f3_sh1": ("L3_ffn_h1_s", None),
    "f3_h2": ("L3_ffn_h2_w", lambda a: a.T), "f3_sh2": ("L3_ffn_h2_s", None),
    "f3_w3": ("L3_ffn_w3_w", lambda a: a.T), "f3_s3": ("L3_ffn_w3_s", None),
}


def rotary_table(np, n, half, base=10000.0):
    inv = (np.float32(1.0) / np.float32(base) ** (np.arange(half, dtype=np.float32) / np.float32(half)))
    angle = np.arange(n, dtype=np.float32)[:, None] * inv.astype(np.float32)[None, :]
    return np.ascontiguousarray(np.stack([np.cos(angle), np.sin(angle)], axis=1).astype(np.float32))


def kernel(**inputs):
    import numpy as np
    import concourse.bacc as bacc
    from concourse.bass_utils import run_bass_kernel_spmd as run

    nc = bacc.Bacc("TRN2", target_bir_lowering=False, num_devices=1)
    arrays, t = {}, {}
    for name, (source, lay) in NAMES.items():
        a = np.asarray(inputs[source])
        a = np.ascontiguousarray(lay(a) if lay else a)
        arrays["in_" + name] = a
        t[name] = nc.dram_tensor("in_" + name, a.shape, mybir.dt.from_np(a.dtype), kind="ExternalInput").ap()
    shape = inputs["L0_attn_x"].shape
    arrays["in_rotary"] = rotary_table(np, shape[1], 4)
    t["rotary"] = nc.dram_tensor("in_rotary", arrays["in_rotary"].shape, F32, kind="ExternalInput").ap()
    out = nc.dram_tensor("out", shape[1:], F32, kind="ExternalOutput").ap()
    program(nc, t, out)
    r = run(nc, [arrays], core_ids=[0])
    return r.results[0]["out"].reshape(shape)
```

```python
from contextlib import ExitStack

import concourse.bass as bass
from concourse import mybir

F32 = mybir.dt.float32
BF16 = mybir.dt.bfloat16
U32 = mybir.dt.uint32
ALU = mybir.AluOpType
ACT = mybir.ActivationFunctionType
AX = mybir.AxisListType

P = 128
CT = 4
CW = CT * P
EPS = 1e-5
MASKED = -1.0e30
PARTS = ("mamba", "moe0", "linear", "moe1", "decay", "deep", "window", "ffn3")


class Core:

    def __init__(self, nc, ctx, t):
        self.nc, self.ctx, self.t = nc, ctx, t
        self.N = t["x"].shape[0]
        self.T = self.N // P
        self.C = self.T // CT
        self.E = t["moe0_gate_w"].shape[1]
        self.L = 0
        self.bank = [ctx.enter_context(nc.psum_tensor(f"bank{i}", [P, 512], F32)) for i in range(8)]
        self.X = self.sb("X", [P, self.T, P])
        self.xnT = self.sb("xnT", [P, self.N])
        self.stats = self.sb("stats", [P, CT, 6])
        self.meanvar = self.sb("meanvar", [P, CT, 2])
        self.veps = self.sb("veps", [P, CT])
        self.rstd = self.sb("rstd", [P, CT])
        self.xn = self.sb("xn", [P, CT, P])
        self.ident = self.sb("ident", [P, P])
        self.identb = self.sb("identb", [P, P], BF16)
        self.ones = self.sb("ones", [P, P])
        self.mhalf = self.sb("mhalf", [P, 32])
        self.part_sems = []
        self.passed = self.sem("passed")
        self.ln_st = self.sem("ln_st")
        self.ln_mv = self.sem("ln_mv")
        self.ln_ve = self.sem("ln_ve")
        self.ln_rs = self.sem("ln_rs")
        self.ln_xn = self.sem("ln_xn")
        self.ln_tr = self.sem("ln_tr")
        self.ln_ev = self.sem("ln_ev")
        self.part_sems = []

    def sb(self, name, shape, dt=F32, ctx=None):
        return (ctx or self.ctx).enter_context(self.nc.sbuf_tensor(name, shape, dt))

    def sem(self, name):
        handle = self.nc.alloc_semaphore(name=name)
        self.part_sems.append(handle)
        return handle

    def end_part(self):
        self.nc.clear_and_free_semaphores(self.part_sems)
        self.nc.all_engine_barrier()
        self.part_sems = []

    def wait_alone(self, engine, sem, value):
        engine.wait_ge(sem, value)
        engine.sem_inc(self.passed, 1)

    def norm_vector(self, L, c):
        nc, v = self.nc, self.nc.vector
        tile = lambda i: self.X[:, bass.ds(c * CT + i, 1), :]
        for i in range(CT):
            last = v.bn_stats(self.stats[:, i, :], tile(i))
        last.then_inc(self.ln_st, 1)
        self.wait_alone(v, self.ln_st, L + 1)
        for i in range(CT):
            last = v.bn_aggr(self.meanvar[:, i, :], self.stats[:, i, :])
        last.then_inc(self.ln_mv, 1)
        v.wait_ge(self.ln_mv, L + 1)
        v.tensor_scalar(self.veps[:], self.meanvar[:, :, 1], EPS, None, ALU.add).then_inc(self.ln_ve, 1)
        v.wait_ge(self.ln_rs, L + 1)
        if not isinstance(L, int) or L > 0:
            v.wait_ge(self.ln_tr, L)
        for i in range(CT):
            last = v.tensor_scalar(self.xn[:, i, :], tile(i), self.meanvar[:, i, 0:1], self.rstd[:, i:i + 1],
                                   ALU.subtract, ALU.mult)
        last.then_inc(self.ln_xn, 1)

    def norm_pool(self, L):
        self.nc.gpsimd.wait_ge(self.ln_ve, L + 1)
        self.nc.gpsimd.tensor_tensor(self.rstd[:], self.veps[:], self.mhalf[:, 0:CT], ALU.pow)\
            .then_inc(self.ln_rs, 1)

    def norm_tensor(self, L):
        pe = self.nc.tensor
        pe.wait_ge(self.ln_xn, L + 1)
        if not isinstance(L, int) or L > 0:
            pe.wait_ge(self.ln_ev, L)
        for i in range(CT):
            last = pe.transpose(self.bank[7][:, i * P:(i + 1) * P], self.xn[:, i, :], self.ident[:])
        last.then_inc(self.ln_tr, 1)

    def norm_scalar(self, L, dst):
        self.nc.scalar.wait_ge(self.ln_tr, L + 1)
        self.nc.scalar.activation(dst, self.bank[7][:], ACT.Copy).then_inc(self.ln_ev, 1)


def constants(k):
    nc = k.nc
    loaded, zeroed, made = k.sem("x_loaded"), k.sem("const_zeroed"), k.sem("const_made")
    with nc.Block() as block:
        @block.sync
        def _(sp):
            sp.dma_start(k.X[:], k.t["x"].rearrange("(t p) d -> p t d", p=P)).then_inc(loaded, 16)
            sp.wait_ge(loaded, 16)

        @block.gpsimd
        def _(pool):
            nc.gpsimd.memset(k.ident[:], 0.0)
            nc.gpsimd.memset(k.ones[:], 1.0)
            nc.gpsimd.memset(k.mhalf[:], -0.5).then_inc(zeroed, 1)
            pool.wait_ge(zeroed, 1)
            nc.gpsimd.affine_select(out=k.ident[:], in_=k.ident[:], compare_op=ALU.not_equal, fill=1.0, base=0,
                                    pattern=[[-1, P]], channel_multiplier=1).then_inc(made, 1)

        @block.vector
        def _(dve):
            dve.wait_ge(made, 1)
            nc.vector.tensor_copy(k.identb[:], k.ident[:])


def mamba(k):
    nc, t, N, C = k.nc, k.t, k.N, k.C
    DI = t["in_proj_w"].shape[1] // 2
    H = DI // P
    NS = t["A_log"].shape[1]
    R = t["dt_proj_w"].shape[0]
    FB = t["ffn_w1"].shape[1] // P
    KC = t["conv_w"].shape[1]
    PAD = KC - 1
    L0 = k.L
    bank = k.bank
    tmp = ExitStack()
    sb = lambda name, shape, dt=F32: k.sb(name, shape, dt, tmp)
    with tmp:
        inw = sb("inw", [P, 2 * DI])
        g1 = sb("g1", [P, 1])
        b1 = sb("b1", [P, 1])
        g2 = sb("g2", [P, 1])
        b2 = sb("b2", [P, 1])
        cw = sb("cw", [P, H, KC])
        cb = sb("cb", [P, H])
        xpw = sb("xpw", [P, H, R + 2 * NS])
        xpw3 = sb("xpw3", [P, H, 3, 2 * NS])
        dtw = sb("dtw", [R, DI])
        dtb = sb("dtb", [P, H])
        A = sb("A", [P, H, NS])
        Dp = sb("Dp", [P, H])
        outw = sb("outw", [P, H, P])
        w1 = sb("m_w1", [P, FB * P])
        w1b = sb("m_w1b", [P, FB])
        w2 = sb("m_w2", [P, FB, P])
        w2b = sb("m_w2b", [1, P])
        xo = sb("xo", [P, k.T, P])
        xi = sb("xi", [P, H, PAD + N])
        sz = sb("sz", [P, H, N])
        xc = sb("xc", [P, H, N])
        dt = sb("dt", [P, H, N])
        dtx = sb("dtx", [P, H, N])
        BC3 = sb("BC3", [96, N], BF16)
        sel = sb("sel", [96, 2 * NS, P], BF16)
        rt1 = sb("rt1", [96, CW])
        rt2 = sb("rt2", [96, CW])
        hib = sb("hib", [96, CW], BF16)
        midb = sb("midb", [96, CW], BF16)
        lr = sb("lr", [R, CW])
        dA = sb("dA", [P, 2, H, CW])
        dBx = sb("dBx", [P, 2, H, CW])
        h = sb("h", [P, 2, H, CW])
        hC = sb("hC", [P, 2, H, CW])
        Cs = sb("Cs", [P, 2, CW])
        state = sb("state", [P, NS, H])
        r2 = sb("r2", [P, CT])

        wl, sel0, selm = k.sem("m_weights"), k.sem("m_sel_zeroed"), k.sem("m_sel_made")
        s_r2 = k.sem("m_r2")
        s_ve2 = k.sem("m_ve2")
        s_xo = k.sem("m_xo")
        s_un = k.sem("m_un")
        s_in = k.sem("m_in")
        s_inev = k.sem("m_inev")
        s_cv = k.sem("m_conv")
        s_xc = k.sem("m_xc")
        s_xd = k.sem("m_xd")
        s_xde = k.sem("m_xde")
        s_bc = k.sem("m_bc")
        s_dtm = k.sem("m_dtm")
        s_dta = k.sem("m_dta")
        s_sp = k.sem("m_softplus")
        s_dt = k.sem("m_dt")
        s_dtx = k.sem("m_dtx")
        s_A = k.sem("m_A")

        wloads = [
            (inw[:], t["in_proj_w"]), (g1[:], t["ln1_g"].rearrange("(p o) -> p o", o=1)),
            (b1[:], t["ln1_b"].rearrange("(p o) -> p o", o=1)), (g2[:], t["ln2_g"].rearrange("(p o) -> p o", o=1)),
            (b2[:], t["ln2_b"].rearrange("(p o) -> p o", o=1)),
            (cw[:], t["conv_w"].rearrange("(h p) k -> p h k", p=P)),
            (cb[:], t["conv_b"].rearrange("(h p) -> p h", p=P)),
            (xpw[:], t["x_proj_w"].rearrange("(h p) k -> p h k", p=P)),
            (dtw[:], t["dt_proj_w"]), (dtb[:], t["dt_proj_b"].rearrange("(h p) -> p h", p=P)),
            (A[:], t["A_log"].rearrange("(h p) n -> p h n", p=P)), (Dp[:], t["D"].rearrange("(h p) -> p h", p=P)),
            (outw[:], t["out_proj_w"].rearrange("(h p) d -> p h d", p=P)),
            (w1[:], t["ffn_w1"]), (w1b[:], t["ffn_b1"].rearrange("(f p) -> p f", p=P)),
            (w2[:], t["ffn_w2"].rearrange("(f p) d -> p f d", p=P)),
            (w2b[:], t["ffn_b2"].rearrange("(o d) -> o d", o=1)),
        ]

        with nc.Block() as block:
            @block.sync
            def _(sp):
                with nc.allow_non_contiguous_dma(reason="small weights"):
                    for dst, src in wloads:
                        sp.dma_start(dst, src).then_inc(wl, 16)

            @block.gpsimd
            def _(pool):
                nc.gpsimd.memset(sel[:], 0.0)
                nc.gpsimd.memset(state[:], 0.0)
                nc.gpsimd.memset(xi[:, :, 0:PAD], 0.0).then_inc(sel0, 1)
                pool.wait_ge(sel0, 1)
                for part in range(3):
                    last = nc.gpsimd.affine_select(out=sel[:], in_=sel[:], compare_op=ALU.not_equal, fill=1.0,
                                                   base=-32 * part, pattern=[[-1, 2 * NS], [0, P]],
                                                   channel_multiplier=1)
                    last.then_inc(selm, 1)
                    pool.wait_ge(selm, part + 1)
                for c in range(C):
                    k.norm_pool(L0 + c)
                    pool.wait_ge(s_ve2, c + 1)
                    nc.gpsimd.tensor_tensor(r2[:], r2[:], k.mhalf[:, 0:CT], ALU.pow).then_inc(s_r2, 1)

            @block.vector
            def _(dve):
                dve.wait_ge(wl, 16 * len(wloads))
                for p in range(3):
                    last = nc.vector.tensor_copy(xpw3[:, :, p, :], xpw[:, :, R:R + 2 * NS])
                last.then_inc(s_A, 1)

                def norm(c):
                    L = L0 + c
                    v = nc.vector
                    tile = lambda i: k.X[:, c * CT + i, :]
                    for i in range(CT):
                        last = v.bn_stats(k.stats[:, i, :], tile(i))
                    last.then_inc(k.ln_st, 1)
                    v.wait_ge(k.ln_st, L + 1)
                    for i in range(CT):
                        last = v.bn_aggr(k.meanvar[:, i, :], k.stats[:, i, :])
                    last.then_inc(k.ln_mv, 1)
                    v.wait_ge(k.ln_mv, L + 1)
                    v.tensor_scalar(k.veps[:], k.meanvar[:, :, 1], EPS, None, ALU.add).then_inc(k.ln_ve, 1)
                    v.wait_ge(k.ln_rs, L + 1)
                    for i in range(CT):
                        last = v.tensor_scalar(xo[:, c * CT + i, :], tile(i), k.meanvar[:, i, 0:1],
                                               k.rstd[:, i:i + 1], ALU.subtract, ALU.mult)
                    last.then_inc(s_xo, 1)
                    v.tensor_tensor(r2[:], k.meanvar[:, :, 1], k.rstd[:], ALU.mult).then_inc(s_un, 1)
                    v.wait_ge(s_un, 3 * c + 1)
                    v.tensor_tensor(r2[:], r2[:], k.rstd[:], ALU.mult).then_inc(s_un, 1)
                    v.wait_ge(s_un, 3 * c + 2)
                    v.tensor_scalar(r2[:], r2[:], EPS, None, ALU.add).then_inc(s_ve2, 1)
                    v.wait_ge(s_r2, c + 1)
                    v.wait_ge(s_xo, c + 1)
                    if c:
                        v.wait_ge(k.ln_tr, L)
                    for i in range(CT):
                        last = v.tensor_scalar(k.xn[:, i, :], xo[:, c * CT + i, :], r2[:, i:i + 1], None, ALU.mult)
                    last.then_inc(k.ln_xn, 1)
                    v.nop().then_inc(s_un, 1)

                def conv(c):
                    a = PAD + c * CW
                    for hh in range(H):
                        acc = xc[:, hh, c * CW:(c + 1) * CW]
                        dve.wait_ge(s_inev, 2 * H * c + hh + 1)
                        n0 = KC * (c * H + hh)
                        nc.vector.tensor_scalar(acc, xi[:, hh, a - PAD:a - PAD + CW], cw[:, hh, 0:1],
                                                cb[:, hh:hh + 1], ALU.mult, ALU.add).then_inc(s_cv, 1)
                        for j in range(1, KC):
                            dve.wait_ge(s_cv, n0 + j)
                            nc.vector.scalar_tensor_tensor(
                                out=acc, in0=xi[:, hh, a - PAD + j:a - PAD + j + CW], scalar=cw[:, hh, j:j + 1],
                                in1=acc, op0=ALU.mult, op1=ALU.add).then_inc(s_cv, 1)

                def split(c):
                    cs = slice(c * CW, (c + 1) * CW)
                    v = nc.vector
                    dve.wait_ge(s_xd, 2 * c + 1)
                    n0 = 8 * c
                    v.tensor_copy(hib[:], bank[4][0:96, :]).then_inc(s_bc, 1)
                    dve.wait_ge(s_bc, n0 + 1)
                    v.tensor_tensor(rt1[:], bank[4][0:96, :], hib[:], ALU.subtract).then_inc(s_bc, 1)
                    v.tensor_copy(BC3[0:32, cs], hib[0:32, :]).then_inc(s_bc, 1)
                    dve.wait_ge(s_bc, n0 + 2)
                    v.tensor_copy(midb[:], rt1[:]).then_inc(s_bc, 1)
                    dve.wait_ge(s_bc, n0 + 4)
                    v.tensor_tensor(rt2[:], rt1[:], midb[:], ALU.subtract).then_inc(s_bc, 1)
                    v.tensor_copy(BC3[32:64, cs], midb[32:64, :]).then_inc(s_bc, 1)
                    dve.wait_ge(s_bc, n0 + 5)
                    v.tensor_copy(BC3[64:96, cs], rt2[64:96, :]).then_inc(s_bc, 1)
                    dve.wait_ge(s_xd, 2 * c + 2)
                    v.tensor_copy(lr[:], bank[5][0:R, :]).then_inc(s_bc, 1)

                for c in range(C):
                    norm(c)
                    conv(c)
                    split(c)
                for c in range(C):
                    cs = slice(c * CW, (c + 1) * CW)
                    dve.wait_ge(s_sp, 2)
                    nc.vector.tensor_tensor(dt[:, :, cs], dt[:, :, cs], dtx[:, :, cs], ALU.add).then_inc(s_dt, 1)
                    dve.wait_ge(s_dt, c + 1)
                    nc.vector.tensor_tensor(dtx[:, :, cs], dt[:, :, cs], xc[:, :, cs], ALU.mult)

            @block.tensor
            def _(pe):
                pe.wait_ge(wl, 16 * len(wloads))
                pe.wait_ge(s_A, 1)
                for c in range(C):
                    cs = slice(c * CW, (c + 1) * CW)
                    k.norm_tensor(L0 + c)
                    pe.wait_ge(k.ln_ev, L0 + c + 1)
                    if c:
                        pe.wait_ge(s_inev, 2 * H * c)
                    for b in range(2 * H):
                        nc.tensor.matmul(bank[b][:], inw[:, b * P:(b + 1) * P], k.xnT[:, cs], start=True, stop=True)\
                            .then_inc(s_in, 1)
                    pe.wait_ge(s_xc, c + 1)
                    if c:
                        pe.wait_ge(s_bc, 8 * c)
                        pe.wait_ge(s_dta, 2 * H * c)
                    for hh in range(H):
                        last = nc.tensor.matmul(bank[4][0:96, :], xpw3[:, hh].rearrange("p a b -> p (a b)"),
                                                xc[:, hh, cs], start=(hh == 0), stop=(hh == H - 1))
                    last.then_inc(s_xd, 1)
                    for hh in range(H):
                        last = nc.tensor.matmul(bank[5][0:R, :], xpw[:, hh, 0:R], xc[:, hh, cs],
                                                start=(hh == 0), stop=(hh == H - 1))
                    last.then_inc(s_xd, 1)
                    pe.wait_ge(s_bc, 8 * c + 8)
                    for hh in range(H):
                        if hh or c:
                            pe.wait_ge(s_dta, 2 * (c * H + hh))
                        nc.tensor.matmul(bank[6][:], dtw[:, hh * P:(hh + 1) * P], lr[:], start=True, stop=True)\
                            .then_inc(s_dtm, 1)

            @block.scalar
            def _(act):
                act.wait_ge(wl, 16 * len(wloads))
                act.wait_ge(sel0, 1)
                for c in range(C):
                    cs = slice(c * CW, (c + 1) * CW)
                    act.wait_ge(k.ln_tr, L0 + c + 1)
                    nc.scalar.activation(k.xnT[:, cs], bank[7][:], ACT.Identity, bias=b1[:], scale=g1[:])\
                        .then_inc(k.ln_ev, 1)
                    for b in range(2 * H):
                        act.wait_ge(s_in, 2 * H * c + b + 1)
                        if b < H:
                            nc.scalar.activation(xi[:, b, PAD + c * CW:PAD + (c + 1) * CW], bank[b][:], ACT.Copy)\
                                .then_inc(s_inev, 1)
                        else:
                            nc.scalar.activation(sz[:, b - H, cs], bank[b][:], ACT.Silu).then_inc(s_inev, 1)
                    act.wait_ge(s_cv, KC * H * (c + 1))
                    nc.scalar.activation(xc[:, :, cs], xc[:, :, cs], ACT.Silu).then_inc(s_xc, 1)
                    for hh in range(H):
                        act.wait_ge(s_dtm, c * H + hh + 1)
                        nc.scalar.activation(dt[:, hh, cs], bank[6][:], ACT.Relu, bias=dtb[:, hh:hh + 1])\
                            .then_inc(s_dta, 1)
                        nc.scalar.activation(dtx[:, hh, cs], bank[6][:], ACT.Abs, bias=dtb[:, hh:hh + 1])\
                            .then_inc(s_dta, 1)
                act.wait_ge(s_dta, 2 * H * C)
                nc.scalar.activation(dtx[:], dtx[:], ACT.Exp, scale=-1.0).then_inc(s_sp, 1)
                nc.scalar.activation(A[:], A[:], ACT.Exp).then_inc(s_A, 1)
                act.wait_ge(s_sp, 1)
                nc.scalar.activation(dtx[:], dtx[:], ACT.Ln, bias=1.0).then_inc(s_sp, 1)
                act.wait_ge(s_A, 2)
                nc.scalar.mul(A[:], A[:], -1.0)
        k.L += C

        q_bc = k.sem("q_bc")
        q_dA = k.sem("q_dA")
        q_cs = k.sem("q_cs")
        q_dBx = k.sem("q_dBx")
        q_h = k.sem("q_h")
        q_hC = k.sem("q_hC")
        q_st = k.sem("q_st")
        q_y = k.sem("q_y")
        q_yc = k.sem("q_yc")
        q_yg = k.sem("q_yg")
        yT = sb("yT", [P, H, CW])
        o_mm = k.sem("o_mm")
        o_x1 = k.sem("o_x1")
        x1 = xo
        assert H == 2
        with nc.Block() as block:
            def y_sum(pe, c, n):
                pe.wait_ge(q_hC, c * NS + n + 1)
                for hh in range(H):
                    last = nc.tensor.matmul(bank[4 + hh][:], k.ident[:], hC[:, n % 2, hh, :],
                                            start=(n == 0), stop=(n == NS - 1))
                last.then_inc(q_y, 1)

            @block.tensor
            def _(pe):
                nc.tensor.sem_inc(q_bc, 4)
                nc.tensor.sem_inc(q_y, 1)
                with pe.Fori(0, C) as c:
                    for n in range(NS):
                        u = c * NS + n
                        if n >= 2:
                            pe.wait_ge(q_dBx, u - 1)
                            pe.wait_ge(q_cs, u - 1)
                        for j in range(2):
                            nc.tensor.matmul(bank[2 * j + n % 2][:], sel[:, j * NS + n, :],
                                             BC3[:, bass.ds(c * CW, CW)], start=True, stop=True).then_inc(q_bc, 1)
                        if n >= 1:
                            y_sum(pe, c, n - 1)
                    y_sum(pe, c, NS - 1)
                    pe.wait_ge(q_yg, c + 1)
                    for i in range(CT):
                        for hh in range(H):
                            last = nc.tensor.matmul(bank[6][:, i * P:(i + 1) * P], yT[:, hh, i * P:(i + 1) * P],
                                                    outw[:, hh, :], start=(hh == 0), stop=(hh == H - 1))
                    last.then_inc(o_mm, 1)
                    pe.wait_ge(o_x1, c + 1)

            @block.scalar
            def _(act):
                with act.Fori(0, C) as c:
                    for n in range(NS):
                        u = c * NS + n
                        if n >= 2:
                            k.wait_alone(act, q_h, 2 * u - 2)
                        for hh in range(H):
                            nc.scalar.activation(dA[:, n % 2, hh, :], dt[:, hh, bass.ds(c * CW, CW)], ACT.Exp,
                                                 scale=A[:, hh, n:n + 1]).then_inc(q_dA, 1)
                        act.wait_ge(q_bc, 2 * u + 2 + 4)
                        if n >= 2:
                            act.wait_ge(q_hC, u - 1)
                        nc.scalar.activation(Cs[:, n % 2, :], bank[2 + n % 2][:], ACT.Copy).then_inc(q_cs, 1)
                    act.wait_ge(q_hC, c * NS + NS)

            @block.vector
            def _(dve):
                with dve.Fori(0, C) as c:
                    for n in range(NS):
                        u = c * NS + n
                        dve.wait_ge(q_bc, 2 * u + 1 + 4)
                        nc.vector.tensor_tensor(dBx[:, n % 2], dtx[:, :, bass.ds(c * CW, CW)],
                                                bank[n % 2][:, None, :].to_broadcast([P, H, CW]), ALU.mult)\
                            .then_inc(q_dBx, 1)
                        dve.wait_ge(q_dBx, u + 1)
                        dve.wait_ge(q_dA, 2 * u + 2)
                        if n >= 2:
                            dve.wait_ge(q_hC, u - 1)
                            dve.wait_ge(q_st, u - 1)
                        for hh in range(H):
                            nc.vector.tensor_tensor_scan(h[:, n % 2, hh, :], dA[:, n % 2, hh, :], dBx[:, n % 2, hh, :],
                                                         state[:, n, hh:hh + 1], ALU.mult, ALU.add).then_inc(q_h, 1)
                    dve.wait_ge(q_y, c * NS + NS + 1)
                    for hh in range(H):
                        nc.vector.scalar_tensor_tensor(out=yT[:, hh, :], in0=xc[:, hh, bass.ds(c * CW, CW)],
                                                       scalar=Dp[:, hh:hh + 1], in1=bank[4 + hh][:],
                                                       op0=ALU.mult, op1=ALU.add).then_inc(q_yc, 1)
                    dve.wait_ge(q_yc, 2 * c + 2)
                    nc.vector.tensor_tensor(yT[:], yT[:], sz[:, :, bass.ds(c * CW, CW)], ALU.mult).then_inc(q_yg, 1)
                    dve.wait_ge(o_mm, c + 1)
                    xt = x1[:, bass.ds(c * CT, CT), :]
                    nc.vector.tensor_tensor(xt, bank[6][:].rearrange("p (i d) -> p i d", i=CT), xt, ALU.add)\
                        .then_inc(o_x1, 1)
                    dve.wait_ge(q_st, c * NS + NS)

            @block.gpsimd
            def _(pool):
                with pool.Fori(0, C) as c:
                    for n in range(NS):
                        u = c * NS + n
                        pool.wait_ge(q_h, 2 * u + 2)
                        pool.wait_ge(q_cs, u + 1)
                        if n >= 2:
                            pool.wait_ge(q_y, u - 1 + 1)
                        nc.gpsimd.tensor_tensor(hC[:, n % 2], h[:, n % 2],
                                                Cs[:, n % 2, None, :].to_broadcast([P, H, CW]), ALU.mult)\
                            .then_inc(q_hC, 1)
                        nc.gpsimd.tensor_copy(state[:, n, :], h[:, n % 2, :, CW - 1]).then_inc(q_st, 1)
                    pool.wait_ge(q_y, c * NS + NS + 1)

        hT = [dtx[:].rearrange("p h n -> p (h n)")[:, b * FB * CW:(b + 1) * FB * CW].rearrange("p (f w) -> p f w", f=FB)
              for b in range(2)]
        f_x = k.sem("f_x")
        f_cp = k.sem("f_cp")
        f_h = k.sem("f_h")
        f_ev = k.sem("f_ev")
        f_y = k.sem("f_y")
        L1 = k.L
        with nc.Block() as block:
            @block.gpsimd
            def _(pool):
                for c in range(C):
                    k.norm_pool(L1 + c)

            @block.vector
            def _(dve):
                for c in range(C):
                    xt = k.X[:, c * CT:(c + 1) * CT, :]
                    nc.vector.tensor_tensor(xt, xt, x1[:, c * CT:(c + 1) * CT, :], ALU.add).then_inc(f_x, 1)
                keep, k.X = k.X, x1
                for c in range(C):
                    k.norm_vector(L1 + c, c)
                k.X = keep
                for c in range(C):
                    dve.wait_ge(f_x, c + 1)
                    dve.wait_ge(f_y, c + 1)
                    xt = k.X[:, c * CT:(c + 1) * CT, :]
                    nc.vector.tensor_tensor(xt, bank[4 + c % 2][:].rearrange("p (i d) -> p i d", i=CT), xt, ALU.add)\
                        .then_inc(f_cp, 1)

            @block.tensor
            def _(pe):
                for c in range(C):
                    k.norm_tensor(L1 + c)
                    pe.wait_ge(k.ln_ev, L1 + c + 1)
                    for f in range(FB):
                        if c:
                            pe.wait_ge(f_ev, (c - 1) * FB + f + 1)
                        nc.tensor.matmul(bank[f][:], w1[:, f * P:(f + 1) * P], k.xnT[:, c * CW:(c + 1) * CW],
                                         start=True, stop=True).then_inc(f_h, 1)
                    if c >= 2:
                        pe.wait_ge(f_cp, c - 1)
                    pe.wait_ge(f_ev, c * FB + FB)
                    for i in range(CT):
                        dst = bank[4 + c % 2][:, i * P:(i + 1) * P]
                        nc.tensor.matmul(dst, k.ones[0:1, :], w2b[:], start=True, stop=False)
                        for f in range(FB):
                            last = nc.tensor.matmul(dst, hT[c % 2][:, f, i * P:(i + 1) * P], w2[:, f, :],
                                                    start=False, stop=(f == FB - 1))
                    last.then_inc(f_y, 1)

            @block.scalar
            def _(act):
                for c in range(C):
                    act.wait_ge(k.ln_tr, L1 + c + 1)
                    nc.scalar.activation(k.xnT[:, c * CW:(c + 1) * CW], bank[7][:], ACT.Identity, bias=b2[:],
                                         scale=g2[:]).then_inc(k.ln_ev, 1)
                    for f in range(FB):
                        act.wait_ge(f_h, c * FB + f + 1)
                        if c >= 2:
                            act.wait_ge(f_y, c - 1)
                        nc.scalar.activation(hT[c % 2][:, f, :], bank[f][:], ACT.Gelu_apprx_tanh,
                                             bias=w1b[:, f:f + 1]).then_inc(f_ev, 1)
        k.L += C


def top_two(k, dve, act_sem, src, top, ti, tf, s):
    nc = k.nc
    for i in range(k.T):
        last = nc.vector.max(top[:, i, :], src[:, i, :])
    last.then_inc(s, 1)
    dve.wait_ge(s, act_sem + 1)
    for i in range(k.T):
        last = nc.vector.max_index(ti[:, i, :], top[:, i, :], src[:, i, :])
    last.then_inc(s, 1)
    dve.wait_ge(s, act_sem + 2)
    nc.vector.tensor_copy(tf[:], ti[:, :, 0:2]).then_inc(s, 1)


def experts(k, name, gated):
    nc, t, C, T, E = k.nc, k.t, k.C, k.T, k.E
    L0, bank, pre = k.L, k.bank, name
    FB = t[pre + "_w1"].shape[2] // P
    tmp = ExitStack()
    sb = lambda n, shape, dt=F32: k.sb(f"{name}_{n}", shape, dt, tmp)
    sem = lambda n: k.sem(f"{name}_{n}")
    with tmp:
        gw = sb("gw", [P, E])
        gb = sb("gb", [1, E])
        lg = sb("lg", [P, T, E])
        top = sb("top", [P, T, E])
        ti = sb("ti", [P, T, E], U32)
        tf = sb("tf", [P, T, 2])
        ex = sb("ex", [P, T])
        den = sb("den", [P, T])
        wt = sb("wt", [P, 2, T])
        pick = sb("pick", [P, 2, T])
        comb = sb("comb", [P, E, T])
        wa = [sb(f"wa{u}", [P, FB * P]) for u in range(2)]
        wu = [sb(f"wu{u}", [P, FB * P]) for u in range(2)] if gated else None
        wd = [sb(f"wd{u}", [P, FB, P]) for u in range(2)]
        ba = None if gated else [sb(f"ba{u}", [P, FB]) for u in range(2)]
        bd = None if gated else [sb(f"bd{u}", [1, P]) for u in range(2)]
        sg = sb("sg", [P, 2, CW]) if gated else None
        hT = [sb(f"hT{b}", [P, FB, CW]) for b in range(2)]
        NH = 2 if gated else 4
        ND = 3 if gated else 4

        g_w, g_mm, g_top, g_ex, g_cb = sem("gate_w"), sem("gate_mm"), sem("gate_top"), sem("gate_ex"), sem("gate_cb")
        w_ready = [sem(f"w_ready{u}") for u in range(2)]
        s_h, s_sg, s_hev, s_y, s_x, s_e = (sem(n) for n in ("h", "sg", "hev", "y", "x", "e_done"))

        with nc.Block() as block:
            @block.sync
            def _(sp):
                sp.dma_start(gw[:], t[pre + "_gate_w"]).then_inc(g_w, 16)
                if not gated:
                    sp.dma_start(gb[:], t[pre + "_gate_b"].rearrange("(o e) -> o e", o=1)).then_inc(g_w, 16)

            @block.gpsimd
            def _(pool):
                for c in range(C):
                    k.norm_pool(L0 + c)

            @block.scalar
            def _(act):
                for c in range(C):
                    k.norm_scalar(L0 + c, k.xnT[:, c * CW:(c + 1) * CW])
                act.wait_ge(g_cb, 2)
                nc.scalar.activation(ex[:], den[:], ACT.Exp).then_inc(g_ex, 1)

            @block.tensor
            def _(pe):
                pe.wait_ge(g_w, 16 if gated else 32)
                for c in range(C):
                    k.norm_tensor(L0 + c)
                    pe.wait_ge(k.ln_ev, L0 + c + 1)
                    for i in range(c * CT, (c + 1) * CT):
                        dst = bank[6][:, i * E:(i + 1) * E]
                        last = nc.tensor.matmul(dst, k.xnT[:, i * P:(i + 1) * P], gw[:], start=True, stop=gated)
                        if not gated:
                            last = nc.tensor.matmul(dst, k.ones[0:1, :], gb[:], start=False, stop=True)
                last.then_inc(g_mm, 1)

            @block.vector
            def _(dve):
                for c in range(C):
                    k.norm_vector(L0 + c, c)
                dve.wait_ge(g_mm, 1)
                nc.vector.tensor_copy(lg[:], bank[6][:, 0:T * E].rearrange("p (t e) -> p t e", t=T)).then_inc(g_cb, 1)
                dve.wait_ge(g_cb, 1)
                top_two(k, dve, 0, lg, top, ti, tf, g_top)
                nc.vector.tensor_tensor(den[:], top[:, :, 1], top[:, :, 0], ALU.subtract).then_inc(g_cb, 1)
                dve.wait_ge(g_ex, 1)
                nc.vector.tensor_scalar(den[:], ex[:], 1.0, None, ALU.add).then_inc(g_cb, 1)
                dve.wait_ge(g_cb, 3)
                nc.vector.reciprocal(wt[:, 0, :], den[:]).then_inc(g_cb, 1)
                dve.wait_ge(g_cb, 4)
                nc.vector.tensor_tensor(wt[:, 1, :], ex[:], wt[:, 0, :], ALU.mult).then_inc(g_cb, 1)
                dve.wait_ge(g_cb, 5)
                dve.wait_ge(g_top, 3)
                for e in range(E):
                    if e:
                        dve.wait_ge(g_cb, 5 + 2 * e)
                    for j in range(2):
                        last = nc.vector.scalar_tensor_tensor(out=pick[:, j, :], in0=tf[:, :, j], scalar=float(e),
                                                              in1=wt[:, j, :], op0=ALU.is_equal, op1=ALU.mult)
                    last.then_inc(g_cb, 1)
                    dve.wait_ge(g_cb, 6 + 2 * e)
                    nc.vector.tensor_tensor(comb[:, e, :], pick[:, 0, :], pick[:, 1, :], ALU.add).then_inc(g_cb, 1)
        k.L += C

        with nc.Block() as block:
            @block.sync
            def _(sp):
                with nc.allow_non_contiguous_dma(reason="bias columns"):
                    with sp.Fori(0, E // 2) as ep:
                        for u in range(2):
                            e = ep * 2 + u
                            sp.wait_ge(s_e, e + 1)
                            one = lambda n: t[pre + n][bass.ds(e, 1)]
                            loads = [(wa[u][:], one("_w1").rearrange("o p f -> (o p) f")),
                                     (wd[u][:], one("_w2").rearrange("o (f p) d -> (o p) f d", p=P))]
                            if gated:
                                loads.append((wu[u][:], one("_wu").rearrange("o p f -> (o p) f")))
                            else:
                                loads.append((ba[u][:], one("_b1").rearrange("o (f p) -> (o p) f", p=P)))
                                loads.append((bd[u][:], one("_b2")))
                            for dst, src in loads:
                                sp.dma_start(dst, src).then_inc(w_ready[u], 16)

            @block.tensor
            def _(pe):
                nc.tensor.sem_inc(s_e, 2)
                nc.tensor.sem_inc(s_y, 2)

                def hidden(ep, u, c):
                    q = (ep * 2 + u) * C + c
                    if c == 0:
                        pe.wait_ge(w_ready[u], (ep + 1) * (16 * ND))
                    for f in range(FB):
                        pe.wait_ge(s_hev, q * FB + f + 1)
                        xc = k.xnT[:, c * CW:(c + 1) * CW]
                        last = nc.tensor.matmul(bank[f % NH][:], wa[u][:, f * P:(f + 1) * P], xc, start=True, stop=True)
                        if gated:
                            last.then_inc(s_h, 1)
                            last = nc.tensor.matmul(bank[2 + f % 2][:], wu[u][:, f * P:(f + 1) * P], xc,
                                                    start=True, stop=True)
                        last.then_inc(s_h, 1)

                def down(ep, u, c):
                    q = (ep * 2 + u) * C + c
                    pe.wait_ge(s_hev, q * FB + FB + NH)
                    pe.wait_ge(s_x, q + 1)
                    for i in range(CT):
                        dst = bank[4 + c % 2][:, i * P:(i + 1) * P]
                        if not gated:
                            nc.tensor.matmul(dst, k.ones[0:1, :], bd[u][:], start=True, stop=False)
                        for f in range(FB):
                            last = nc.tensor.matmul(dst, hT[c % 2][:, f, i * P:(i + 1) * P], wd[u][:, f, :],
                                                    start=(gated and f == 0), stop=(f == FB - 1))
                    last.then_inc(s_y, 1)

                with pe.Fori(0, E // 2) as ep:
                    units = [(u, c) for u in range(2) for c in range(C)]
                    hidden(ep, *units[0])
                    for n, unit in enumerate(units):
                        if n + 1 < len(units):
                            hidden(ep, *units[n + 1])
                        down(ep, *unit)
                        if unit[1] == C - 1:
                            nc.tensor.drain().then_inc(s_e, 1)

            @block.scalar
            def _(act):
                if not gated:
                    nc.scalar.sem_inc(s_hev, NH)
                with act.Fori(0, E // 2) as ep:
                    for u in range(2):
                        for c in range(C):
                            q = (ep * 2 + u) * C + c
                            for f in range(FB):
                                b = q * FB + f
                                if gated:
                                    act.wait_ge(s_hev, b + 1)
                                    act.wait_ge(s_h, 2 * b + 1)
                                    nc.scalar.activation(sg[:, f % 2, :], bank[f % 2][:], ACT.Silu).then_inc(s_sg, 1)
                                else:
                                    if f == 0:
                                        act.wait_ge(s_y, q + 1)
                                    act.wait_ge(s_h, b + 1)
                                    nc.scalar.activation(hT[c % 2][:, f, :], bank[f][:], ACT.Relu,
                                                         bias=ba[u][:, f:f + 1]).then_inc(s_hev, 1)

            @block.vector
            def _(dve):
                nc.vector.sem_inc(s_x, 2)
                if gated:
                    nc.vector.sem_inc(s_hev, NH)

                def up(ep, u, c):
                    q = (ep * 2 + u) * C + c
                    for f in range(FB):
                        b = q * FB + f
                        if f == 0:
                            dve.wait_ge(s_y, q + 1)
                        dve.wait_ge(s_h, 2 * b + 2)
                        dve.wait_ge(s_sg, b + 1)
                        nc.vector.tensor_tensor(hT[c % 2][:, f, :], bank[2 + f % 2][:], sg[:, f % 2, :], ALU.mult)\
                            .then_inc(s_hev, 1)

                def add(ep, u, c):
                    e = ep * 2 + u
                    q = e * C + c
                    dve.wait_ge(s_x, q + 1)
                    dve.wait_ge(s_y, q + 1 + 2)
                    for i in range(CT):
                        xt = k.X[:, c * CT + i, :]
                        last = nc.vector.scalar_tensor_tensor(
                            out=xt, in0=bank[4 + c % 2][:, i * P:(i + 1) * P],
                            scalar=comb[:, bass.ds(e, 1), c * CT + i], in1=xt, op0=ALU.mult, op1=ALU.add)
                    last.then_inc(s_x, 1)

                with dve.Fori(0, E // 2) as ep:
                    units = [(u, c) for u in range(2) for c in range(C)]
                    if gated:
                        up(ep, *units[0])
                    for n, unit in enumerate(units):
                        if gated and n + 1 < len(units):
                            up(ep, *units[n + 1])
                        add(ep, *unit)


def linear(k):
    nc, t, C, T = k.nc, k.t, k.C, k.T
    L0, bank = k.L, k.bank
    EPSA = 1e-6
    tmp = ExitStack()
    sb = lambda n, shape, dt=F32: k.sb("lin_" + n, shape, dt, tmp)
    sem = lambda n: k.sem("lin_" + n)
    with tmp:
        wqk, bqk, wv = sb("wqk", [P, 2 * P]), sb("bqk", [1, 2 * P]), sb("wv", [P, P])
        bv, gam = sb("bv", [P, 1]), sb("gam", [P, 1])
        qk, sq = sb("qk", [P, 2, 2 * P]), sb("sq", [P, 2, 2 * P])
        half = sb("half", [P, P])
        sums = sb("sums", [P, 2 * P])
        nk = sb("nk", [P, 1])
        Gn, tl, H, M = (sb(n, [P, P]) for n in ("Gn", "tl", "H", "M"))
        rrow = sb("rrow", [1, P])
        lw, s_qk, s_ev, s_g, s_p, s_v, s_m, s_h = (sem(n) for n in ("w", "qk", "ev", "g", "pow", "v", "m", "half"))
        s_o, s_x = sem("o"), sem("x")
        with nc.Block() as block:
            @block.sync
            def _(sp):
                with nc.allow_non_contiguous_dma(reason="small weights"):
                    for dst, src in ((wqk[:, 0:P], t["lin_wqT"]), (wqk[:, P:2 * P], t["lin_wkT"]), (wv[:], t["lin_wv"]),
                                     (bqk[:, 0:P], t["lin_bq"].rearrange("(o d) -> o d", o=1)),
                                     (bqk[:, P:2 * P], t["lin_bk"].rearrange("(o d) -> o d", o=1)),
                                     (bv[:], t["lin_bv"].rearrange("(d o) -> d o", o=1)),
                                     (gam[:], t["lin_gamma"].partition_broadcast(P))):
                        sp.dma_start(dst, src).then_inc(lw, 16)

            @block.gpsimd
            def _(pool):
                nc.gpsimd.memset(half[:], -0.5).then_inc(s_h, 1)
                for c in range(C):
                    k.norm_pool(L0 + c)
                pool.wait_ge(s_h, 1)
                pool.wait_ge(s_v, 2)
                nc.gpsimd.tensor_tensor(sums[:, P:2 * P], sums[:, P:2 * P], half[:], ALU.pow).then_inc(s_p, 1)
                nc.gpsimd.tensor_tensor(nk[:], nk[:], half[:, 0:1], ALU.pow).then_inc(s_p, 1)

            @block.scalar
            def _(act):
                for c in range(C):
                    k.norm_scalar(L0 + c, k.xnT[:, c * CW:(c + 1) * CW])
                    for i in range(c * CT, (c + 1) * CT):
                        act.wait_ge(s_qk, i + 1)
                        if i >= 2:
                            act.wait_ge(s_g, i - 1)
                        nc.scalar.activation(qk[:, i % 2, :], bank[i % 2][:, 0:2 * P], ACT.Copy).then_inc(s_ev, 1)
                        nc.scalar.activation(sq[:, i % 2, :], bank[i % 2][:, 0:2 * P], ACT.Square).then_inc(s_ev, 1)

            @block.tensor
            def _(pe):
                pe.wait_ge(lw, 16 * 7)

                def gram(i):
                    pe.wait_ge(s_ev, 2 * i + 2)
                    q, kk, q2, k2 = (a[:, i % 2, b * P:(b + 1) * P] for a in (qk, sq) for b in range(2))
                    f, z = i == 0, i == T - 1
                    nc.tensor.matmul(bank[2][:, 0:P], kk, q, start=f, stop=z)
                    nc.tensor.matmul(bank[3][:, 0:P], k.ones[:], q, start=f, stop=z)
                    nc.tensor.matmul(bank[4][:, 0:P], k.ones[:], q2, start=f, stop=z)
                    nc.tensor.matmul(bank[5][:, 0:1], k2, k.ones[:, 0:1], start=f, stop=z).then_inc(s_g, 1)

                for c in range(C):
                    k.norm_tensor(L0 + c)
                    pe.wait_ge(k.ln_ev, L0 + c + 1)
                    for i in range(c * CT, (c + 1) * CT):
                        if i >= 2:
                            pe.wait_ge(s_ev, 2 * i - 2)
                        nc.tensor.matmul(bank[i % 2][:, 0:2 * P], k.xnT[:, i * P:(i + 1) * P], wqk[:], start=True, stop=False)
                        nc.tensor.matmul(bank[i % 2][:, 0:2 * P], k.ones[0:1, :], bqk[:], start=False, stop=True)\
                            .then_inc(s_qk, 1)
                        if i:
                            gram(i - 1)
                gram(T - 1)
                pe.wait_ge(s_v, 3)
                nc.tensor.matmul(bank[3][:, 0:P], k.ones[:], Gn[:], start=True, stop=True).then_inc(s_m, 1)
                pe.wait_ge(s_v, 8)
                nc.tensor.matmul(bank[4][:, 0:P], wv[:], H[:], start=True, stop=True)
                nc.tensor.matmul(bank[5][0:1, 0:P], bv[:], H[:], start=True, stop=True).then_inc(s_m, 1)

            @block.vector
            def _(dve):
                v = nc.vector
                for c in range(C):
                    k.norm_vector(L0 + c, c)
                dve.wait_ge(lw, 16 * 7)
                dve.wait_ge(s_g, T)
                v.tensor_copy(sums[:, 0:P], bank[3][:, 0:P])
                v.tensor_copy(sums[:, P:2 * P], bank[4][:, 0:P]).then_inc(s_v, 1)
                v.tensor_copy(nk[:], bank[5][:, 0:1]).then_inc(s_v, 1)
                dve.wait_ge(s_p, 2)
                v.scalar_tensor_tensor(out=Gn[:], in0=bank[2][:, 0:P], scalar=nk[:], in1=sums[:, P:2 * P],
                                       op0=ALU.mult, op1=ALU.mult).then_inc(s_v, 1)
                dve.wait_ge(s_v, 3)
                v.scalar_tensor_tensor(out=tl[:], in0=sums[:, 0:P], scalar=EPSA, in1=sums[:, P:2 * P],
                                       op0=ALU.mult, op1=ALU.mult).then_inc(s_v, 1)
                dve.wait_ge(s_v, 4)
                dve.wait_ge(s_m, 1)
                v.scalar_tensor_tensor(out=tl[:], in0=tl[:], scalar=float(P), in1=bank[3][:, 0:P],
                                       op0=ALU.add, op1=ALU.add).then_inc(s_v, 1)
                dve.wait_ge(s_v, 5)
                v.reciprocal(tl[:], tl[:]).then_inc(s_v, 1)
                dve.wait_ge(s_v, 6)
                v.scalar_tensor_tensor(out=H[:], in0=Gn[:], scalar=1.0, in1=tl[:], op0=ALU.add, op1=ALU.mult)\
                    .then_inc(s_v, 1)
                dve.wait_ge(s_v, 7)
                v.tensor_scalar(H[:], H[:], gam[:], None, ALU.mult).then_inc(s_v, 1)
                dve.wait_ge(s_m, 2)
                v.tensor_tensor(M[:], bank[4][:, 0:P], k.ident[:], ALU.add)
                v.tensor_copy(rrow[:], bank[5][0:1, 0:P])
        k.L += C
        with nc.Block() as block:
            @block.tensor
            def _(pe):
                for c in range(C):
                    if c >= 2:
                        pe.wait_ge(s_x, c - 1)
                    for i in range(CT):
                        dst = bank[c % 2][:, i * P:(i + 1) * P]
                        a = (c * CT + i) * P
                        nc.tensor.matmul(dst, k.xnT[:, a:a + P], M[:], start=True, stop=False)
                        last = nc.tensor.matmul(dst, k.ones[0:1, :], rrow[:], start=False, stop=True)
                    last.then_inc(s_o, 1)

            @block.vector
            def _(dve):
                for c in range(C):
                    dve.wait_ge(s_o, c + 1)
                    xt = k.X[:, c * CT:(c + 1) * CT, :]
                    nc.vector.tensor_tensor(xt, bank[c % 2][:].rearrange("p (i d) -> p i d", i=CT), xt, ALU.add)\
                        .then_inc(s_x, 1)


def deep(k):
    nc, t, C, T, E = k.nc, k.t, k.C, k.T, k.E
    L0, bank = k.L, k.bank
    tmp = ExitStack()
    sb = lambda n, shape, dt=F32: k.sb("deep_" + n, shape, dt, tmp)
    sem = lambda n: k.sem("deep_" + n)
    with tmp:
        gw, gb = sb("gw", [P, E]), sb("gb", [E, 1])
        w1, w2, w3 = (sb(n, [P, E, P]) for n in ("w1", "w2", "w3"))
        c1, c2, r3 = sb("c1", [P, E]), sb("c2", [P, E]), sb("r3", [1, E, P])
        W = [sb(f"W{i}", [P, 3, P]) for i in range(2)]
        lg = sb("lg", [E, k.N])
        mx, sm = sb("mx", [E, 1]), sb("sm", [E, 1])
        pr, top, ti = sb("pr", [P, T, E]), sb("top", [P, T, E]), sb("ti", [P, T, E], U32)
        tf = sb("tf", [P, T, 2])
        pick = sb("pick", [P, 4, T])
        comb, ind = sb("comb", [P, E, T]), sb("ind", [P, T, E])
        h1 = [sb(f"h1{b}", [P, CW]) for b in range(2)]
        h2 = [sb(f"h2{b}", [P, CW]) for b in range(2)]
        ry = [sb(f"ry{b}", [P, CW]) for b in range(2)]
        vrow, vE = sb("vrow", [1, E, P]), sb("vE", [E, P])
        indT = sb("indT", [E, T, P])
        lw, s_lg, s_lge, s_sm, s_ex, s_pt, s_pc, s_top, s_cb = (
            sem(n) for n in ("w", "lg", "lge", "sm", "ex", "pt", "pc", "top", "cb"))
        with nc.Block() as block:
            @block.sync
            def _(sp):
                with nc.allow_non_contiguous_dma(reason="small weights"):
                    for dst, src in ((gw[:], t["deep_gate_w"]), (gb[:], t["deep_gate_b"].rearrange("(e o) -> e o", o=1)),
                                     (w1[:], t["deep_w1"].rearrange("e p o -> p e o")),
                                     (w2[:], t["deep_w2"].rearrange("e p o -> p e o")),
                                     (w3[:], t["deep_w3"].rearrange("e p o -> p e o")),
                                     (c1[:], t["deep_b1"].rearrange("e p -> p e")),
                                     (c2[:], t["deep_b2"].rearrange("e p -> p e")),
                                     (r3[:], t["deep_b3"].rearrange("(o e) p -> o e p", o=1))):
                        sp.dma_start(dst, src).then_inc(lw, 16)

            @block.gpsimd
            def _(pool):
                for c in range(C):
                    k.norm_pool(L0 + c)

            @block.scalar
            def _(act):
                act.wait_ge(lw, 16 * 8)
                for c in range(C):
                    k.norm_scalar(L0 + c, k.xnT[:, c * CW:(c + 1) * CW])
                    act.wait_ge(s_lg, c + 1)
                    nc.scalar.activation(lg[:, c * CW:(c + 1) * CW], bank[c % 2][0:E, :], ACT.Identity, bias=gb[:])\
                        .then_inc(s_lge, 1)
                act.wait_ge(s_sm, 1)
                nc.scalar.activation(lg[:], lg[:], ACT.Exp, bias=mx[:], accum_out=sm[:]).then_inc(s_ex, 1)

            @block.tensor
            def _(pe):
                pe.wait_ge(lw, 16 * 8)
                for c in range(C):
                    k.norm_tensor(L0 + c)
                    pe.wait_ge(k.ln_ev, L0 + c + 1)
                    if c >= 2:
                        pe.wait_ge(s_lge, c - 1)
                    nc.tensor.matmul(bank[c % 2][0:E, :], gw[:], k.xnT[:, c * CW:(c + 1) * CW], start=True, stop=True)\
                        .then_inc(s_lg, 1)
                pe.wait_ge(s_sm, 3)
                for i in range(T):
                    last = nc.tensor.transpose(bank[2][:, i * E:(i + 1) * E], lg[:, i * P:(i + 1) * P], k.ident[0:E, 0:E])
                last.then_inc(s_pt, 1)
                pe.wait_ge(s_cb, 1 + E)
                for h in range(T // CT):
                    for i in range(CT):
                        last = nc.tensor.transpose(bank[3 + h][0:E, i * P:(i + 1) * P], ind[:, h * CT + i, :], k.ident[:])
                    last.then_inc(s_pt, 1)

            @block.vector
            def _(dve):
                v = nc.vector
                for c in range(C):
                    k.norm_vector(L0 + c, c)
                dve.wait_ge(s_lge, C)
                v.tensor_reduce(mx[:], lg[:], AX.X, ALU.max, negate=True).then_inc(s_sm, 1)
                dve.wait_ge(s_ex, 1)
                v.reciprocal(sm[:], sm[:]).then_inc(s_sm, 1)
                dve.wait_ge(s_sm, 2)
                v.tensor_scalar(lg[:], lg[:], sm[:], None, ALU.mult).then_inc(s_sm, 1)
                dve.wait_ge(s_pt, 1)
                v.tensor_copy(pr[:], bank[2][:, 0:T * E].rearrange("p (t e) -> p t e", t=T)).then_inc(s_cb, 1)
                dve.wait_ge(s_cb, 1)
                top_two(k, dve, 0, pr, top, ti, tf, s_top)
                dve.wait_ge(s_top, 3)
                for e in range(E):
                    if e:
                        dve.wait_ge(s_cb, 1 + e)
                    for j in range(2):
                        v.scalar_tensor_tensor(out=pick[:, j, :], in0=tf[:, :, j], scalar=float(e),
                                               in1=top[:, :, j], op0=ALU.is_equal, op1=ALU.mult)
                        last = v.tensor_scalar(pick[:, 2 + j, :], tf[:, :, j], float(e), None, ALU.is_equal)
                    last.then_inc(s_pc, 1)
                    dve.wait_ge(s_pc, e + 1)
                    v.tensor_tensor(comb[:, e, :], pick[:, 0, :], pick[:, 1, :], ALU.add)
                    v.tensor_tensor(ind[:, :, e], pick[:, 2, :], pick[:, 3, :], ALU.add).then_inc(s_cb, 1)
                for h in range(T // CT):
                    dve.wait_ge(s_pt, 2 + h)
                    v.tensor_copy(indT[:, h * CT:(h + 1) * CT, :],
                                  bank[3 + h][0:E, :].rearrange("p (i q) -> p i q", i=CT))
        k.L += C

        s_W, s_a, s_ae, s_b, s_be, s_y, s_ye, s_v, s_ve, s_e, s_dma, s_o, s_x = (
            sem(n) for n in ("W", "a", "ae", "b", "be", "y", "ye", "v", "ve", "e", "dma", "o", "x"))
        with nc.Block() as block:
            @block.sync
            def _(sp):
                sp.wait_ge(s_ve, E)
                sp.dma_start(vE[:], vrow[:]).then_inc(s_dma, 16)

            @block.gpsimd
            def _(pool):
                for e in range(E):
                    if e >= 2:
                        pool.wait_ge(s_e, e - 1)
                    for n, w in enumerate((w1, w2, w3)):
                        last = nc.gpsimd.tensor_copy(W[e % 2][:, n, :], w[:, e, :])
                    last.then_inc(s_W, 1)

            @block.scalar
            def _(act):
                for e in range(E):
                    for c in range(C):
                        q = e * C + c
                        act.wait_ge(s_a, q + 1)
                        if q >= 2:
                            act.wait_ge(s_b, q - 1)
                        nc.scalar.activation(h1[c % 2][:], bank[c % 2][:], ACT.Relu, bias=c1[:, e:e + 1]).then_inc(s_ae, 1)
                        act.wait_ge(s_b, q + 1)
                        if q >= 2:
                            act.wait_ge(s_y, q - 1)
                        nc.scalar.activation(h2[c % 2][:], bank[2 + c % 2][:], ACT.Relu, bias=c2[:, e:e + 1])\
                            .then_inc(s_be, 1)

            @block.tensor
            def _(pe):
                def first(e, c):
                    q = e * C + c
                    if c == 0:
                        pe.wait_ge(s_W, e + 1)
                    if q >= 2:
                        pe.wait_ge(s_ae, q - 1)
                    nc.tensor.matmul(bank[c % 2][:], W[e % 2][:, 0, :], k.xnT[:, c * CW:(c + 1) * CW],
                                     start=True, stop=True).then_inc(s_a, 1)

                def second(e, c):
                    q = e * C + c
                    pe.wait_ge(s_ae, q + 1)
                    if q >= 2:
                        pe.wait_ge(s_be, q - 1)
                    nc.tensor.matmul(bank[2 + c % 2][:], W[e % 2][:, 1, :], h1[c % 2][:], start=True, stop=True)\
                        .then_inc(s_b, 1)

                def third(e, c):
                    q = e * C + c
                    pe.wait_ge(s_be, q + 1)
                    if q >= 2:
                        pe.wait_ge(s_ye, q - 1)
                    for i in range(CT):
                        dst = bank[4 + c % 2][:, i * P:(i + 1) * P]
                        nc.tensor.matmul(dst, h2[c % 2][:, i * P:(i + 1) * P], W[e % 2][:, 2, :], start=True, stop=False)
                        last = nc.tensor.matmul(dst, k.ones[0:1, :], r3[:, e, :], start=False, stop=True)
                    last.then_inc(s_y, 1)

                def total(e, c):
                    q = e * C + c
                    pe.wait_ge(s_ye, q + 1)
                    if c == 0 and e:
                        pe.wait_ge(s_ve, e)
                    nc.tensor.matmul(bank[6][0:1, :], k.ones[:, 0:1], ry[c % 2][:], start=(c == 0), stop=(c == C - 1))\
                        .then_inc(s_v, 1)

                units = [(e, c) for e in range(E) for c in range(C)]
                for n in range(len(units) + 3):
                    if n < len(units):
                        first(*units[n])
                    if 0 <= n - 1 < len(units):
                        second(*units[n - 1])
                    if 0 <= n - 2 < len(units):
                        third(*units[n - 2])
                        if units[n - 2][1] == C - 1:
                            nc.tensor.drain().then_inc(s_e, 1)
                    if 0 <= n - 3 < len(units):
                        total(*units[n - 3])
                pe.wait_ge(s_dma, 16)
                for c in range(C):
                    if c >= 2:
                        pe.wait_ge(s_x, c - 1)
                    for i in range(CT):
                        last = nc.tensor.matmul(bank[c % 2][:, i * P:(i + 1) * P], indT[:, c * CT + i, :], vE[:],
                                                start=True, stop=True)
                    last.then_inc(s_o, 1)

            def flush(dve, e):
                dve.wait_ge(s_v, C * (e + 1))
                nc.vector.tensor_reduce(vrow[:, e, :], bank[6][0:1, :].rearrange("p (i o) -> p o i", i=CT), AX.X, ALU.add)\
                    .then_inc(s_ve, 1)

            @block.vector
            def _(dve):
                v = nc.vector
                for e in range(E):
                    for c in range(C):
                        q = e * C + c
                        dve.wait_ge(s_y, q + 1)
                        if q >= 2:
                            dve.wait_ge(s_v, q - 1)
                        for i in range(CT):
                            last = v.tensor_scalar(ry[c % 2][:, i * P:(i + 1) * P], bank[4 + c % 2][:, i * P:(i + 1) * P],
                                                   0.0, comb[:, e, c * CT + i:c * CT + i + 1], ALU.max, ALU.mult)
                        last.then_inc(s_ye, 1)
                        if c == 0 and e:
                            flush(dve, e - 1)
                flush(dve, E - 1)
                for c in range(C):
                    dve.wait_ge(s_o, c + 1)
                    xt = k.X[:, c * CT:(c + 1) * CT, :]
                    v.tensor_tensor(xt, bank[c % 2][:].rearrange("p (i d) -> p i d", i=CT), xt, ALU.add).then_inc(s_x, 1)


def softmax_mixer(k, name, windowed):
    nc, t, C, T = k.nc, k.t, k.C, k.T
    bank = k.bank
    HEADS, HD = 16, P // 16
    G = HEADS // 2
    R = 4
    SLOTS = 8
    MAXROW = 6 * HD
    ROWS = MAXROW + 4
    WINDOW = 64
    SCALE = float(HD) ** -0.5
    NW = HEADS // 2
    heads = lambda w: (4 * (w // 2) + w % 2, 4 * (w // 2) + w % 2 + 2)
    tmp = ExitStack()
    sb = lambda n, shape, dt=F32: k.sb(f"{name}_{n}", shape, dt, tmp)
    sem = lambda n: k.sem(f"{name}_{n}")
    with tmp:
        wqkv, bqkv = sb("wqkv", [P, 3 * P]), sb("bqkv", [1, 3 * P])
        wo = sb("wo", [P, 4, P])
        biasf = sb("biasf", [P, 2, 2, P])
        q_bias = sb("q_bias", [P, 4 * P], BF16)
        k_bias = sb("k_bias", [P, 4 * P], BF16)
        spread = sb("spread", [P, P])
        raw = sb("raw", [P, 2, HEADS, HD // 2, 2]) if windowed else None
        rot = sb("rot", [P, 4, 2 * HEADS, HD // 2]) if windowed else None
        cs = sb("cs", [P, T, 2, HD // 2]) if windowed else None
        xs = sb("xs", [P, P])
        qk = sb("qk", [P, 2, HEADS, HD])
        left = sb("left", [P, 2, 2, HEADS, HD])
        qp, kp, mp = (sb(n, [P, HEADS, SLOTS, HD], BF16) for n in ("qp", "kp", "mp"))
        mx = sb("mx", [P, HEADS])
        mleft = sb("mleft", [P, 2, HEADS])
        V = sb("V", [P, R, HEADS, 32])
        kT = sb("kT", [P, R, G, P], BF16)
        qT = sb("qT", [P, 2, G, P], BF16)
        q2 = sb("q2", [P, 2, G, P], BF16)
        pb = sb("pb", [P, 2, 4 * P])
        osb, rec, on = (sb(n, [P, 4 * P]) for n in ("osb", "rec", "on"))
        bf16_bank = lambda b: bank[b][:].bitcast(BF16)

        lw, s_bi, s_z, s_sc = sem("w"), sem("bias"), sem("zero"), sem("spread")
        s_xs, s_qkv, s_raw, s_rot, s_sp, s_kt, s_kev, s_qt, s_qev = (
            sem(n) for n in ("xs", "qkv", "raw", "rot", "split", "kt", "kev", "qt", "qev"))
        s_s, s_mx, s_mp, s_mt, s_q2, s_t, s_ex, s_pv = (
            sem(n) for n in ("s", "mx", "mp", "mt", "q2", "t", "ex", "pv"))
        s_osb, s_rep, s_rec, s_on, s_pr, s_x = (sem(n) for n in ("osb", "rep", "rec", "on", "proj", "x"))
        loads = []
        if windowed:
            loads += [(wqkv[:], t[name + "_wqkv"]), (cs[:], t["rotary"].rearrange("(t p) a d -> p t a d", p=P))]
        else:
            row = lambda n: t[f"{name}_{n}"].rearrange("(o d) -> o d", o=1)
            for a, n in enumerate("qkv"):
                loads += [(wqkv[:, a * P:(a + 1) * P], t[f"{name}_w{n}"]), (bqkv[:, a * P:(a + 1) * P], row(f"b{n}"))]
        late = [(wo[32 * u:32 * u + HD], t[name + "_wo"].rearrange("(g u d) o -> u d g o", u=4, d=HD)[u])
                for u in range(4)]
        if not windowed:
            late.append((wo[HD:HD + 1, 0], row("bo")))

        L0 = k.L
        with nc.Block() as block:
            @block.sync
            def _(sp):
                for dst, src in loads:
                    sp.dma_start(dst, src).then_inc(lw, 16)
                sp.wait_ge(s_z, 1)
                for dst, src in late:
                    sp.dma_start(dst, src).then_inc(lw, 16)
                sp.wait_ge(lw, 16 * len(loads + late))

            @block.gpsimd
            def _(pool):
                n = 0

                def step(ins):
                    nonlocal n
                    n += 1
                    ins.then_inc(s_bi, 1)
                    pool.wait_ge(s_bi, n)

                nc.gpsimd.memset(wo[:], 0.0).then_inc(s_z, 1)
                for c in range(C):
                    k.norm_pool(L0 + c)
                flat = biasf[:].rearrange("p a b c -> p (a b c)")
                for dst, base, chan, pat in ((q_bias, P, 1, [[0, 2], [-P, 2], [-1, P]]),
                                             (k_bias, P, -1, [[0, 2], [-P, 2], [1, P]])):
                    neg = [[-a, b] for a, b in pat]
                    if windowed:
                        step(nc.gpsimd.memset(biasf[:], 0.0))
                    else:
                        step(nc.gpsimd.iota(biasf[:], pattern=neg, base=-base, channel_multiplier=-chan,
                                            allow_small_or_imprecise_dtypes=True))
                    step(nc.gpsimd.affine_select(out=biasf[:], in_=biasf[:], compare_op=ALU.is_ge, fill=MASKED,
                                                 base=base, pattern=pat, channel_multiplier=chan))
                    if windowed:
                        step(nc.gpsimd.affine_select(out=biasf[:], in_=biasf[:], compare_op=ALU.is_ge, fill=MASKED,
                                                     base=WINDOW - base, pattern=neg, channel_multiplier=-chan))
                    step(nc.gpsimd.tensor_copy(dst[:], flat))
                before = kT[:, R - 1]
                step(nc.gpsimd.memset(before, 0.0))
                for u in range(2):
                    step(nc.gpsimd.affine_select(out=before, in_=before, compare_op=ALU.not_equal, fill=MASKED,
                                                 base=-(64 * u + MAXROW + 3), pattern=[[0, G], [0, P]],
                                                 channel_multiplier=1))
                step(nc.gpsimd.memset(spread[:], 0.0))
                step(nc.gpsimd.affine_select(out=spread[:].rearrange("p (u m) -> p u m", u=4),
                                             in_=spread[:].rearrange("p (u m) -> p u m", u=4),
                                             compare_op=ALU.not_equal, fill=1.0, base=-HD,
                                             pattern=[[-32, 4], [0, 32]], channel_multiplier=1))

            @block.vector
            def _(dve):
                v = nc.vector
                for a in (qp, mp, V):
                    v.memset(a[:], 0.0)
                v.memset(kp[:], 0.0).then_inc(s_sc, 1)
                for c in range(C):
                    k.norm_vector(L0 + c, c)
                dve.wait_ge(s_sc, 1)
                v.memset(V[:, :, :, HD], 1.0)
                v.memset(kp[:, :, 6, 0:3], 1.0)
                v.memset(qp[:, :, 6, 3], 1.0)

            @block.tensor
            def _(pe):
                for c in range(C):
                    k.norm_tensor(L0 + c)

            @block.scalar
            def _(act):
                for c in range(C):
                    k.norm_scalar(L0 + c, k.xnT[:, c * CW:(c + 1) * CW])
        k.L += C

        IN_LOOP = (T - 4) // R
        last_steps = range(IN_LOOP * R + 1, T)

        def steps(engine, step):
            step(0, 0)
            with engine.Fori(0, IN_LOOP) as c:
                for i in range(R):
                    step(c * R + (i + 1), (i + 1) % R)
            for s in last_steps:
                step(s, s % R)

        to_come = lambda t, ahead: not isinstance(t, int) or t + ahead < T

        def wait(engine, sem, count):
            if not isinstance(count, int) or count > 0:
                engine.wait_ge(sem, count)

        with nc.Block() as block:
            def qkv(pe, y):
                pe.wait_ge(s_xs, y + 1)
                wait(pe, s_qev, y)
                dst = bank[6][:, 0:3 * P]
                last = nc.tensor.matmul(dst, xs[:], wqkv[:], start=True, stop=windowed)
                if not windowed:
                    last = nc.tensor.matmul(dst, k.ones[0:1, :], bqkv[:], start=False, stop=True)
                last.then_inc(s_qkv, 1)

            def turn(pe, y):
                pe.wait_ge(s_sp, 5 * y + 5)
                wait(pe, s_q2, y - 1)
                for b, src, done in ((5, kp, s_kt), (6, qp, s_qt)):
                    for g in range(G):
                        last = nc.tensor.transpose(bf16_bank(b)[:, g * P:(g + 1) * P],
                                                   src[:, 2 * g:2 * g + 2].rearrange("p h s d -> p (h s d)"), k.identb[:])
                    last.then_inc(done, 1)

            def first_pass(pe, y, slot, w):
                if w == 0:
                    pe.wait_ge(s_qev, y + 1)
                wait(pe, s_mx, y * NW + (w - 1))
                out = bank[w % 2]
                nc.tensor.matmul(out[:], k.identb[:], q_bias[:], start=True, stop=False, skip_group_check=True)
                for j, h in enumerate(heads(w)):
                    rows = slice(64 * (h % 2), 64 * (h % 2) + ROWS)
                    for s in range(2):
                        last = nc.tensor.matmul(out[:, (2 * j + s) * P:(2 * j + s + 1) * P],
                                                qT[rows, slot % 2, h // 2, :], kT[rows, (slot - 1 + s) % R, h // 2, :],
                                                start=False, stop=(j == 1 and s == 1), skip_group_check=True)
                last.then_inc(s_s, 1)

            def turn_maxima(pe, y):
                pe.wait_ge(s_mp, 5 * y + 5)
                pe.wait_ge(s_kev, y + 2 if to_come(y, 1) else T)
                for g in range(G):
                    last = nc.tensor.transpose(bf16_bank(5)[:, g * P:(g + 1) * P],
                                               mp[:, 2 * g:2 * g + 2].rearrange("p h s d -> p (h s d)"), k.identb[:])
                last.then_inc(s_mt, 1)

            def second_pass(pe, y, slot, w):
                if w == 0:
                    pe.wait_ge(s_q2, y + 1)
                wait(pe, s_ex, y * NW + (w - 1))
                out = bank[2 + w % 2]
                nc.tensor.matmul(out[:], k.identb[:], k_bias[:], start=True, stop=False, skip_group_check=True)
                for j, h in enumerate(heads(w)):
                    rows = slice(64 * (h % 2), 64 * (h % 2) + ROWS)
                    for s in range(2):
                        last = nc.tensor.matmul(out[:, (2 * j + s) * P:(2 * j + s + 1) * P],
                                                kT[rows, (slot - 1 + s) % R, h // 2, :], q2[rows, slot % 2, h // 2, :],
                                                start=False, stop=(j == 1 and s == 1), skip_group_check=True)
                last.then_inc(s_t, 1)

            def values(pe, y, slot, w):
                if w == 0:
                    wait(pe, s_osb, y)
                pe.wait_ge(s_ex, y * NW + (w + 1))
                for j, h in enumerate(heads(w)):
                    u, g = h % 4, h // 4
                    for s in range(2):
                        last = nc.tensor.matmul(bank[4][32 * u:32 * u + 32, g * P:(g + 1) * P],
                                                V[:, (slot - 1 + s) % R, h, :],
                                                pb[:, w % 2, (2 * j + s) * P:(2 * j + s + 1) * P],
                                                start=(s == 0), stop=(s == 1), skip_group_check=True)
                last.then_inc(s_pv, 1)

            def spread_sums(pe, y):
                pe.wait_ge(s_osb, y + 1)
                nc.tensor.matmul(bank[7][:], spread[:], osb[:], start=True, stop=True).then_inc(s_rep, 1)

            def project(pe, y):
                pe.wait_ge(s_on, y + 1)
                for g in range(4):
                    last = nc.tensor.matmul(bank[7][:, 0:P], on[:, g * P:(g + 1) * P], wo[:, g, :],
                                            start=(g == 0), stop=(g == 3))
                last.then_inc(s_pr, 1)

            def tensor_step(pe, y, slot):
                for w in range(NW):
                    if w == 1 and to_come(y, 2):
                        qkv(pe, y + 2)
                    if w < 4 and to_come(y, 1):
                        first_pass(pe, y + 1, slot + 1, 2 * w)
                        first_pass(pe, y + 1, slot + 1, 2 * w + 1)
                    if not isinstance(y, int) or y > 0:
                        if w == 1:
                            spread_sums(pe, y - 1)
                        if w == 3:
                            project(pe, y - 1)
                    if w == 5 and to_come(y, 2):
                        turn(pe, y + 2)
                    if w == 6 and to_come(y, 1):
                        turn_maxima(pe, y + 1)
                    second_pass(pe, y, slot, w)
                    if w:
                        values(pe, y, slot, w - 1)
                values(pe, y, slot, NW - 1)

            @block.tensor
            def _(pe):
                qkv(pe, 0)
                turn(pe, 0)
                qkv(pe, 1)
                for w in range(NW):
                    first_pass(pe, 0, 0, w)
                turn(pe, 1)
                turn_maxima(pe, 0)
                steps(pe, lambda y, slot: tensor_step(pe, y, slot))
                spread_sums(pe, T - 1)
                project(pe, T - 1)

            def stage(act, y):
                if isinstance(y, int):
                    wait(act, s_qkv, y)
                else:
                    k.wait_alone(act, s_qkv, y)
                tile = k.xnT[:].rearrange("p (t q) -> p t q", q=P)[:, bass.ds(y, 1), :]
                nc.scalar.activation(xs[:].rearrange("p (o q) -> p o q", o=1), tile, ACT.Copy).then_inc(s_xs, 1)

            def take_qkv(act, y, slot):
                act.wait_ge(s_qkv, y + 1)
                part = lambda a: bank[6][:, a * P:(a + 1) * P]
                dst = (raw[:].rearrange("p a h d e -> p a (h d e)") if windowed
                       else qk[:].rearrange("p a h d -> p a (h d)"))
                nc.scalar.activation(dst[:, 0], part(0), ACT.Copy, scale=SCALE)
                nc.scalar.activation(dst[:, 1], part(1), ACT.Copy)
                nc.scalar.activation(V[:, slot % R, :, 0:HD], part(2).rearrange("p (h d) -> p h d", d=HD), ACT.Copy)\
                    .then_inc(s_raw, 1)

            def take_turned(act, y, slot):
                act.wait_ge(s_kt, y + 1)
                nc.scalar.activation(kT[:, slot % R].rearrange("p g q -> p (g q)"), bf16_bank(5), ACT.Copy)\
                    .then_inc(s_kev, 1)
                act.wait_ge(s_qt, y + 1)
                nc.scalar.activation(qT[:, slot % 2].rearrange("p g q -> p (g q)"), bf16_bank(6), ACT.Copy)\
                    .then_inc(s_qev, 1)

            def scalar_step(act, y, slot):
                if to_come(y, 2):
                    stage(act, y + 2)
                for w in range(NW):
                    wait(act, s_pv, y * NW + (w - 1))
                    act.wait_ge(s_t, y * NW + (w + 1))
                    nc.scalar.activation(pb[:, w % 2, :], bank[2 + w % 2][:], ACT.Exp).then_inc(s_ex, 1)
                    if w == 1 and to_come(y, 2):
                        take_qkv(act, y + 2, slot + 2)
                    if w == 4 and to_come(y, 2):
                        take_turned(act, y + 2, slot + 2)

            @block.scalar
            def _(act):
                for y in range(2):
                    stage(act, y)
                    take_qkv(act, y, y)
                    take_turned(act, y, y)
                steps(act, lambda y, slot: scalar_step(act, y, slot))

            def maximum(dve, y, w):
                h = heads(w)[0]
                dve.wait_ge(s_s, y * NW + (w + 1))
                nc.vector.tensor_reduce(mx[:, h:h + 3:2], bank[w % 2][:].rearrange("p (j q) -> p j q", j=2),
                                        AX.X, ALU.max, negate=True).then_inc(s_mx, 1)

            def split_maxima(dve, y):
                dve.wait_ge(s_mx, y * NW + NW)
                at = lambda n: mp[:, :, 6, n]
                v = nc.vector
                v.tensor_copy(at(0), mx[:]).then_inc(s_mp, 1)
                dve.wait_ge(s_mp, 5 * y + 1)
                v.tensor_tensor(mleft[:, 0], mx[:], at(0), ALU.subtract).then_inc(s_mp, 1)
                dve.wait_ge(s_mp, 5 * y + 2)
                v.tensor_copy(at(1), mleft[:, 0]).then_inc(s_mp, 1)
                dve.wait_ge(s_mp, 5 * y + 3)
                v.tensor_tensor(mleft[:, 1], mleft[:, 0], at(1), ALU.subtract).then_inc(s_mp, 1)
                dve.wait_ge(s_mp, 5 * y + 4)
                v.tensor_copy(at(2), mleft[:, 1]).then_inc(s_mp, 1)

            def maxima_onto_q(dve, y, slot):
                dve.wait_ge(s_mt, y + 1)
                flat = lambda a: a[:, slot % 2].rearrange("p g q -> p (g q)")
                nc.vector.tensor_tensor(flat(q2), flat(qT), bf16_bank(5), ALU.add).then_inc(s_q2, 1)

            def take_values(dve, y):
                dve.wait_ge(s_pv, y * NW + NW)
                nc.vector.tensor_copy(osb[:], bank[4][:]).then_inc(s_osb, 1)

            def invert(dve, y):
                dve.wait_ge(s_rep, y + 1)
                nc.vector.reciprocal(rec[:], bank[7][:]).then_inc(s_rec, 1)

            def normalise(dve, y):
                dve.wait_ge(s_rec, y + 1)
                nc.vector.tensor_tensor(on[:], osb[:], rec[:], ALU.mult).then_inc(s_on, 1)

            def add(dve, y):
                dve.wait_ge(s_pr, y + 1)
                xt = k.X[:, bass.ds(y, 1), :]
                nc.vector.tensor_tensor(xt, bank[7][:, 0:P].rearrange("p (o q) -> p o q", o=1), xt, ALU.add)\
                    .then_inc(s_x, 1)

            def vector_step(dve, y, slot):
                before = not isinstance(y, int) or y > 0
                if before:
                    take_values(dve, y - 1)
                for w in range(NW):
                    if to_come(y, 1):
                        maximum(dve, y + 1, w)
                    if before and w == 1:
                        invert(dve, y - 1)
                    if before and w == 2:
                        normalise(dve, y - 1)
                    if before and w == 6:
                        add(dve, y - 1)
                if to_come(y, 1):
                    split_maxima(dve, y + 1)
                    maxima_onto_q(dve, y + 1, slot + 1)

            @block.vector
            def _(dve):
                for w in range(NW):
                    maximum(dve, 0, w)
                split_maxima(dve, 0)
                maxima_onto_q(dve, 0, 0)
                steps(dve, lambda y, slot: vector_step(dve, y, slot))
                take_values(dve, T - 1)
                invert(dve, T - 1)
                normalise(dve, T - 1)
                add(dve, T - 1)

            def rotate(pool, tile):
                even, odd = (raw[:, :, :, :, a].rearrange("p a h d -> p (a h) d") for a in range(2))
                for n, (x, a) in enumerate(((even, 0), (odd, 1), (odd, 0), (even, 1))):
                    f = cs[:, bass.ds(tile, 1), a, :].to_broadcast([P, 2 * HEADS, HD // 2])
                    last = nc.gpsimd.tensor_tensor(rot[:, n], x, f, ALU.mult)
                last.then_inc(s_rot, 1)
                k.wait_alone(pool, s_rot, tile * 2 + 1)
                to = qk[:].rearrange("p a h (d two) -> p two (a h) d", two=2)
                nc.gpsimd.tensor_tensor(to[:, 0], rot[:, 0], rot[:, 1], ALU.subtract)
                nc.gpsimd.tensor_tensor(to[:, 1], rot[:, 2], rot[:, 3], ALU.add).then_inc(s_rot, 1)
                k.wait_alone(pool, s_rot, tile * 2 + 2)

            @block.gpsimd
            def _(pool):
                with pool.Fori(0, T) as y:
                    k.wait_alone(pool, s_raw, y + 1)
                    if windowed:
                        rotate(pool, y)
                    wide = lambda a, n: a[:, :, None, :].to_broadcast([P, HEADS, n, HD])
                    copy, g = nc.gpsimd.tensor_copy, nc.gpsimd
                    src = qk
                    for n, (qs, ks) in enumerate((((0, 3), ((0, 4, 3), (5, 6, 1))), ((3, 5), ((1, 5, 3),)),
                                                  ((5, 6), ((2, 3, 1),)))):
                        copy(qp[:, :, qs[0]:qs[1], :], wide(src[:, 0], qs[1] - qs[0]))
                        for a, b, stride in ks:
                            last = copy(kp[:, :, a:b:stride, :], wide(src[:, 1], len(range(a, b, stride))))
                        last.then_inc(s_sp, 1)
                        if n == 2:
                            break
                        k.wait_alone(pool, s_sp, 5 * y + 2 * n + 1)
                        rest = left[:, n]
                        g.tensor_tensor(rest[:, 0], src[:, 0], qp[:, :, qs[0], :], ALU.subtract)
                        g.tensor_tensor(rest[:, 1], src[:, 1], kp[:, :, n, :], ALU.subtract).then_inc(s_sp, 1)
                        k.wait_alone(pool, s_sp, 5 * y + 2 * n + 2)
                        src = rest


def ffn3(k):
    nc, t, C = k.nc, k.t, k.C
    L0, bank = k.L, k.bank
    F = t["f3_w1"].shape[1]
    FB = F // P
    tmp = ExitStack()
    sb = lambda n, shape, dt=F32: k.sb("f3_" + n, shape, dt, tmp)
    sem = lambda n: k.sem("f3_" + n)
    with tmp:
        w1, w2 = sb("w1", [P, F]), sb("w2", [P, F])
        hw = [sb("h1w", [P, FB, F]), sb("h2w", [P, FB, F])]
        w3 = sb("w3", [P, FB, P])
        sc1, sc2, sch1, sch2 = (sb(n, [P, FB]) for n in ("sc1", "sc2", "sch1", "sch2"))
        s3 = sb("s3", [P, P])
        sg = sb("sg", [P, 2, CW])
        hA = [sb(f"hA{b}", [P, FB, CW]) for b in range(2)]
        hB = [sb(f"hB{b}", [P, FB, CW]) for b in range(2)]
        ys = sb("ys", [P, CT, P])
        lw, s_ab, s_sg, s_a, s_m, s_g, s_y, s_ys, s_x = (
            sem(n) for n in ("w", "ab", "sg", "a", "m", "g", "y", "ys", "x"))
        col = lambda n: t[n].rearrange("(f p) -> p f", p=P)
        mat = lambda n: t[n].rearrange("(f p) o -> p f o", p=P)
        loads = [(w1[:], t["f3_w1"]), (w2[:], t["f3_w2"]), (hw[0][:], mat("f3_h1")), (hw[1][:], mat("f3_h2")),
                 (w3[:], mat("f3_w3")), (sc1[:], col("f3_s1")), (sc2[:], col("f3_s2")), (sch1[:], col("f3_sh1")),
                 (sch2[:], col("f3_sh2")), (s3[:], t["f3_s3"].partition_broadcast(P))]
        with nc.Block() as block:
            @block.sync
            def _(sp):
                with nc.allow_non_contiguous_dma(reason="scale columns"):
                    for dst, src in loads:
                        sp.dma_start(dst, src).then_inc(lw, 16)

            @block.gpsimd
            def _(pool):
                for c in range(C):
                    k.norm_pool(L0 + c)

            @block.scalar
            def _(act):
                for c in range(C):
                    k.norm_scalar(L0 + c, k.xnT[:, c * CW:(c + 1) * CW])

            @block.tensor
            def _(pe):
                for c in range(C):
                    k.norm_tensor(L0 + c)
                pe.wait_ge(lw, 16 * len(loads))

            @block.vector
            def _(dve):
                for c in range(C):
                    k.norm_vector(L0 + c, c)
        k.L += C

        with nc.Block() as block:
            @block.tensor
            def _(pe):
                with pe.Fori(0, C // 2) as it:
                    for b in range(2):
                        if b == 0:
                            pe.wait_ge(s_ys, it * 2 + 2)
                        for f in range(FB):
                            pe.wait_ge(s_a, it * (2 * FB) + (b * FB + f) + 1)
                            for j, w in enumerate((w1, w2)):
                                nc.tensor.matmul(bank[2 * (f % 2) + j][:], w[:, f * P:(f + 1) * P],
                                                 k.xnT[:, bass.ds(it * (2 * CW) + b * CW, CW)], start=True, stop=True)\
                                    .then_inc(s_ab, 1)
                    for layer in range(2):
                        for b in range(2):
                            src = hA[b] if layer == 0 else hB[b]
                            if layer == 0:
                                pe.wait_ge(s_a, it * (2 * FB) + (b + 1) * FB + 2)
                            else:
                                pe.wait_ge(s_g, it * (4 * FB) + (b + 1) * FB + 4)
                            for f in range(FB):
                                m = (layer * 2 + b) * FB + f
                                pe.wait_ge(s_g, it * (4 * FB) + m + 1)
                                for i in range(FB):
                                    last = nc.tensor.matmul(bank[4 + m % 4][:], hw[layer][:, i, f * P:(f + 1) * P],
                                                            src[:, i, :], start=(i == 0), stop=(i == FB - 1))
                                last.then_inc(s_m, 1)
                    for b in range(2):
                        pe.wait_ge(s_g, it * (4 * FB) + (2 + b + 1) * FB + 4)
                        for i in range(CT):
                            for f in range(FB):
                                last = nc.tensor.matmul(bank[b][:, i * P:(i + 1) * P],
                                                        hA[b][:, f, i * P:(i + 1) * P], w3[:, f, :],
                                                        start=(f == 0), stop=(f == FB - 1))
                        last.then_inc(s_y, 1)

            @block.scalar
            def _(act):
                nc.scalar.sem_inc(s_g, 4)
                with act.Fori(0, C // 2) as it:
                    for b in range(2):
                        for f in range(FB):
                            n = it * (2 * FB) + (b * FB + f)
                            act.wait_ge(s_ab, n * 2 + 1)
                            act.wait_ge(s_a, n + 1)
                            nc.scalar.activation(sg[:, f % 2, :], bank[2 * (f % 2)][:], ACT.Silu, scale=sc1[:, f:f + 1])\
                                .then_inc(s_sg, 1)
                    for layer, (dst, sc) in enumerate(((hB, sch1), (hA, sch2))):
                        for b in range(2):
                            for f in range(FB):
                                m = (layer * 2 + b) * FB + f
                                act.wait_ge(s_m, it * (4 * FB) + m + 1)
                                nc.scalar.activation(dst[b][:, f, :], bank[4 + m % 4][:], ACT.Gelu, scale=sc[:, f:f + 1])\
                                    .then_inc(s_g, 1)

            @block.vector
            def _(dve):
                v = nc.vector
                v.sem_inc(s_a, 2)
                v.sem_inc(s_ys, 2)
                with dve.Fori(0, C // 2) as it:
                    for b in range(2):
                        for f in range(FB):
                            n = it * (2 * FB) + (b * FB + f)
                            dve.wait_ge(s_ab, n * 2 + 2)
                            dve.wait_ge(s_sg, n + 1)
                            v.scalar_tensor_tensor(out=hA[b][:, f, :], in0=bank[2 * (f % 2) + 1][:],
                                                   scalar=sc2[:, f:f + 1], in1=sg[:, f % 2, :], op0=ALU.mult,
                                                   op1=ALU.mult).then_inc(s_a, 1)
                    for b in range(2):
                        q = it * 2 + b
                        dve.wait_ge(s_y, q + 1)
                        v.tensor_tensor(ys[:], bank[b][:].rearrange("p (i d) -> p i d", i=CT),
                                        s3[:, None, :].to_broadcast([P, CT, P]), ALU.mult).then_inc(s_ys, 1)
                        dve.wait_ge(s_ys, q + 3)
                        xt = k.X[:, bass.ds(q * CT, CT), :]
                        v.tensor_tensor(xt, xt, ys[:], ALU.add).then_inc(s_x, 1)
                        dve.wait_ge(s_x, q + 1)


def store(k, out):
    stored = k.sem("stored")
    with k.nc.Block() as block:
        @block.sync
        def _(sp):
            sp.dma_start(out.rearrange("(t p) d -> p t d", p=P), k.X[:]).then_inc(stored, 16)
            sp.wait_ge(stored, 16)


def program(nc, t, out, parts=PARTS):
    with ExitStack() as ctx:
        k = Core(nc, ctx, t)
        constants(k)
        for part in parts:
            if part == "mamba":
                mamba(k)
            elif part in ("moe0", "moe1"):
                experts(k, part, gated=(part == "moe1"))
            elif part == "linear":
                linear(k)
            elif part in ("decay", "window"):
                softmax_mixer(k, part, windowed=(part == "window"))
            elif part == "deep":
                deep(k)
            elif part == "ffn3":
                ffn3(k)
            k.end_part()
        store(k, out)


NAMES = {
    "x": ("L0_attn_x", lambda a: a.reshape(a.shape[1:])),
    "ln1_g": ("L0_attn_ln1_g", None), "ln1_b": ("L0_attn_ln1_b", None),
    "in_proj_w": ("L0_attn_in_proj_w", None),
    "conv_w": ("L0_attn_conv_w", lambda a: a.reshape(a.shape[0], a.shape[2])),
    "conv_b": ("L0_attn_conv_b", None), "x_proj_w": ("L0_attn_x_proj_w", None),
    "dt_proj_w": ("L0_attn_dt_proj_w", None), "dt_proj_b": ("L0_attn_dt_proj_b", None),
    "A_log": ("L0_attn_A_log", None), "D": ("L0_attn_D", None), "out_proj_w": ("L0_attn_out_proj_w", None),
    "ln2_g": ("L0_attn_ln2_g", None), "ln2_b": ("L0_attn_ln2_b", None),
    "ffn_w1": ("L0_attn_ffn_w1", None), "ffn_b1": ("L0_attn_ffn_b1", None),
    "ffn_w2": ("L0_attn_ffn_w2", None), "ffn_b2": ("L0_attn_ffn_b2", None),
    "moe0_gate_w": ("L0_ffn_gate_w", None), "moe0_gate_b": ("L0_ffn_gate_b", None),
    "moe0_w1": ("L0_ffn_w1", None), "moe0_b1": ("L0_ffn_b1", None),
    "moe0_w2": ("L0_ffn_w2", None), "moe0_b2": ("L0_ffn_b2", None),
    "lin_wqT": ("L1_attn_Wq", lambda a: a.T), "lin_wkT": ("L1_attn_Wk", lambda a: a.T), "lin_wv": ("L1_attn_Wv", None),
    "lin_bq": ("L1_attn_bq", None), "lin_bk": ("L1_attn_bk", None), "lin_bv": ("L1_attn_bv", None),
    "lin_gamma": ("L1_attn_gamma", None),
    "moe1_gate_w": ("L1_ffn_router_w", lambda a: a.T), "moe1_w1": ("L1_ffn_w_gate", None),
    "moe1_wu": ("L1_ffn_w_up", None), "moe1_w2": ("L1_ffn_w_down", None),
    "decay_wq": ("L2_attn_Wq", lambda a: a.T), "decay_wk": ("L2_attn_Wk", lambda a: a.T),
    "decay_wv": ("L2_attn_Wv", lambda a: a.T), "decay_wo": ("L2_attn_Wo", lambda a: a.T),
    "decay_bq": ("L2_attn_bq", None), "decay_bk": ("L2_attn_bk", None), "decay_bv": ("L2_attn_bv", None),
    "decay_bo": ("L2_attn_bo", None),
    "deep_gate_w": ("L2_ffn_gate_w", None), "deep_gate_b": ("L2_ffn_gate_b", None),
    "deep_w1": ("L2_ffn_w1", None), "deep_b1": ("L2_ffn_b1", None), "deep_w2": ("L2_ffn_w2", None),
    "deep_b2": ("L2_ffn_b2", None), "deep_w3": ("L2_ffn_w3", None), "deep_b3": ("L2_ffn_b3", None),
    "window_wqkv": ("L3_attn_w_qkv", None), "window_wo": ("L3_attn_w_o", None),
    "f3_w1": ("L3_ffn_w1_w", lambda a: a.T), "f3_s1": ("L3_ffn_w1_s", None),
    "f3_w2": ("L3_ffn_w2_w", lambda a: a.T), "f3_s2": ("L3_ffn_w2_s", None),
    "f3_h1": ("L3_ffn_h1_w", lambda a: a.T), "f3_sh1": ("L3_ffn_h1_s", None),
    "f3_h2": ("L3_ffn_h2_w", lambda a: a.T), "f3_sh2": ("L3_ffn_h2_s", None),
    "f3_w3": ("L3_ffn_w3_w", lambda a: a.T), "f3_s3": ("L3_ffn_w3_s", None),
}


def rotary_table(np, n, half, base=10000.0):
    inv = (np.float32(1.0) / np.float32(base) ** (np.arange(half, dtype=np.float32) / np.float32(half)))
    angle = np.arange(n, dtype=np.float32)[:, None] * inv.astype(np.float32)[None, :]
    return np.ascontiguousarray(np.stack([np.cos(angle), np.sin(angle)], axis=1).astype(np.float32))


def kernel(**inputs):
    import numpy as np
    import concourse.bacc as bacc
    from concourse.bass_utils import run_bass_kernel_spmd as run

    nc = bacc.Bacc("TRN2", target_bir_lowering=False, num_devices=1)
    arrays, t = {}, {}
    for name, (source, lay) in NAMES.items():
        a = np.asarray(inputs[source])
        a = np.ascontiguousarray(lay(a) if lay else a)
        arrays["in_" + name] = a
        t[name] = nc.dram_tensor("in_" + name, a.shape, mybir.dt.from_np(a.dtype), kind="ExternalInput").ap()
    shape = inputs["L0_attn_x"].shape
    arrays["in_rotary"] = rotary_table(np, shape[1], 4)
    t["rotary"] = nc.dram_tensor("in_rotary", arrays["in_rotary"].shape, F32, kind="ExternalInput").ap()
    out = nc.dram_tensor("out", shape[1:], F32, kind="ExternalOutput").ap()
    program(nc, t, out)
    r = run(nc, [arrays], core_ids=[0])
    return r.results[0]["out"].reshape(shape)
```

```python
from contextlib import ExitStack

import concourse.bass as bass
from concourse import mybir

F32 = mybir.dt.float32
BF16 = mybir.dt.bfloat16
U32 = mybir.dt.uint32
ALU = mybir.AluOpType
ACT = mybir.ActivationFunctionType
AX = mybir.AxisListType

ENGINE = mybir.EngineType
EVERY_ENGINE = [ENGINE.PE, ENGINE.Activation, ENGINE.Pool, ENGINE.DVE, ENGINE.SP]

P = 128
CT = 4
CW = CT * P
EPS = 1e-5
MASKED = -1.0e30
EXP_IS_ZERO = 104.0
PARTS = ("mamba", "moe0", "linear", "moe1", "decay", "deep", "window", "ffn3")


class Core:

    def __init__(self, nc, ctx, t):
        self.nc, self.ctx, self.t = nc, ctx, t
        self.N = t["x"].shape[0]
        self.T = self.N // P
        self.C = self.T // CT
        self.E = t["moe0_gate_w"].shape[1]
        self.L = 0
        self.bank = [ctx.enter_context(nc.psum_tensor(f"bank{i}", [P, 512], F32)) for i in range(8)]
        self.X = self.sb("X", [P, self.T, P])
        self.xnT = self.sb("xnT", [P, self.N])
        self.stats = self.sb("stats", [P, CT, 6])
        self.meanvar = self.sb("meanvar", [P, CT, 2])
        self.veps = self.sb("veps", [P, CT])
        self.rstd = self.sb("rstd", [P, CT])
        self.xn = self.sb("xn", [P, CT, P])
        self.ident = self.sb("ident", [P, P])
        self.identb = self.sb("identb", [P, P], BF16)
        self.ones = self.sb("ones", [P, P])
        self.mhalf = self.sb("mhalf", [P, 32])
        self.part_sems = []
        self.passed = self.sem("passed")
        self.stored = self.sem("stored")
        self.ln_st = self.sem("ln_st")
        self.ln_mv = self.sem("ln_mv")
        self.ln_ve = self.sem("ln_ve")
        self.ln_rs = self.sem("ln_rs")
        self.ln_xn = self.sem("ln_xn")
        self.ln_tr = self.sem("ln_tr")
        self.ln_ev = self.sem("ln_ev")
        self.part_sems = []

    def sb(self, name, shape, dt=F32, ctx=None):
        return (ctx or self.ctx).enter_context(self.nc.sbuf_tensor(name, shape, dt))

    def sem(self, name):
        handle = self.nc.alloc_semaphore(name=name)
        self.part_sems.append(handle)
        return handle

    def end_part(self):
        self.nc.clear_and_free_semaphores(self.part_sems)
        self.nc.all_engine_barrier()
        self.part_sems = []

    def wait_alone(self, engine, sem, value):
        engine.wait_ge(sem, value)
        engine.sem_inc(self.passed, 1)

    def norm_vector(self, L, c):
        nc, v = self.nc, self.nc.vector
        tile = lambda i: self.X[:, bass.ds(c * CT + i, 1), :]
        for i in range(CT):
            last = v.bn_stats(self.stats[:, i, :], tile(i))
        last.then_inc(self.ln_st, 1)
        self.wait_alone(v, self.ln_st, L + 1)
        for i in range(CT):
            last = v.bn_aggr(self.meanvar[:, i, :], self.stats[:, i, :])
        last.then_inc(self.ln_mv, 1)
        v.wait_ge(self.ln_mv, L + 1)
        v.tensor_scalar(self.veps[:], self.meanvar[:, :, 1], EPS, None, ALU.add).then_inc(self.ln_ve, 1)
        v.wait_ge(self.ln_rs, L + 1)
        if not isinstance(L, int) or L > 0:
            v.wait_ge(self.ln_tr, L)
        for i in range(CT):
            last = v.tensor_scalar(self.xn[:, i, :], tile(i), self.meanvar[:, i, 0:1], self.rstd[:, i:i + 1],
                                   ALU.subtract, ALU.mult)
        last.then_inc(self.ln_xn, 1)

    def norm_pool(self, L):
        self.nc.gpsimd.wait_ge(self.ln_ve, L + 1)
        self.nc.gpsimd.tensor_tensor(self.rstd[:], self.veps[:], self.mhalf[:, 0:CT], ALU.pow)\
            .then_inc(self.ln_rs, 1)

    def norm_tensor(self, L):
        pe = self.nc.tensor
        pe.wait_ge(self.ln_xn, L + 1)
        if not isinstance(L, int) or L > 0:
            pe.wait_ge(self.ln_ev, L)
        for i in range(CT):
            last = pe.transpose(self.bank[7][:, i * P:(i + 1) * P], self.xn[:, i, :], self.ident[:])
        last.then_inc(self.ln_tr, 1)

    def norm_scalar(self, L, dst):
        self.nc.scalar.wait_ge(self.ln_tr, L + 1)
        self.nc.scalar.activation(dst, self.bank[7][:], ACT.Copy).then_inc(self.ln_ev, 1)


def constants(k):
    nc = k.nc
    loaded, zeroed, made = k.sem("x_loaded"), k.sem("const_zeroed"), k.sem("const_made")
    with nc.Block() as block:
        @block.sync
        def _(sp):
            sp.dma_start(k.X[:], k.t["x"].rearrange("(t p) d -> p t d", p=P)).then_inc(loaded, 16)
            sp.wait_ge(loaded, 16)

        @block.gpsimd
        def _(pool):
            nc.gpsimd.memset(k.ident[:], 0.0)
            nc.gpsimd.memset(k.ones[:], 1.0)
            nc.gpsimd.memset(k.mhalf[:], -0.5).then_inc(zeroed, 1)
            pool.wait_ge(zeroed, 1)
            nc.gpsimd.affine_select(out=k.ident[:], in_=k.ident[:], compare_op=ALU.not_equal, fill=1.0, base=0,
                                    pattern=[[-1, P]], channel_multiplier=1).then_inc(made, 1)

        @block.vector
        def _(dve):
            dve.wait_ge(made, 1)
            nc.vector.tensor_copy(k.identb[:], k.ident[:])


def mamba(k):
    nc, t, N, C = k.nc, k.t, k.N, k.C
    DI = t["in_proj_w"].shape[1] // 2
    H = DI // P
    NS = t["A_log"].shape[1]
    R = t["dt_proj_w"].shape[0]
    FB = t["ffn_w1"].shape[1] // P
    KC = t["conv_w"].shape[1]
    PAD = KC - 1
    L0 = k.L
    bank = k.bank
    tmp = ExitStack()
    sb = lambda name, shape, dt=F32: k.sb(name, shape, dt, tmp)
    with tmp:
        inw = sb("inw", [P, 2 * DI])
        g1 = sb("g1", [P, 1])
        b1 = sb("b1", [P, 1])
        g2 = sb("g2", [P, 1])
        b2 = sb("b2", [P, 1])
        cw = sb("cw", [P, H, KC])
        cb = sb("cb", [P, H])
        xpw = sb("xpw", [P, H, R + 2 * NS])
        xpw3 = sb("xpw3", [P, H, 3, 2 * NS])
        dtw = sb("dtw", [R, DI])
        dtb = sb("dtb", [P, H])
        A = sb("A", [P, H, NS])
        Dp = sb("Dp", [P, H])
        outw = sb("outw", [P, H, P])
        w1 = sb("m_w1", [P, FB * P])
        w1b = sb("m_w1b", [P, FB])
        w2 = sb("m_w2", [P, FB, P])
        w2b = sb("m_w2b", [1, P])
        xo = sb("xo", [P, k.T, P])
        xi = sb("xi", [P, H, PAD + N])
        sz = sb("sz", [P, H, N])
        xc = sb("xc", [P, H, N])
        dt = sb("dt", [P, H, N])
        dtx = sb("dtx", [P, H, N])
        BC3 = sb("BC3", [96, N], BF16)
        sel = sb("sel", [96, 2 * NS, P], BF16)
        rt1 = sb("rt1", [96, CW])
        rt2 = sb("rt2", [96, CW])
        hib = sb("hib", [96, CW], BF16)
        midb = sb("midb", [96, CW], BF16)
        lr = sb("lr", [R, CW])
        dA = sb("dA", [P, 2, H, CW])
        dBx = sb("dBx", [P, 2, H, CW])
        h = sb("h", [P, 2, H, CW])
        hC = sb("hC", [P, 2, H, CW])
        Cs = sb("Cs", [P, 2, CW])
        state = sb("state", [P, NS, H])
        r2 = sb("r2", [P, CT])

        wl, sel0, selm = k.sem("m_weights"), k.sem("m_sel_zeroed"), k.sem("m_sel_made")
        s_r2 = k.sem("m_r2")
        s_ve2 = k.sem("m_ve2")
        s_xo = k.sem("m_xo")
        s_un = k.sem("m_un")
        s_in = k.sem("m_in")
        s_inev = k.sem("m_inev")
        s_cv = k.sem("m_conv")
        s_xc = k.sem("m_xc")
        s_xd = k.sem("m_xd")
        s_xde = k.sem("m_xde")
        s_bc = k.sem("m_bc")
        s_dtm = k.sem("m_dtm")
        s_dta = k.sem("m_dta")
        s_sp = k.sem("m_softplus")
        s_dt = k.sem("m_dt")
        s_dtx = k.sem("m_dtx")
        s_A = k.sem("m_A")

        wloads = [
            (inw[:], t["in_proj_w"]), (g1[:], t["ln1_g"].rearrange("(p o) -> p o", o=1)),
            (b1[:], t["ln1_b"].rearrange("(p o) -> p o", o=1)), (g2[:], t["ln2_g"].rearrange("(p o) -> p o", o=1)),
            (b2[:], t["ln2_b"].rearrange("(p o) -> p o", o=1)),
            (cw[:], t["conv_w"].rearrange("(h p) k -> p h k", p=P)),
            (cb[:], t["conv_b"].rearrange("(h p) -> p h", p=P)),
            (xpw[:], t["x_proj_w"].rearrange("(h p) k -> p h k", p=P)),
            (dtw[:], t["dt_proj_w"]), (dtb[:], t["dt_proj_b"].rearrange("(h p) -> p h", p=P)),
            (A[:], t["A_log"].rearrange("(h p) n -> p h n", p=P)), (Dp[:], t["D"].rearrange("(h p) -> p h", p=P)),
            (outw[:], t["out_proj_w"].rearrange("(h p) d -> p h d", p=P)),
            (w1[:], t["ffn_w1"]), (w1b[:], t["ffn_b1"].rearrange("(f p) -> p f", p=P)),
            (w2[:], t["ffn_w2"].rearrange("(f p) d -> p f d", p=P)),
            (w2b[:], t["ffn_b2"].rearrange("(o d) -> o d", o=1)),
        ]

        with nc.Block() as block:
            @block.sync
            def _(sp):
                with nc.allow_non_contiguous_dma(reason="small weights"):
                    for dst, src in wloads:
                        sp.dma_start(dst, src).then_inc(wl, 16)

            @block.gpsimd
            def _(pool):
                nc.gpsimd.memset(sel[:], 0.0)
                nc.gpsimd.memset(state[:], 0.0)
                nc.gpsimd.memset(xi[:, :, 0:PAD], 0.0).then_inc(sel0, 1)
                pool.wait_ge(sel0, 1)
                for part in range(3):
                    last = nc.gpsimd.affine_select(out=sel[:], in_=sel[:], compare_op=ALU.not_equal, fill=1.0,
                                                   base=-32 * part, pattern=[[-1, 2 * NS], [0, P]],
                                                   channel_multiplier=1)
                    last.then_inc(selm, 1)
                    pool.wait_ge(selm, part + 1)
                for c in range(C):
                    k.norm_pool(L0 + c)
                    pool.wait_ge(s_ve2, c + 1)
                    nc.gpsimd.tensor_tensor(r2[:], r2[:], k.mhalf[:, 0:CT], ALU.pow).then_inc(s_r2, 1)

            @block.vector
            def _(dve):
                dve.wait_ge(wl, 16 * len(wloads))
                for p in range(3):
                    last = nc.vector.tensor_copy(xpw3[:, :, p, :], xpw[:, :, R:R + 2 * NS])
                last.then_inc(s_A, 1)

                def norm(c):
                    L = L0 + c
                    v = nc.vector
                    tile = lambda i: k.X[:, c * CT + i, :]
                    for i in range(CT):
                        last = v.bn_stats(k.stats[:, i, :], tile(i))
                    last.then_inc(k.ln_st, 1)
                    v.wait_ge(k.ln_st, L + 1)
                    for i in range(CT):
                        last = v.bn_aggr(k.meanvar[:, i, :], k.stats[:, i, :])
                    last.then_inc(k.ln_mv, 1)
                    v.wait_ge(k.ln_mv, L + 1)
                    v.tensor_scalar(k.veps[:], k.meanvar[:, :, 1], EPS, None, ALU.add).then_inc(k.ln_ve, 1)
                    v.wait_ge(k.ln_rs, L + 1)
                    for i in range(CT):
                        last = v.tensor_scalar(xo[:, c * CT + i, :], tile(i), k.meanvar[:, i, 0:1],
                                               k.rstd[:, i:i + 1], ALU.subtract, ALU.mult)
                    last.then_inc(s_xo, 1)
                    v.tensor_tensor(r2[:], k.meanvar[:, :, 1], k.rstd[:], ALU.mult).then_inc(s_un, 1)
                    v.wait_ge(s_un, 3 * c + 1)
                    v.tensor_tensor(r2[:], r2[:], k.rstd[:], ALU.mult).then_inc(s_un, 1)
                    v.wait_ge(s_un, 3 * c + 2)
                    v.tensor_scalar(r2[:], r2[:], EPS, None, ALU.add).then_inc(s_ve2, 1)
                    v.wait_ge(s_r2, c + 1)
                    v.wait_ge(s_xo, c + 1)
                    if c:
                        v.wait_ge(k.ln_tr, L)
                    for i in range(CT):
                        last = v.tensor_scalar(k.xn[:, i, :], xo[:, c * CT + i, :], r2[:, i:i + 1], None, ALU.mult)
                    last.then_inc(k.ln_xn, 1)
                    v.nop().then_inc(s_un, 1)

                def conv(c):
                    a = PAD + c * CW
                    for hh in range(H):
                        acc = xc[:, hh, c * CW:(c + 1) * CW]
                        dve.wait_ge(s_inev, 2 * H * c + hh + 1)
                        n0 = KC * (c * H + hh)
                        nc.vector.tensor_scalar(acc, xi[:, hh, a - PAD:a - PAD + CW], cw[:, hh, 0:1],
                                                cb[:, hh:hh + 1], ALU.mult, ALU.add).then_inc(s_cv, 1)
                        for j in range(1, KC):
                            dve.wait_ge(s_cv, n0 + j)
                            nc.vector.scalar_tensor_tensor(
                                out=acc, in0=xi[:, hh, a - PAD + j:a - PAD + j + CW], scalar=cw[:, hh, j:j + 1],
                                in1=acc, op0=ALU.mult, op1=ALU.add).then_inc(s_cv, 1)

                def split(c):
                    cs = slice(c * CW, (c + 1) * CW)
                    v = nc.vector
                    dve.wait_ge(s_xd, 2 * c + 1)
                    n0 = 8 * c
                    v.tensor_copy(hib[:], bank[4][0:96, :]).then_inc(s_bc, 1)
                    dve.wait_ge(s_bc, n0 + 1)
                    v.tensor_tensor(rt1[:], bank[4][0:96, :], hib[:], ALU.subtract).then_inc(s_bc, 1)
                    v.tensor_copy(BC3[0:32, cs], hib[0:32, :]).then_inc(s_bc, 1)
                    dve.wait_ge(s_bc, n0 + 2)
                    v.tensor_copy(midb[:], rt1[:]).then_inc(s_bc, 1)
                    dve.wait_ge(s_bc, n0 + 4)
                    v.tensor_tensor(rt2[:], rt1[:], midb[:], ALU.subtract).then_inc(s_bc, 1)
                    v.tensor_copy(BC3[32:64, cs], midb[32:64, :]).then_inc(s_bc, 1)
                    dve.wait_ge(s_bc, n0 + 5)
                    v.tensor_copy(BC3[64:96, cs], rt2[64:96, :]).then_inc(s_bc, 1)
                    dve.wait_ge(s_xd, 2 * c + 2)
                    v.tensor_copy(lr[:], bank[5][0:R, :]).then_inc(s_bc, 1)

                norm(0)
                for c in range(C + 1):
                    if c + 1 < C:
                        norm(c + 1)
                    if c < C:
                        conv(c)
                    if c:
                        split(c - 1)
                for c in range(C):
                    cs = slice(c * CW, (c + 1) * CW)
                    dve.wait_ge(s_sp, 2)
                    nc.vector.tensor_tensor(dt[:, :, cs], dt[:, :, cs], dtx[:, :, cs], ALU.add).then_inc(s_dt, 1)
                    dve.wait_ge(s_dt, c + 1)
                    nc.vector.tensor_tensor(dtx[:, :, cs], dt[:, :, cs], xc[:, :, cs], ALU.mult)

            @block.tensor
            def _(pe):
                pe.wait_ge(wl, 16 * len(wloads))
                pe.wait_ge(s_A, 1)
                def branches(c):
                    k.norm_tensor(L0 + c)
                    pe.wait_ge(k.ln_ev, L0 + c + 1)
                    if c:
                        pe.wait_ge(s_inev, 2 * H * c)
                    for b in range(2 * H):
                        nc.tensor.matmul(bank[b][:], inw[:, b * P:(b + 1) * P], k.xnT[:, c * CW:(c + 1) * CW],
                                         start=True, stop=True).then_inc(s_in, 1)

                def b_c_rank(c):
                    cs = slice(c * CW, (c + 1) * CW)
                    pe.wait_ge(s_xc, c + 1)
                    if c:
                        pe.wait_ge(s_bc, 8 * c)
                    for hh in range(H):
                        last = nc.tensor.matmul(bank[4][0:96, :], xpw3[:, hh].rearrange("p a b -> p (a b)"),
                                                xc[:, hh, cs], start=(hh == 0), stop=(hh == H - 1))
                    last.then_inc(s_xd, 1)
                    for hh in range(H):
                        last = nc.tensor.matmul(bank[5][0:R, :], xpw[:, hh, 0:R], xc[:, hh, cs],
                                                start=(hh == 0), stop=(hh == H - 1))
                    last.then_inc(s_xd, 1)

                def steps_dt(c):
                    pe.wait_ge(s_bc, 8 * c + 8)
                    for hh in range(H):
                        if hh or c:
                            pe.wait_ge(s_dta, 2 * (c * H + hh))
                        nc.tensor.matmul(bank[6][:], dtw[:, hh * P:(hh + 1) * P], lr[:], start=True, stop=True)\
                            .then_inc(s_dtm, 1)

                branches(0)
                for c in range(C + 1):
                    if c + 1 < C:
                        branches(c + 1)
                    if c:
                        steps_dt(c - 1)
                    if c < C:
                        b_c_rank(c)

            @block.scalar
            def _(act):
                act.wait_ge(wl, 16 * len(wloads))
                act.wait_ge(sel0, 1)
                def take_branches(c):
                    cs = slice(c * CW, (c + 1) * CW)
                    act.wait_ge(k.ln_tr, L0 + c + 1)
                    nc.scalar.activation(k.xnT[:, cs], bank[7][:], ACT.Identity, bias=b1[:], scale=g1[:])\
                        .then_inc(k.ln_ev, 1)
                    for b in range(2 * H):
                        act.wait_ge(s_in, 2 * H * c + b + 1)
                        if b < H:
                            nc.scalar.activation(xi[:, b, PAD + c * CW:PAD + (c + 1) * CW], bank[b][:], ACT.Copy)\
                                .then_inc(s_inev, 1)
                        else:
                            nc.scalar.activation(sz[:, b - H, cs], bank[b][:], ACT.Silu).then_inc(s_inev, 1)

                def take_dt(c):
                    cs = slice(c * CW, (c + 1) * CW)
                    for hh in range(H):
                        act.wait_ge(s_dtm, c * H + hh + 1)
                        nc.scalar.activation(dt[:, hh, cs], bank[6][:], ACT.Relu, bias=dtb[:, hh:hh + 1])\
                            .then_inc(s_dta, 1)
                        nc.scalar.activation(dtx[:, hh, cs], bank[6][:], ACT.Abs, bias=dtb[:, hh:hh + 1])\
                            .then_inc(s_dta, 1)

                take_branches(0)
                for c in range(C + 1):
                    if c + 1 < C:
                        take_branches(c + 1)
                    if c:
                        take_dt(c - 1)
                    if c < C:
                        cs = slice(c * CW, (c + 1) * CW)
                        act.wait_ge(s_cv, KC * H * (c + 1))
                        nc.scalar.activation(xc[:, :, cs], xc[:, :, cs], ACT.Silu).then_inc(s_xc, 1)
                act.wait_ge(s_dta, 2 * H * C)
                nc.scalar.activation(dtx[:], dtx[:], ACT.Exp, scale=-1.0).then_inc(s_sp, 1)
                nc.scalar.activation(A[:], A[:], ACT.Exp).then_inc(s_A, 1)
                act.wait_ge(s_sp, 1)
                nc.scalar.activation(dtx[:], dtx[:], ACT.Ln, bias=1.0).then_inc(s_sp, 1)
                act.wait_ge(s_A, 2)
                nc.scalar.mul(A[:], A[:], -1.0)
        k.L += C

        q_bc = k.sem("q_bc")
        q_dA = k.sem("q_dA")
        q_cs = k.sem("q_cs")
        q_dBx = k.sem("q_dBx")
        q_h = k.sem("q_h")
        q_hC = k.sem("q_hC")
        q_st = k.sem("q_st")
        q_y = k.sem("q_y")
        q_yc = k.sem("q_yc")
        q_yg = k.sem("q_yg")
        yT = sb("yT", [P, H, CW])
        o_mm = k.sem("o_mm")
        o_x1 = k.sem("o_x1")
        x1 = xo
        assert H == 2
        with nc.Block() as block:
            def spread(pe, c, n):
                u = c * NS + n
                if n >= 2:
                    pe.wait_ge(q_dBx, u - 1)
                    pe.wait_ge(q_cs, u - 1)
                for j in range(2):
                    nc.tensor.matmul(bank[2 * j + n % 2][:], sel[:, j * NS + n, :], BC3[:, bass.ds(c * CW, CW)],
                                     start=True, stop=True).then_inc(q_bc, 1)

            def y_sum(pe, c, n):
                pe.wait_ge(q_hC, c * NS + n + 1)
                for hh in range(H):
                    last = nc.tensor.matmul(bank[4 + hh][:], k.ident[:], hC[:, n % 2, hh, :],
                                            start=(n == 0), stop=(n == NS - 1))
                last.then_inc(q_y, 1)

            @block.tensor
            def _(pe):
                nc.tensor.sem_inc(q_bc, 4)
                nc.tensor.sem_inc(q_y, 1)
                with pe.Fori(0, C) as c:
                    spread(pe, c, 0)
                    for n in range(NS):
                        if n + 1 < NS:
                            spread(pe, c, n + 1)
                        if n >= 1:
                            y_sum(pe, c, n - 1)
                    y_sum(pe, c, NS - 1)
                    pe.wait_ge(q_yg, c + 1)
                    for i in range(CT):
                        for hh in range(H):
                            last = nc.tensor.matmul(bank[6][:, i * P:(i + 1) * P], yT[:, hh, i * P:(i + 1) * P],
                                                    outw[:, hh, :], start=(hh == 0), stop=(hh == H - 1))
                    last.then_inc(o_mm, 1)
                    pe.wait_ge(o_x1, c + 1)

            @block.scalar
            def _(act):
                with act.Fori(0, C) as c:
                    for n in range(NS):
                        u = c * NS + n
                        if n >= 2:
                            k.wait_alone(act, q_h, 2 * u - 2)
                        for hh in range(H):
                            nc.scalar.activation(dA[:, n % 2, hh, :], dt[:, hh, bass.ds(c * CW, CW)], ACT.Exp,
                                                 scale=A[:, hh, n:n + 1]).then_inc(q_dA, 1)
                        act.wait_ge(q_bc, 2 * u + 2 + 4)
                        if n >= 2:
                            act.wait_ge(q_hC, u - 1)
                        nc.scalar.activation(Cs[:, n % 2, :], bank[2 + n % 2][:], ACT.Copy).then_inc(q_cs, 1)
                    act.wait_ge(q_hC, c * NS + NS)

            @block.vector
            def _(dve):
                with dve.Fori(0, C) as c:
                    for n in range(NS):
                        u = c * NS + n
                        dve.wait_ge(q_bc, 2 * u + 1 + 4)
                        nc.vector.tensor_tensor(dBx[:, n % 2], dtx[:, :, bass.ds(c * CW, CW)],
                                                bank[n % 2][:, None, :].to_broadcast([P, H, CW]), ALU.mult)\
                            .then_inc(q_dBx, 1)
                        dve.wait_ge(q_dBx, u + 1)
                        dve.wait_ge(q_dA, 2 * u + 2)
                        if n >= 2:
                            dve.wait_ge(q_hC, u - 1)
                            dve.wait_ge(q_st, u - 1)
                        for hh in range(H):
                            nc.vector.tensor_tensor_scan(h[:, n % 2, hh, :], dA[:, n % 2, hh, :], dBx[:, n % 2, hh, :],
                                                         state[:, n, hh:hh + 1], ALU.mult, ALU.add).then_inc(q_h, 1)
                    dve.wait_ge(q_y, c * NS + NS + 1)
                    for hh in range(H):
                        nc.vector.scalar_tensor_tensor(out=yT[:, hh, :], in0=xc[:, hh, bass.ds(c * CW, CW)],
                                                       scalar=Dp[:, hh:hh + 1], in1=bank[4 + hh][:],
                                                       op0=ALU.mult, op1=ALU.add).then_inc(q_yc, 1)
                    dve.wait_ge(q_yc, 2 * c + 2)
                    nc.vector.tensor_tensor(yT[:], yT[:], sz[:, :, bass.ds(c * CW, CW)], ALU.mult).then_inc(q_yg, 1)
                    dve.wait_ge(o_mm, c + 1)
                    xt = x1[:, bass.ds(c * CT, CT), :]
                    nc.vector.tensor_tensor(xt, bank[6][:].rearrange("p (i d) -> p i d", i=CT), xt, ALU.add)\
                        .then_inc(o_x1, 1)
                    dve.wait_ge(q_st, c * NS + NS)

            @block.gpsimd
            def _(pool):
                with pool.Fori(0, C) as c:
                    for n in range(NS):
                        u = c * NS + n
                        pool.wait_ge(q_h, 2 * u + 2)
                        pool.wait_ge(q_cs, u + 1)
                        if n >= 2:
                            pool.wait_ge(q_y, u - 1 + 1)
                        nc.gpsimd.tensor_tensor(hC[:, n % 2], h[:, n % 2],
                                                Cs[:, n % 2, None, :].to_broadcast([P, H, CW]), ALU.mult)\
                            .then_inc(q_hC, 1)
                        nc.gpsimd.tensor_copy(state[:, n, :], h[:, n % 2, :, CW - 1]).then_inc(q_st, 1)
                    pool.wait_ge(q_y, c * NS + NS + 1)

        hT = [dtx[:].rearrange("p h n -> p (h n)")[:, b * FB * CW:(b + 1) * FB * CW].rearrange("p (f w) -> p f w", f=FB)
              for b in range(2)]
        f_x = k.sem("f_x")
        f_cp = k.sem("f_cp")
        f_h = k.sem("f_h")
        f_ev = k.sem("f_ev")
        f_y = k.sem("f_y")
        L1 = k.L
        with nc.Block() as block:
            @block.gpsimd
            def _(pool):
                for c in range(C):
                    k.norm_pool(L1 + c)

            @block.vector
            def _(dve):
                for c in range(C):
                    xt = k.X[:, c * CT:(c + 1) * CT, :]
                    nc.vector.tensor_tensor(xt, xt, x1[:, c * CT:(c + 1) * CT, :], ALU.add).then_inc(f_x, 1)
                keep, k.X = k.X, x1
                for c in range(C):
                    k.norm_vector(L1 + c, c)
                k.X = keep
                for c in range(C):
                    dve.wait_ge(f_x, c + 1)
                    dve.wait_ge(f_y, c + 1)
                    xt = k.X[:, c * CT:(c + 1) * CT, :]
                    nc.vector.tensor_tensor(xt, bank[4 + c % 2][:].rearrange("p (i d) -> p i d", i=CT), xt, ALU.add)\
                        .then_inc(f_cp, 1)

            @block.tensor
            def _(pe):
                for c in range(C):
                    k.norm_tensor(L1 + c)
                    pe.wait_ge(k.ln_ev, L1 + c + 1)
                    for f in range(FB):
                        if c:
                            pe.wait_ge(f_ev, (c - 1) * FB + f + 1)
                        nc.tensor.matmul(bank[f][:], w1[:, f * P:(f + 1) * P], k.xnT[:, c * CW:(c + 1) * CW],
                                         start=True, stop=True).then_inc(f_h, 1)
                    if c >= 2:
                        pe.wait_ge(f_cp, c - 1)
                    pe.wait_ge(f_ev, c * FB + FB)
                    for i in range(CT):
                        dst = bank[4 + c % 2][:, i * P:(i + 1) * P]
                        nc.tensor.matmul(dst, k.ones[0:1, :], w2b[:], start=True, stop=False)
                        for f in range(FB):
                            last = nc.tensor.matmul(dst, hT[c % 2][:, f, i * P:(i + 1) * P], w2[:, f, :],
                                                    start=False, stop=(f == FB - 1))
                    last.then_inc(f_y, 1)

            @block.scalar
            def _(act):
                for c in range(C):
                    act.wait_ge(k.ln_tr, L1 + c + 1)
                    nc.scalar.activation(k.xnT[:, c * CW:(c + 1) * CW], bank[7][:], ACT.Identity, bias=b2[:],
                                         scale=g2[:]).then_inc(k.ln_ev, 1)
                    for f in range(FB):
                        act.wait_ge(f_h, c * FB + f + 1)
                        if c >= 2:
                            act.wait_ge(f_y, c - 1)
                        nc.scalar.activation(hT[c % 2][:, f, :], bank[f][:], ACT.Gelu_apprx_tanh,
                                             bias=w1b[:, f:f + 1]).then_inc(f_ev, 1)
        k.L += C


def top_two(k, dve, act_sem, src, top, ti, tf, s):
    nc = k.nc
    for i in range(k.T):
        last = nc.vector.max(top[:, i, :], src[:, i, :])
    last.then_inc(s, 1)
    dve.wait_ge(s, act_sem + 1)
    for i in range(k.T):
        last = nc.vector.max_index(ti[:, i, :], top[:, i, :], src[:, i, :])
    last.then_inc(s, 1)
    dve.wait_ge(s, act_sem + 2)
    nc.vector.tensor_copy(tf[:], ti[:, :, 0:2]).then_inc(s, 1)


def experts(k, name, gated):
    nc, t, C, T, E = k.nc, k.t, k.C, k.T, k.E
    L0, bank, pre = k.L, k.bank, name
    FB = t[pre + "_w1"].shape[2] // P
    tmp = ExitStack()
    sb = lambda n, shape, dt=F32: k.sb(f"{name}_{n}", shape, dt, tmp)
    sem = lambda n: k.sem(f"{name}_{n}")
    with tmp:
        gw = sb("gw", [P, E])
        gb = sb("gb", [1, E])
        lg = sb("lg", [P, T, E])
        top = sb("top", [P, T, E])
        ti = sb("ti", [P, T, E], U32)
        tf = sb("tf", [P, T, 2])
        ex = sb("ex", [P, T])
        den = sb("den", [P, T])
        wt = sb("wt", [P, 2, T])
        pick = sb("pick", [P, 2, T])
        comb = sb("comb", [P, E, T])
        wa = [sb(f"wa{u}", [P, FB * P]) for u in range(2)]
        wu = [sb(f"wu{u}", [P, FB * P]) for u in range(2)] if gated else None
        wd = [sb(f"wd{u}", [P, FB, P]) for u in range(2)]
        ba = None if gated else [sb(f"ba{u}", [P, FB]) for u in range(2)]
        bd = None if gated else sb("bd", [E, P])
        combT = None if gated else sb("combT", [E, T, P])
        sg = sb("sg", [P, 2, CW]) if gated else None
        hT = [sb(f"hT{b}", [P, FB, CW]) for b in range(2)]
        NH = 2 if gated else 4
        ND = 3

        g_w, g_mm, g_top, g_ex, g_cb = sem("gate_w"), sem("gate_mm"), sem("gate_top"), sem("gate_ex"), sem("gate_cb")
        w_ready = [sem(f"w_ready{u}") for u in range(2)]
        s_h, s_sg, s_hev, s_y, s_x, s_e = (sem(n) for n in ("h", "sg", "hev", "y", "x", "e_done"))
        s_ct, s_cc, s_bo, s_bx = (sem(n) for n in ("comb_turned", "comb_copied", "bias_out", "bias_added"))

        with nc.Block() as block:
            @block.sync
            def _(sp):
                sp.dma_start(gw[:], t[pre + "_gate_w"]).then_inc(g_w, 16)
                if not gated:
                    sp.dma_start(gb[:], t[pre + "_gate_b"].rearrange("(o e) -> o e", o=1)).then_inc(g_w, 16)
                    sp.dma_start(bd[:], t[pre + "_b2"]).then_inc(g_w, 16)

            @block.gpsimd
            def _(pool):
                for c in range(C):
                    k.norm_pool(L0 + c)

            @block.scalar
            def _(act):
                for c in range(C):
                    k.norm_scalar(L0 + c, k.xnT[:, c * CW:(c + 1) * CW])
                act.wait_ge(g_cb, 2)
                nc.scalar.activation(ex[:], den[:], ACT.Exp).then_inc(g_ex, 1)

            @block.tensor
            def _(pe):
                pe.wait_ge(g_w, 16 if gated else 48)
                for c in range(C):
                    k.norm_tensor(L0 + c)
                    pe.wait_ge(k.ln_ev, L0 + c + 1)
                    for i in range(c * CT, (c + 1) * CT):
                        dst = bank[6][:, i * E:(i + 1) * E]
                        last = nc.tensor.matmul(dst, k.xnT[:, i * P:(i + 1) * P], gw[:], start=True, stop=gated)
                        if not gated:
                            last = nc.tensor.matmul(dst, k.ones[0:1, :], gb[:], start=False, stop=True)
                last.then_inc(g_mm, 1)

            @block.vector
            def _(dve):
                for c in range(C):
                    k.norm_vector(L0 + c, c)
                dve.wait_ge(g_mm, 1)
                nc.vector.tensor_copy(lg[:], bank[6][:, 0:T * E].rearrange("p (t e) -> p t e", t=T)).then_inc(g_cb, 1)
                dve.wait_ge(g_cb, 1)
                top_two(k, dve, 0, lg, top, ti, tf, g_top)
                nc.vector.tensor_tensor(den[:], top[:, :, 1], top[:, :, 0], ALU.subtract).then_inc(g_cb, 1)
                dve.wait_ge(g_ex, 1)
                nc.vector.tensor_scalar(den[:], ex[:], 1.0, None, ALU.add).then_inc(g_cb, 1)
                dve.wait_ge(g_cb, 3)
                nc.vector.reciprocal(wt[:, 0, :], den[:]).then_inc(g_cb, 1)
                dve.wait_ge(g_cb, 4)
                nc.vector.tensor_tensor(wt[:, 1, :], ex[:], wt[:, 0, :], ALU.mult).then_inc(g_cb, 1)
                dve.wait_ge(g_cb, 5)
                dve.wait_ge(g_top, 3)
                for e in range(E):
                    if e:
                        dve.wait_ge(g_cb, 5 + 2 * e)
                    for j in range(2):
                        last = nc.vector.scalar_tensor_tensor(out=pick[:, j, :], in0=tf[:, :, j], scalar=float(e),
                                                              in1=wt[:, j, :], op0=ALU.is_equal, op1=ALU.mult)
                    last.then_inc(g_cb, 1)
                    dve.wait_ge(g_cb, 6 + 2 * e)
                    nc.vector.tensor_tensor(comb[:, e, :], pick[:, 0, :], pick[:, 1, :], ALU.add).then_inc(g_cb, 1)
        k.L += C

        with nc.Block() as block:
            @block.sync
            def _(sp):
                with nc.allow_non_contiguous_dma(reason="bias columns"):
                    with sp.Fori(0, E // 2) as ep:
                        for u in range(2):
                            e = ep * 2 + u
                            sp.wait_ge(s_e, e + 1)
                            one = lambda n: t[pre + n][bass.ds(e, 1)]
                            loads = [(wa[u][:], one("_w1").rearrange("o p f -> (o p) f")),
                                     (wd[u][:], one("_w2").rearrange("o (f p) d -> (o p) f d", p=P))]
                            if gated:
                                loads.append((wu[u][:], one("_wu").rearrange("o p f -> (o p) f")))
                            else:
                                loads.append((ba[u][:], one("_b1").rearrange("o (f p) -> (o p) f", p=P)))
                            for dst, src in loads:
                                sp.dma_start(dst, src).then_inc(w_ready[u], 16)

            @block.tensor
            def _(pe):
                nc.tensor.sem_inc(s_e, 2)
                nc.tensor.sem_inc(s_y, 2)

                def hidden(ep, u, c):
                    q = (ep * 2 + u) * C + c
                    if c == 0:
                        pe.wait_ge(w_ready[u], (ep + 1) * (16 * ND))
                    for f in range(FB):
                        pe.wait_ge(s_hev, q * FB + f + 1)
                        xc = k.xnT[:, c * CW:(c + 1) * CW]
                        last = nc.tensor.matmul(bank[f % NH][:], wa[u][:, f * P:(f + 1) * P], xc, start=True, stop=True)
                        if gated:
                            last.then_inc(s_h, 1)
                            last = nc.tensor.matmul(bank[2 + f % 2][:], wu[u][:, f * P:(f + 1) * P], xc,
                                                    start=True, stop=True)
                        last.then_inc(s_h, 1)

                def down(ep, u, c):
                    q = (ep * 2 + u) * C + c
                    pe.wait_ge(s_hev, q * FB + FB + NH)
                    pe.wait_ge(s_x, q + 1)
                    for i in range(CT):
                        dst = bank[4 + c % 2][:, i * P:(i + 1) * P]
                        for f in range(FB):
                            last = nc.tensor.matmul(dst, hT[c % 2][:, f, i * P:(i + 1) * P], wd[u][:, f, :],
                                                    start=(f == 0), stop=(f == FB - 1))
                    last.then_inc(s_y, 1)

                if not gated:
                    for c in range(C):
                        for i in range(CT):
                            last = nc.tensor.transpose(bank[4 + c][0:E, i * P:(i + 1) * P], comb[:, :, c * CT + i],
                                                       k.ident[:])
                        last.then_inc(s_ct, 1)
                    for c in range(C):
                        pe.wait_ge(s_cc, c + 1)
                        for i in range(CT):
                            last = nc.tensor.matmul(bank[c][:, i * P:(i + 1) * P], combT[:, c * CT + i, :], bd[:],
                                                    start=True, stop=True)
                        last.then_inc(s_bo, 1)
                    pe.wait_ge(s_bx, C)
                with pe.Fori(0, E // 2) as ep:
                    units = [(u, c) for u in range(2) for c in range(C)]
                    hidden(ep, *units[0])
                    for n, unit in enumerate(units):
                        if n + 1 < len(units):
                            hidden(ep, *units[n + 1])
                        down(ep, *unit)
                        if unit[1] == C - 1:
                            nc.tensor.drain().then_inc(s_e, 1)

            @block.scalar
            def _(act):
                if not gated:
                    nc.scalar.sem_inc(s_hev, NH)
                with act.Fori(0, E // 2) as ep:
                    for u in range(2):
                        for c in range(C):
                            q = (ep * 2 + u) * C + c
                            for f in range(FB):
                                b = q * FB + f
                                if gated:
                                    act.wait_ge(s_hev, b + 1)
                                    act.wait_ge(s_h, 2 * b + 1)
                                    nc.scalar.activation(sg[:, f % 2, :], bank[f % 2][:], ACT.Silu).then_inc(s_sg, 1)
                                else:
                                    if f == 0:
                                        act.wait_ge(s_y, q + 1)
                                    act.wait_ge(s_h, b + 1)
                                    nc.scalar.activation(hT[c % 2][:, f, :], bank[f][:], ACT.Relu,
                                                         bias=ba[u][:, f:f + 1]).then_inc(s_hev, 1)

            @block.vector
            def _(dve):
                nc.vector.sem_inc(s_x, 2)
                if gated:
                    nc.vector.sem_inc(s_hev, NH)

                def up(ep, u, c):
                    q = (ep * 2 + u) * C + c
                    for f in range(FB):
                        b = q * FB + f
                        if f == 0:
                            dve.wait_ge(s_y, q + 1)
                        dve.wait_ge(s_h, 2 * b + 2)
                        dve.wait_ge(s_sg, b + 1)
                        nc.vector.tensor_tensor(hT[c % 2][:, f, :], bank[2 + f % 2][:], sg[:, f % 2, :], ALU.mult)\
                            .then_inc(s_hev, 1)

                def add(ep, u, c):
                    e = ep * 2 + u
                    q = e * C + c
                    dve.wait_ge(s_x, q + 1)
                    dve.wait_ge(s_y, q + 1 + 2)
                    for i in range(CT):
                        xt = k.X[:, c * CT + i, :]
                        last = nc.vector.scalar_tensor_tensor(
                            out=xt, in0=bank[4 + c % 2][:, i * P:(i + 1) * P],
                            scalar=comb[:, bass.ds(e, 1), c * CT + i], in1=xt, op0=ALU.mult, op1=ALU.add)
                    last.then_inc(s_x, 1)

                if not gated:
                    for c in range(C):
                        dve.wait_ge(s_ct, c + 1)
                        nc.vector.tensor_copy(combT[:, c * CT:(c + 1) * CT, :],
                                              bank[4 + c][0:E, :].rearrange("p (i q) -> p i q", i=CT)).then_inc(s_cc, 1)
                    for c in range(C):
                        dve.wait_ge(s_bo, c + 1)
                        xt = k.X[:, c * CT:(c + 1) * CT, :]
                        nc.vector.tensor_tensor(xt, bank[c][:].rearrange("p (i d) -> p i d", i=CT), xt, ALU.add)\
                            .then_inc(s_bx, 1)
                    dve.wait_ge(s_bx, C)
                with dve.Fori(0, E // 2) as ep:
                    units = [(u, c) for u in range(2) for c in range(C)]
                    if gated:
                        up(ep, *units[0])
                    for n, unit in enumerate(units):
                        if gated and n + 1 < len(units):
                            up(ep, *units[n + 1])
                        add(ep, *unit)


def linear(k):
    nc, t, C, T = k.nc, k.t, k.C, k.T
    L0, bank = k.L, k.bank
    EPSA = 1e-6
    tmp = ExitStack()
    sb = lambda n, shape, dt=F32: k.sb("lin_" + n, shape, dt, tmp)
    sem = lambda n: k.sem("lin_" + n)
    with tmp:
        wqk, bqk, wv = sb("wqk", [P, 2 * P]), sb("bqk", [1, 2 * P]), sb("wv", [P, P])
        bv, gam = sb("bv", [P, 1]), sb("gam", [P, 1])
        qk, sq = sb("qk", [P, 2, 2 * P]), sb("sq", [P, 2, 2 * P])
        half = sb("half", [P, 2])
        sums = sb("sums", [P, 2 * P])
        nk = sb("nk", [P, 2])
        diag = sb("diag", [P, P])
        Gn, tl, H, M = (sb(n, [P, P]) for n in ("Gn", "tl", "H", "M"))
        rrow = sb("rrow", [1, P])
        lw, s_qk, s_ev, s_g, s_p, s_v, s_m, s_h = (sem(n) for n in ("w", "qk", "ev", "g", "pow", "v", "m", "half"))
        s_o, s_x, s_row = sem("o"), sem("x"), sem("row")
        with nc.Block() as block:
            @block.sync
            def _(sp):
                with nc.allow_non_contiguous_dma(reason="small weights"):
                    for dst, src in ((wqk[:, 0:P], t["lin_wqT"]), (wqk[:, P:2 * P], t["lin_wkT"]), (wv[:], t["lin_wv"]),
                                     (bqk[:, 0:P], t["lin_bq"].rearrange("(o d) -> o d", o=1)),
                                     (bqk[:, P:2 * P], t["lin_bk"].rearrange("(o d) -> o d", o=1)),
                                     (bv[:], t["lin_bv"].rearrange("(d o) -> d o", o=1)),
                                     (gam[:], t["lin_gamma"].partition_broadcast(P))):
                        sp.dma_start(dst, src).then_inc(lw, 16)

            @block.gpsimd
            def _(pool):
                nc.gpsimd.memset(half[:], -0.5).then_inc(s_h, 1)
                for c in range(C):
                    k.norm_pool(L0 + c)
                pool.wait_ge(s_h, 1)
                pool.wait_ge(s_v, 2)
                nc.gpsimd.tensor_tensor(nk[:], nk[:], half[:], ALU.pow).then_inc(s_p, 1)

            @block.scalar
            def _(act):
                for c in range(C):
                    k.norm_scalar(L0 + c, k.xnT[:, c * CW:(c + 1) * CW])
                    for i in range(c * CT, (c + 1) * CT):
                        act.wait_ge(s_qk, i + 1)
                        if i >= 2:
                            act.wait_ge(s_g, i - 1)
                        nc.scalar.activation(qk[:, i % 2, :], bank[i % 2][:, 0:2 * P], ACT.Copy).then_inc(s_ev, 1)
                        nc.scalar.activation(sq[:, i % 2, :], bank[i % 2][:, 0:2 * P], ACT.Square).then_inc(s_ev, 1)

            @block.tensor
            def _(pe):
                pe.wait_ge(lw, 16 * 7)

                def gram(i):
                    pe.wait_ge(s_ev, 2 * i + 2)
                    q, kk, q2, k2 = (a[:, i % 2, b * P:(b + 1) * P] for a in (qk, sq) for b in range(2))
                    f, z = i == 0, i == T - 1
                    nc.tensor.matmul(bank[2][:, 0:P], kk, q, start=f, stop=z)
                    nc.tensor.matmul(bank[3][:, 0:P], k.ones[:], q, start=f, stop=z)
                    nc.tensor.matmul(bank[4][:, 0:1], q2, k.ones[:, 0:1], start=f, stop=z)
                    nc.tensor.matmul(bank[5][:, 0:1], k2, k.ones[:, 0:1], start=f, stop=z).then_inc(s_g, 1)

                for c in range(C):
                    k.norm_tensor(L0 + c)
                    pe.wait_ge(k.ln_ev, L0 + c + 1)
                    for i in range(c * CT, (c + 1) * CT):
                        if i >= 2:
                            pe.wait_ge(s_ev, 2 * i - 2)
                        nc.tensor.matmul(bank[i % 2][:, 0:2 * P], k.xnT[:, i * P:(i + 1) * P], wqk[:], start=True, stop=False)
                        nc.tensor.matmul(bank[i % 2][:, 0:2 * P], k.ones[0:1, :], bqk[:], start=False, stop=True)\
                            .then_inc(s_qk, 1)
                        if i:
                            gram(i - 1)
                gram(T - 1)
                pe.wait_ge(s_row, 1)
                nc.tensor.matmul(bank[4][:, 0:P], k.ones[:], diag[:], start=True, stop=True).then_inc(s_row, 1)
                pe.wait_ge(s_v, 3)
                nc.tensor.matmul(bank[3][:, 0:P], k.ones[:], Gn[:], start=True, stop=True).then_inc(s_m, 1)
                pe.wait_ge(s_v, 8)
                nc.tensor.matmul(bank[4][:, 0:P], wv[:], H[:], start=True, stop=True)
                nc.tensor.matmul(bank[5][0:1, 0:P], bv[:], H[:], start=True, stop=True).then_inc(s_m, 1)

            @block.vector
            def _(dve):
                v = nc.vector
                for c in range(C):
                    k.norm_vector(L0 + c, c)
                dve.wait_ge(lw, 16 * 7)
                dve.wait_ge(s_g, T)
                v.tensor_copy(sums[:, 0:P], bank[3][:, 0:P]).then_inc(s_v, 1)
                v.tensor_copy(nk[:, 1:2], bank[4][:, 0:1])
                v.tensor_copy(nk[:, 0:1], bank[5][:, 0:1]).then_inc(s_v, 1)
                dve.wait_ge(s_p, 1)
                v.tensor_scalar(diag[:], k.ident[:], nk[:, 1:2], None, ALU.mult).then_inc(s_row, 1)
                dve.wait_ge(s_row, 2)
                v.tensor_copy(sums[:, P:2 * P], bank[4][:, 0:P]).then_inc(s_row, 1)
                dve.wait_ge(s_row, 3)
                v.scalar_tensor_tensor(out=Gn[:], in0=bank[2][:, 0:P], scalar=nk[:, 0:1], in1=sums[:, P:2 * P],
                                       op0=ALU.mult, op1=ALU.mult).then_inc(s_v, 1)
                dve.wait_ge(s_v, 3)
                v.scalar_tensor_tensor(out=tl[:], in0=sums[:, 0:P], scalar=EPSA, in1=sums[:, P:2 * P],
                                       op0=ALU.mult, op1=ALU.mult).then_inc(s_v, 1)
                dve.wait_ge(s_v, 4)
                dve.wait_ge(s_m, 1)
                v.scalar_tensor_tensor(out=tl[:], in0=tl[:], scalar=float(P), in1=bank[3][:, 0:P],
                                       op0=ALU.add, op1=ALU.add).then_inc(s_v, 1)
                dve.wait_ge(s_v, 5)
                v.reciprocal(tl[:], tl[:]).then_inc(s_v, 1)
                dve.wait_ge(s_v, 6)
                v.scalar_tensor_tensor(out=H[:], in0=Gn[:], scalar=1.0, in1=tl[:], op0=ALU.add, op1=ALU.mult)\
                    .then_inc(s_v, 1)
                dve.wait_ge(s_v, 7)
                v.tensor_scalar(H[:], H[:], gam[:], None, ALU.mult).then_inc(s_v, 1)
                dve.wait_ge(s_m, 2)
                v.tensor_tensor(M[:], bank[4][:, 0:P], k.ident[:], ALU.add)
                v.tensor_copy(rrow[:], bank[5][0:1, 0:P])
        k.L += C
        with nc.Block() as block:
            @block.tensor
            def _(pe):
                for c in range(C):
                    if c >= 2:
                        pe.wait_ge(s_x, c - 1)
                    for i in range(CT):
                        dst = bank[c % 2][:, i * P:(i + 1) * P]
                        a = (c * CT + i) * P
                        nc.tensor.matmul(dst, k.xnT[:, a:a + P], M[:], start=True, stop=False)
                        last = nc.tensor.matmul(dst, k.ones[0:1, :], rrow[:], start=False, stop=True)
                    last.then_inc(s_o, 1)

            @block.vector
            def _(dve):
                for c in range(C):
                    dve.wait_ge(s_o, c + 1)
                    xt = k.X[:, c * CT:(c + 1) * CT, :]
                    nc.vector.tensor_tensor(xt, bank[c % 2][:].rearrange("p (i d) -> p i d", i=CT), xt, ALU.add)\
                        .then_inc(s_x, 1)


def deep(k):
    nc, t, C, T, E = k.nc, k.t, k.C, k.T, k.E
    L0, bank = k.L, k.bank
    tmp = ExitStack()
    sb = lambda n, shape, dt=F32: k.sb("deep_" + n, shape, dt, tmp)
    sem = lambda n: k.sem("deep_" + n)
    with tmp:
        gw, gb = sb("gw", [P, E]), sb("gb", [E, 1])
        w1, w2, w3 = (sb(n, [P, E, P]) for n in ("w1", "w2", "w3"))
        c1, c2, r3 = sb("c1", [P, E]), sb("c2", [P, E]), sb("r3", [P, E, P])
        W = [sb(f"W{i}", [P, 3, P]) for i in range(2)]
        lg = sb("lg", [E, k.N])
        mx, sm = sb("mx", [E, 1]), sb("sm", [E, 1])
        pr, top, ti = sb("pr", [P, T, E]), sb("top", [P, T, E]), sb("ti", [P, T, E], U32)
        tf = sb("tf", [P, T, 2])
        pick = sb("pick", [P, 4, T])
        comb, ind = sb("comb", [P, E, T]), sb("ind", [P, T, E])
        h1 = [sb(f"h1{b}", [P, CW]) for b in range(2)]
        h2 = [sb(f"h2{b}", [P, CW]) for b in range(2)]
        ry = [sb(f"ry{b}", [P, CW]) for b in range(2)]
        vrow, vE = sb("vrow", [1, E, P]), sb("vE", [E, P])
        indT = sb("indT", [E, T, P])
        lw, s_lg, s_lge, s_sm, s_ex, s_pt, s_pc, s_top, s_cb = (
            sem(n) for n in ("w", "lg", "lge", "sm", "ex", "pt", "pc", "top", "cb"))
        with nc.Block() as block:
            @block.sync
            def _(sp):
                with nc.allow_non_contiguous_dma(reason="small weights"):
                    for dst, src in ((gw[:], t["deep_gate_w"]), (gb[:], t["deep_gate_b"].rearrange("(e o) -> e o", o=1)),
                                     (w1[:], t["deep_w1"].rearrange("e p o -> p e o")),
                                     (w2[:], t["deep_w2"].rearrange("e p o -> p e o")),
                                     (w3[:], t["deep_w3"].rearrange("e p o -> p e o")),
                                     (c1[:], t["deep_b1"].rearrange("e p -> p e")),
                                     (c2[:], t["deep_b2"].rearrange("e p -> p e")),
                                     (r3[:].rearrange("p e o -> p (e o)"),
                                      t["deep_b3"].rearrange("e o -> (e o)").partition_broadcast(P))):
                        sp.dma_start(dst, src).then_inc(lw, 16)

            @block.gpsimd
            def _(pool):
                for c in range(C):
                    k.norm_pool(L0 + c)

            @block.scalar
            def _(act):
                act.wait_ge(lw, 16 * 8)
                for c in range(C):
                    k.norm_scalar(L0 + c, k.xnT[:, c * CW:(c + 1) * CW])
                    act.wait_ge(s_lg, c + 1)
                    nc.scalar.activation(lg[:, c * CW:(c + 1) * CW], bank[c % 2][0:E, :], ACT.Identity, bias=gb[:])\
                        .then_inc(s_lge, 1)
                act.wait_ge(s_sm, 1)
                nc.scalar.activation(lg[:], lg[:], ACT.Exp, bias=mx[:], accum_out=sm[:]).then_inc(s_ex, 1)

            @block.tensor
            def _(pe):
                pe.wait_ge(lw, 16 * 8)
                for c in range(C):
                    k.norm_tensor(L0 + c)
                    pe.wait_ge(k.ln_ev, L0 + c + 1)
                    if c >= 2:
                        pe.wait_ge(s_lge, c - 1)
                    nc.tensor.matmul(bank[c % 2][0:E, :], gw[:], k.xnT[:, c * CW:(c + 1) * CW], start=True, stop=True)\
                        .then_inc(s_lg, 1)
                pe.wait_ge(s_sm, 3)
                for i in range(T):
                    last = nc.tensor.transpose(bank[2][:, i * E:(i + 1) * E], lg[:, i * P:(i + 1) * P], k.ident[0:E, 0:E])
                last.then_inc(s_pt, 1)
                pe.wait_ge(s_cb, 1 + E)
                for h in range(T // CT):
                    for i in range(CT):
                        last = nc.tensor.transpose(bank[3 + h][0:E, i * P:(i + 1) * P], ind[:, h * CT + i, :], k.ident[:])
                    last.then_inc(s_pt, 1)

            @block.vector
            def _(dve):
                v = nc.vector
                for c in range(C):
                    k.norm_vector(L0 + c, c)
                dve.wait_ge(s_lge, C)
                v.tensor_reduce(mx[:], lg[:], AX.X, ALU.max, negate=True).then_inc(s_sm, 1)
                dve.wait_ge(s_ex, 1)
                v.reciprocal(sm[:], sm[:]).then_inc(s_sm, 1)
                dve.wait_ge(s_sm, 2)
                v.tensor_scalar(lg[:], lg[:], sm[:], None, ALU.mult).then_inc(s_sm, 1)
                dve.wait_ge(s_pt, 1)
                v.tensor_copy(pr[:], bank[2][:, 0:T * E].rearrange("p (t e) -> p t e", t=T)).then_inc(s_cb, 1)
                dve.wait_ge(s_cb, 1)
                top_two(k, dve, 0, pr, top, ti, tf, s_top)
                dve.wait_ge(s_top, 3)
                for e in range(E):
                    if e:
                        dve.wait_ge(s_cb, 1 + e)
                    for j in range(2):
                        v.scalar_tensor_tensor(out=pick[:, j, :], in0=tf[:, :, j], scalar=float(e),
                                               in1=top[:, :, j], op0=ALU.is_equal, op1=ALU.mult)
                        last = v.tensor_scalar(pick[:, 2 + j, :], tf[:, :, j], float(e), None, ALU.is_equal)
                    last.then_inc(s_pc, 1)
                    dve.wait_ge(s_pc, e + 1)
                    v.tensor_tensor(comb[:, e, :], pick[:, 0, :], pick[:, 1, :], ALU.add)
                    v.tensor_tensor(ind[:, :, e], pick[:, 2, :], pick[:, 3, :], ALU.add).then_inc(s_cb, 1)
                for h in range(T // CT):
                    dve.wait_ge(s_pt, 2 + h)
                    v.tensor_copy(indT[:, h * CT:(h + 1) * CT, :],
                                  bank[3 + h][0:E, :].rearrange("p (i q) -> p i q", i=CT))
        k.L += C

        s_W, s_a, s_ae, s_b, s_be, s_y, s_yb, s_ye, s_v, s_ve, s_e, s_dma, s_o, s_x = (
            sem(n) for n in ("W", "a", "ae", "b", "be", "y", "yb", "ye", "v", "ve", "e", "dma", "o", "x"))
        with nc.Block() as block:
            @block.sync
            def _(sp):
                sp.wait_ge(s_ve, E)
                sp.dma_start(vE[:], vrow[:]).then_inc(s_dma, 16)

            @block.gpsimd
            def _(pool):
                for e in range(E):
                    if e >= 2:
                        pool.wait_ge(s_e, e - 1)
                    for n, w in enumerate((w1, w2, w3)):
                        last = nc.gpsimd.tensor_copy(W[e % 2][:, n, :], w[:, e, :])
                    last.then_inc(s_W, 1)

            @block.scalar
            def _(act):
                for e in range(E):
                    for c in range(C):
                        q = e * C + c
                        act.wait_ge(s_a, q + 1)
                        if q >= 2:
                            act.wait_ge(s_b, q - 1)
                        nc.scalar.activation(h1[c % 2][:], bank[c % 2][:], ACT.Relu, bias=c1[:, e:e + 1]).then_inc(s_ae, 1)
                        act.wait_ge(s_b, q + 1)
                        if q >= 2:
                            act.wait_ge(s_y, q - 1)
                        nc.scalar.activation(h2[c % 2][:], bank[2 + c % 2][:], ACT.Relu, bias=c2[:, e:e + 1])\
                            .then_inc(s_be, 1)

            @block.tensor
            def _(pe):
                def first(e, c):
                    q = e * C + c
                    if c == 0:
                        pe.wait_ge(s_W, e + 1)
                    if q >= 2:
                        pe.wait_ge(s_ae, q - 1)
                    nc.tensor.matmul(bank[c % 2][:], W[e % 2][:, 0, :], k.xnT[:, c * CW:(c + 1) * CW],
                                     start=True, stop=True).then_inc(s_a, 1)

                def second(e, c):
                    q = e * C + c
                    pe.wait_ge(s_ae, q + 1)
                    if q >= 2:
                        pe.wait_ge(s_be, q - 1)
                    nc.tensor.matmul(bank[2 + c % 2][:], W[e % 2][:, 1, :], h1[c % 2][:], start=True, stop=True)\
                        .then_inc(s_b, 1)

                def third(e, c):
                    q = e * C + c
                    pe.wait_ge(s_be, q + 1)
                    if q >= 2:
                        pe.wait_ge(s_ye, q - 1)
                    for i in range(CT):
                        dst = bank[4 + c % 2][:, i * P:(i + 1) * P]
                        last = nc.tensor.matmul(dst, h2[c % 2][:, i * P:(i + 1) * P], W[e % 2][:, 2, :],
                                                start=True, stop=True)
                    last.then_inc(s_y, 1)

                def total(e, c):
                    q = e * C + c
                    pe.wait_ge(s_ye, q + 1)
                    if c == 0 and e:
                        pe.wait_ge(s_ve, e)
                    nc.tensor.matmul(bank[6][0:1, :], k.ones[:, 0:1], ry[c % 2][:], start=(c == 0), stop=(c == C - 1))\
                        .then_inc(s_v, 1)

                units = [(e, c) for e in range(E) for c in range(C)]
                for n in range(len(units) + 3):
                    if n < len(units):
                        first(*units[n])
                    if 0 <= n - 1 < len(units):
                        second(*units[n - 1])
                    if 0 <= n - 2 < len(units):
                        third(*units[n - 2])
                        if units[n - 2][1] == C - 1:
                            nc.tensor.drain().then_inc(s_e, 1)
                    if 0 <= n - 3 < len(units):
                        total(*units[n - 3])
                pe.wait_ge(s_dma, 16)
                for c in range(C):
                    if c >= 2:
                        pe.wait_ge(s_x, c - 1)
                    for i in range(CT):
                        last = nc.tensor.matmul(bank[c % 2][:, i * P:(i + 1) * P], indT[:, c * CT + i, :], vE[:],
                                                start=True, stop=True)
                    last.then_inc(s_o, 1)

            def flush(dve, e):
                dve.wait_ge(s_v, C * (e + 1))
                nc.vector.tensor_reduce(vrow[:, e, :], bank[6][0:1, :].rearrange("p (i o) -> p o i", i=CT), AX.X, ALU.add)\
                    .then_inc(s_ve, 1)

            @block.vector
            def _(dve):
                v = nc.vector
                for e in range(E):
                    for c in range(C):
                        q = e * C + c
                        dve.wait_ge(s_y, q + 1)
                        if q >= 2:
                            dve.wait_ge(s_v, q - 1)
                        tiles = lambda a: a[:].rearrange("p (i o) -> p i o", i=CT)
                        v.tensor_tensor(tiles(ry[c % 2]), tiles(bank[4 + c % 2]),
                                        r3[:, e, None, :].to_broadcast([P, CT, P]), ALU.add).then_inc(s_yb, 1)
                        dve.wait_ge(s_yb, q + 1)
                        for i in range(CT):
                            yt = ry[c % 2][:, i * P:(i + 1) * P]
                            last = v.tensor_scalar(yt, yt, 0.0, comb[:, e, c * CT + i:c * CT + i + 1], ALU.max, ALU.mult)
                        last.then_inc(s_ye, 1)
                        if c == 0 and e:
                            flush(dve, e - 1)
                flush(dve, E - 1)
                for c in range(C):
                    dve.wait_ge(s_o, c + 1)
                    xt = k.X[:, c * CT:(c + 1) * CT, :]
                    v.tensor_tensor(xt, bank[c % 2][:].rearrange("p (i d) -> p i d", i=CT), xt, ALU.add).then_inc(s_x, 1)


def softmax_mixer(k, name, windowed):
    nc, t, C, T = k.nc, k.t, k.C, k.T
    bank = k.bank
    HEADS, HD = 16, P // 16
    G = HEADS // 2
    R = 4
    SLOTS = 8
    MAXROW = 6 * HD
    ROWS = MAXROW + 4
    WINDOW = 64
    SCALE = float(HD) ** -0.5
    NW = HEADS // 2
    BW = WINDOW if windowed else P
    HW = BW + P
    heads = lambda w: (4 * (w // 2) + w % 2, 4 * (w // 2) + w % 2 + 2)
    tmp = ExitStack()
    sb = lambda n, shape, dt=F32: k.sb(f"{name}_{n}", shape, dt, tmp)
    sem = lambda n: k.sem(f"{name}_{n}")
    with tmp:
        wqkv, bqkv = sb("wqkv", [P, 3 * P]), sb("bqkv", [1, 3 * P])
        wo = sb("wo", [P, 4, P])
        biasf = sb("biasf", [P, 2, HW])
        q_bias = sb("q_bias", [P, 2 * HW], BF16)
        k_bias = sb("k_bias", [P, 2 * HW], BF16)
        spread = sb("spread", [P, P])
        raw = sb("raw", [P, 2, HEADS, HD // 2, 2]) if windowed else None
        rot = sb("rot", [P, 4, 2 * HEADS, HD // 2]) if windowed else None
        cs = sb("cs", [P, T, 2, HD // 2]) if windowed else None
        xs = sb("xs", [P, P])
        qk = sb("qk", [P, 2, HEADS, HD])
        left = sb("left", [P, 2, 2, HEADS, HD])
        qp, kp, mp = (sb(n, [P, HEADS, SLOTS, HD], BF16) for n in ("qp", "kp", "mp"))
        mx = sb("mx", [P, HEADS])
        mleft = sb("mleft", [P, 2, HEADS])
        V = sb("V", [P, R, HEADS, 32])
        kT = sb("kT", [P, R, G, P], BF16)
        qT = sb("qT", [P, 2, G, P], BF16)
        q2 = sb("q2", [P, 2, G, P], BF16)
        pb = sb("pb", [P, 2, 4 * P])
        osb, rec, on = (sb(n, [P, 4 * P]) for n in ("osb", "rec", "on"))
        square = None if windowed else sb("square", [P, 2, HEADS, HD])
        norm2 = None if windowed else sb("norm2", [P, 2 * HEADS])
        norm2max = None if windowed else sb("norm2max", [P, 2 * HEADS])
        X0 = None if windowed else sb("X0", [P, T, P])
        bf16_bank = lambda b: bank[b][:].bitcast(BF16)

        s_nm, s_first = sem("norm2"), sem("first")
        lw, s_bi, s_z, s_sc = sem("w"), sem("bias"), sem("zero"), sem("spread")
        s_xs, s_qkv, s_raw, s_rot, s_sp, s_kt, s_qt, s_qev = (
            sem(n) for n in ("xs", "qkv", "raw", "rot", "split", "kt", "qt", "qev"))
        s_s, s_mx, s_mp, s_mt, s_q2, s_t, s_ex, s_pv = (
            sem(n) for n in ("s", "mx", "mp", "mt", "q2", "t", "ex", "pv"))
        s_osb, s_rep, s_rec, s_on, s_pr, s_x = (sem(n) for n in ("osb", "rep", "rec", "on", "proj", "x"))
        loads = []
        if windowed:
            loads += [(wqkv[:], t[name + "_wqkv"]), (cs[:], t["rotary"].rearrange("(t p) a d -> p t a d", p=P))]
        else:
            row = lambda n: t[f"{name}_{n}"].rearrange("(o d) -> o d", o=1)
            for a, n in enumerate("qkv"):
                loads += [(wqkv[:, a * P:(a + 1) * P], t[f"{name}_w{n}"]), (bqkv[:, a * P:(a + 1) * P], row(f"b{n}"))]
        late = [(wo[32 * u:32 * u + HD], t[name + "_wo"].rearrange("(g u d) o -> u d g o", u=4, d=HD)[u])
                for u in range(4)]
        if not windowed:
            late.append((wo[HD:HD + 1, 0], row("bo")))

        L0 = k.L
        with nc.Block() as block:
            @block.sync
            def _(sp):
                for dst, src in loads:
                    sp.dma_start(dst, src).then_inc(lw, 16)
                sp.wait_ge(s_z, 1)
                for dst, src in late:
                    sp.dma_start(dst, src).then_inc(lw, 16)
                sp.wait_ge(lw, 16 * len(loads + late))

            @block.gpsimd
            def _(pool):
                n = 0

                def step(ins):
                    nonlocal n
                    n += 1
                    ins.then_inc(s_bi, 1)
                    pool.wait_ge(s_bi, n)

                nc.gpsimd.memset(wo[:], 0.0).then_inc(s_z, 1)
                for c in range(C):
                    k.norm_pool(L0 + c)
                for dst, sign, parts in ((q_bias, 1, ((BW, BW), (P, 0))), (k_bias, -1, ((BW, P), (P, 0)))):
                    at = 0
                    for width, base in parts:
                        out = biasf[:, :, at:at + width]
                        at += width
                        pat = lambda f: [[0, 2], [-f * sign, width]]
                        if windowed:
                            step(nc.gpsimd.memset(out, 0.0))
                        else:
                            step(nc.gpsimd.iota(out, pattern=pat(-1), base=-base, channel_multiplier=-sign,
                                                allow_small_or_imprecise_dtypes=True))
                        step(nc.gpsimd.affine_select(out=out, in_=out, compare_op=ALU.is_ge, fill=MASKED, base=base,
                                                     pattern=pat(1), channel_multiplier=sign))
                        if windowed:
                            step(nc.gpsimd.affine_select(out=out, in_=out, compare_op=ALU.is_ge, fill=MASKED,
                                                         base=WINDOW - base, pattern=pat(-1), channel_multiplier=-sign))
                    step(nc.gpsimd.tensor_copy(dst[:], biasf[:].rearrange("p a c -> p (a c)")))
                before = kT[:, R - 1]
                step(nc.gpsimd.memset(before, 0.0))
                for u in range(2):
                    step(nc.gpsimd.affine_select(out=before, in_=before, compare_op=ALU.not_equal, fill=MASKED,
                                                 base=-(64 * u + MAXROW + 3), pattern=[[0, G], [0, P]],
                                                 channel_multiplier=1))
                step(nc.gpsimd.memset(spread[:], 0.0))
                step(nc.gpsimd.affine_select(out=spread[:].rearrange("p (u m) -> p u m", u=4),
                                             in_=spread[:].rearrange("p (u m) -> p u m", u=4),
                                             compare_op=ALU.not_equal, fill=1.0, base=-HD,
                                             pattern=[[-32, 4], [0, 32]], channel_multiplier=1))

            @block.vector
            def _(dve):
                v = nc.vector
                for a in (qp, mp, V):
                    v.memset(a[:], 0.0)
                v.memset(kp[:], 0.0).then_inc(s_sc, 1)
                for c in range(C):
                    k.norm_vector(L0 + c, c)
                if not windowed:
                    v.memset(norm2max[:], 0.0)
                    v.tensor_copy(X0[:], k.X[:])
                dve.wait_ge(s_sc, 1)
                v.memset(V[:, :, :, HD], 1.0)
                v.memset(kp[:, :, 6, 0:3], 1.0)
                v.memset(qp[:, :, 6, 3], 1.0)

            @block.tensor
            def _(pe):
                for c in range(C):
                    k.norm_tensor(L0 + c)

            @block.scalar
            def _(act):
                for c in range(C):
                    k.norm_scalar(L0 + c, k.xnT[:, c * CW:(c + 1) * CW])
        k.L += C

        IN_LOOP = (T - 4) // R
        last_steps = range(IN_LOOP * R + 1, T)

        def steps(engine, step):
            step(0, 0)
            with engine.Fori(0, IN_LOOP) as c:
                for i in range(R):
                    step(c * R + (i + 1), (i + 1) % R)
            for s in last_steps:
                step(s, s % R)

        to_come = lambda t, ahead: not isinstance(t, int) or t + ahead < T

        def wait(engine, sem, count):
            if not isinstance(count, int) or count > 0:
                engine.wait_ge(sem, count)

        with nc.Block() as block:
            def qkv(pe, y):
                pe.wait_ge(s_xs, y + 1)
                dst = bank[6][:, 0:3 * P]
                last = nc.tensor.matmul(dst, xs[:], wqkv[:], start=True, stop=windowed)
                if not windowed:
                    last = nc.tensor.matmul(dst, k.ones[0:1, :], bqkv[:], start=False, stop=True)
                last.then_inc(s_qkv, 1)

            def turn(pe, y):
                pe.wait_ge(s_sp, 4 * y + 4)
                wait(pe, s_mx, NW * y)
                for b, src, done in ((0, kp, s_kt), (1, qp, s_qt)):
                    for g in range(G):
                        last = nc.tensor.transpose(bf16_bank(b)[:, g * P:(g + 1) * P],
                                                   src[:, 2 * g:2 * g + 2].rearrange("p h s d -> p (h s d)"), k.identb[:])
                    last.then_inc(done, 1)

            def first_pass(pe, y, slot, w):
                if w == 0:
                    pe.wait_ge(s_qev, y + 1)
                wait(pe, s_mx, y * NW + (w - 1))
                out = bank[w % 2]
                nc.tensor.matmul(out[:, 0:2 * HW], k.identb[:], q_bias[:], start=True, stop=False, skip_group_check=True)
                for j, h in enumerate(heads(w)):
                    rows = slice(64 * (h % 2), 64 * (h % 2) + ROWS)
                    for s, (a, b) in enumerate(((0, BW), (BW, HW))):
                        last = nc.tensor.matmul(out[:, j * HW + a:j * HW + b], qT[rows, slot % 2, h // 2, :],
                                                kT[rows, (slot - 1 + s) % R, h // 2, P - (b - a):P],
                                                start=False, stop=(j == 1 and s == 1), skip_group_check=True)
                last.then_inc(s_s, 1)

            def turn_maxima(pe, y):
                pe.wait_ge(s_mp, 5 * y + 5)
                for g in range(G):
                    last = nc.tensor.transpose(bf16_bank(5)[:, g * P:(g + 1) * P],
                                               mp[:, 2 * g:2 * g + 2].rearrange("p h s d -> p (h s d)"), k.identb[:])
                last.then_inc(s_mt, 1)

            def second_pass(pe, y, slot, w):
                if w == 0:
                    pe.wait_ge(s_q2, y + 1)
                wait(pe, s_ex, y * NW + (w - 1))
                out = bank[2 + w % 2]
                nc.tensor.matmul(out[:, 0:2 * HW], k.identb[:], k_bias[:], start=True, stop=False, skip_group_check=True)
                for j, h in enumerate(heads(w)):
                    rows = slice(64 * (h % 2), 64 * (h % 2) + ROWS)
                    for s, (a, b) in enumerate(((0, BW), (BW, HW))):
                        last = nc.tensor.matmul(out[:, j * HW + a:j * HW + b],
                                                kT[rows, (slot - 1 + s) % R, h // 2, :],
                                                q2[rows, slot % 2, h // 2, 0:b - a], start=False, stop=(j == 1 and s == 1), skip_group_check=True)
                last.then_inc(s_t, 1)

            def values(pe, y, slot, w):
                if w == 0:
                    wait(pe, s_osb, y)
                pe.wait_ge(s_ex, y * NW + (w + 1))
                for j, h in enumerate(heads(w)):
                    u, g = h % 4, h // 4
                    for s, (a, b) in ((1, (BW, HW)), (0, (0, BW))):
                        last = nc.tensor.matmul(bank[4][32 * u:32 * u + 32, g * P:g * P + b - a],
                                                V[:, (slot - 1 + s) % R, h, :], pb[:, w % 2, j * HW + a:j * HW + b],
                                                start=(s == 1), stop=(s == 0), skip_group_check=True)
                last.then_inc(s_pv, 1)

            def spread_sums(pe, y):
                pe.wait_ge(s_osb, y + 1)
                nc.tensor.matmul(bank[7][:], spread[:], osb[:], start=True, stop=True).then_inc(s_rep, 1)

            def project(pe, y):
                pe.wait_ge(s_on, y + 1)
                for g in range(4):
                    last = nc.tensor.matmul(bank[7][:, 0:P], on[:, g * P:(g + 1) * P], wo[:, g, :],
                                            start=(g == 0), stop=(g == 3))
                last.then_inc(s_pr, 1)

            def tensor_step(pe, y, slot):
                for w in range(NW):
                    if w == 0 and to_come(y, 2):
                        qkv(pe, y + 2)
                    if w == 1 and (not isinstance(y, int) or y > 0):
                        spread_sums(pe, y - 1)
                    if w == 5 and to_come(y, 1):
                        turn_maxima(pe, y + 1)
                    if w == 7 and to_come(y, 2):
                        turn(pe, y + 2)
                    second_pass(pe, y, slot, w)
                    if w < 4 and to_come(y, 1):
                        first_pass(pe, y + 1, slot + 1, 2 * w)
                        first_pass(pe, y + 1, slot + 1, 2 * w + 1)
                    if w:
                        values(pe, y, slot, w - 1)
                if not isinstance(y, int) or y > 0:
                    project(pe, y - 1)
                values(pe, y, slot, NW - 1)

            @block.tensor
            def _(pe):
                qkv(pe, 0)
                turn(pe, 0)
                qkv(pe, 1)
                for w in range(NW):
                    first_pass(pe, 0, 0, w)
                turn(pe, 1)
                turn_maxima(pe, 0)
                steps(pe, lambda y, slot: tensor_step(pe, y, slot))
                spread_sums(pe, T - 1)
                project(pe, T - 1)

            def stage(act, y):
                if isinstance(y, int):
                    wait(act, s_qkv, y)
                else:
                    k.wait_alone(act, s_qkv, y)
                tile = k.xnT[:].rearrange("p (t q) -> p t q", q=P)[:, bass.ds(y, 1), :]
                nc.scalar.activation(xs[:].rearrange("p (o q) -> p o q", o=1), tile, ACT.Copy).then_inc(s_xs, 1)

            def wide_copies(q, k_, scale):
                wide = lambda a, n: a[:, :, None, :].to_broadcast([P, HEADS, n, HD])
                nc.scalar.activation(qp[:, :, 0:3, :], wide(q, 3), ACT.Copy, scale=scale)
                nc.scalar.activation(kp[:, :, 0:4:3, :], wide(k_, 2), ACT.Copy)
                return nc.scalar.activation(kp[:, :, 5:6, :], wide(k_, 1), ACT.Copy)

            def take_qkv(act, y, slot):
                if not windowed:
                    wait(act, s_nm, 3 * y)
                act.wait_ge(s_qkv, y + 1)
                part = lambda a: bank[6][:, a * P:(a + 1) * P]
                dst = (raw[:].rearrange("p a h d e -> p a (h d e)") if windowed
                       else qk[:].rearrange("p a h d -> p a (h d)"))
                nc.scalar.activation(dst[:, 0], part(0), ACT.Copy, scale=SCALE)
                nc.scalar.activation(dst[:, 1], part(1), ACT.Copy)
                if not windowed:
                    wide_copies(part(0).rearrange("p (h d) -> p h d", d=HD),
                                part(1).rearrange("p (h d) -> p h d", d=HD), SCALE)
                nc.scalar.activation(V[:, slot % R, :, 0:HD], part(2).rearrange("p (h d) -> p h d", d=HD), ACT.Copy)\
                    .then_inc(s_raw, 1)

            def first_parts(act, y):
                act.wait_ge(s_rot, 2 * y + 2)
                wide_copies(qk[:, 0], qk[:, 1], 1.0).then_inc(s_first, 1)

            def take_turned(act, y, slot):
                act.wait_ge(s_kt, y + 1)
                nc.scalar.activation(kT[:, slot % R].rearrange("p g q -> p (g q)"), bf16_bank(0), ACT.Copy)
                act.wait_ge(s_qt, y + 1)
                nc.scalar.activation(qT[:, slot % 2].rearrange("p g q -> p (g q)"), bf16_bank(1), ACT.Copy)\
                    .then_inc(s_qev, 1)

            def scalar_step(act, y, slot):
                for w in range(NW):
                    wait(act, s_pv, y * NW + (w - 1))
                    act.wait_ge(s_t, y * NW + (w + 1))
                    nc.scalar.activation(pb[:, w % 2, 0:2 * HW], bank[2 + w % 2][:, 0:2 * HW], ACT.Exp).then_inc(s_ex, 1)
                    if w == 0 and to_come(y, 2):
                        take_qkv(act, y + 2, slot + 2)
                        if to_come(y, 3):
                            stage(act, y + 3)
                    if w == 3 and windowed and to_come(y, 2):
                        first_parts(act, y + 2)
                    if w == 6 and to_come(y, 2):
                        take_turned(act, y + 2, slot + 2)

            @block.scalar
            def _(act):
                stage(act, 0)
                for y in range(2):
                    take_qkv(act, y, y)
                    stage(act, y + 1)
                    if windowed:
                        first_parts(act, y)
                    take_turned(act, y, y)
                steps(act, lambda y, slot: scalar_step(act, y, slot))

            def maximum(dve, y, w):
                h = heads(w)[0]
                dve.wait_ge(s_s, y * NW + (w + 1))
                nc.vector.tensor_reduce(mx[:, h:h + 3:2], bank[w % 2][:, 0:2 * HW].rearrange("p (j q) -> p j q", j=2),
                                        AX.X, ALU.max, negate=True).then_inc(s_mx, 1)

            def lengths(dve, y):
                v = nc.vector
                flat = lambda a: a[:].rearrange("p a h d -> p (a h) d")
                dve.wait_ge(s_raw, y + 1)
                v.tensor_tensor(square[:], qk[:], qk[:], ALU.mult).then_inc(s_nm, 1)
                dve.wait_ge(s_nm, 3 * y + 1)
                v.tensor_reduce(norm2[:], flat(square), AX.X, ALU.add).then_inc(s_nm, 1)
                dve.wait_ge(s_nm, 3 * y + 2)
                v.tensor_tensor(norm2max[:], norm2[:], norm2max[:], ALU.max).then_inc(s_nm, 1)

            def split_maxima(dve, y):
                dve.wait_ge(s_mx, y * NW + NW)
                at = lambda n: mp[:, :, 6, n]
                v = nc.vector
                v.tensor_copy(at(0), mx[:]).then_inc(s_mp, 1)
                dve.wait_ge(s_mp, 5 * y + 1)
                v.tensor_tensor(mleft[:, 0], mx[:], at(0), ALU.subtract).then_inc(s_mp, 1)
                dve.wait_ge(s_mp, 5 * y + 2)
                v.tensor_copy(at(1), mleft[:, 0]).then_inc(s_mp, 1)
                dve.wait_ge(s_mp, 5 * y + 3)
                v.tensor_tensor(mleft[:, 1], mleft[:, 0], at(1), ALU.subtract).then_inc(s_mp, 1)
                dve.wait_ge(s_mp, 5 * y + 4)
                v.tensor_copy(at(2), mleft[:, 1]).then_inc(s_mp, 1)

            def maxima_onto_q(dve, y, slot):
                dve.wait_ge(s_mt, y + 1)
                flat = lambda a: a[:, slot % 2].rearrange("p g q -> p (g q)")
                nc.vector.tensor_tensor(flat(q2), flat(qT), bf16_bank(5), ALU.add).then_inc(s_q2, 1)

            def take_values(dve, y):
                dve.wait_ge(s_pv, y * NW + NW)
                nc.vector.tensor_copy(osb[:], bank[4][:]).then_inc(s_osb, 1)

            def invert(dve, y):
                dve.wait_ge(s_rep, y + 1)
                nc.vector.reciprocal(rec[:], bank[7][:]).then_inc(s_rec, 1)

            def normalise(dve, y):
                dve.wait_ge(s_rec, y + 1)
                nc.vector.tensor_tensor(on[:], osb[:], rec[:], ALU.mult).then_inc(s_on, 1)

            def add(dve, y):
                dve.wait_ge(s_pr, y + 1)
                xt = k.X[:, bass.ds(y, 1), :]
                nc.vector.tensor_tensor(xt, bank[7][:, 0:P].rearrange("p (o q) -> p o q", o=1), xt, ALU.add)\
                    .then_inc(s_x, 1)

            def vector_step(dve, y, slot):
                before = not isinstance(y, int) or y > 0
                if before:
                    take_values(dve, y - 1)
                for w in range(NW):
                    if to_come(y, 1):
                        maximum(dve, y + 1, w)
                if to_come(y, 1):
                    split_maxima(dve, y + 1)
                if before:
                    invert(dve, y - 1)
                if to_come(y, 1):
                    maxima_onto_q(dve, y + 1, slot + 1)
                if before:
                    normalise(dve, y - 1)
                    add(dve, y - 1)
                if not windowed and to_come(y, 2):
                    lengths(dve, y + 2)

            @block.vector
            def _(dve):
                if not windowed:
                    lengths(dve, 0)
                    lengths(dve, 1)
                for w in range(NW):
                    maximum(dve, 0, w)
                split_maxima(dve, 0)
                maxima_onto_q(dve, 0, 0)
                steps(dve, lambda y, slot: vector_step(dve, y, slot))
                take_values(dve, T - 1)
                invert(dve, T - 1)
                normalise(dve, T - 1)
                add(dve, T - 1)

            def rotate(pool, tile):
                even, odd = (raw[:, :, :, :, a].rearrange("p a h d -> p (a h) d") for a in range(2))
                for n, (x, a) in enumerate(((even, 0), (odd, 1), (odd, 0), (even, 1))):
                    f = cs[:, bass.ds(tile, 1), a, :].to_broadcast([P, 2 * HEADS, HD // 2])
                    last = nc.gpsimd.tensor_tensor(rot[:, n], x, f, ALU.mult)
                last.then_inc(s_rot, 1)
                k.wait_alone(pool, s_rot, tile * 2 + 1)
                to = qk[:].rearrange("p a h (d two) -> p two (a h) d", two=2)
                nc.gpsimd.tensor_tensor(to[:, 0], rot[:, 0], rot[:, 1], ALU.subtract)
                nc.gpsimd.tensor_tensor(to[:, 1], rot[:, 2], rot[:, 3], ALU.add).then_inc(s_rot, 1)
                k.wait_alone(pool, s_rot, tile * 2 + 2)

            @block.gpsimd
            def _(pool):
                with pool.Fori(0, T) as y:
                    k.wait_alone(pool, s_raw, y + 1)
                    if windowed:
                        rotate(pool, y)
                        k.wait_alone(pool, s_first, y + 1)
                    split_in_parts(k, pool, y, qk, qp, kp, left, s_sp, first=False)

        if not windowed:
            bound = float(((P + 1 - EXP_IS_ZERO) / 2.0) ** 2)
            flag = sb("flag", [1, 1], U32)
            small, both = sb("small", [P, 2]), sb("both", [1, 4])
            s_f = sem("flag")
            with nc.Block() as block:
                @block.vector
                def _(dve):
                    v = nc.vector
                    v.tensor_reduce(small[:], norm2max[:].rearrange("p (a h) -> p a h", a=2), AX.X, ALU.max)\
                        .then_inc(s_f, 1)
                    dve.wait_ge(s_f, 2)
                    v.tensor_reduce(both[:, 0:2], bank[0][0:1, 0:2 * P].rearrange("p (a q) -> p a q", a=2), AX.X,
                                    ALU.max).then_inc(s_f, 1)
                    dve.wait_ge(s_f, 3)
                    v.tensor_tensor(both[:, 2:3], both[:, 0:1], both[:, 1:2], ALU.mult).then_inc(s_f, 1)
                    dve.wait_ge(s_f, 4)
                    v.tensor_scalar(both[:, 3:4], both[:, 2:3], bound, None, ALU.is_le).then_inc(s_f, 1)
                    dve.wait_ge(s_f, 5)
                    v.tensor_copy(flag[:], both[:, 3:4])

                @block.tensor
                def _(pe):
                    pe.wait_ge(s_f, 1)
                    for a in range(2):
                        last = nc.tensor.matmul(bank[0][0:1, a * P:(a + 1) * P], small[:, a:a + 1], k.ident[:],
                                                start=True, stop=True)
                    last.then_inc(s_f, 1)
            k.end_part()
            band_is_enough = nc.values_load(flag[0:1, 0:1], engines=EVERY_ENGINE, min_val=0, max_val=1,
                                            skip_runtime_bounds_check_because="a comparison's result, zero or one")
            with nc.If(band_is_enough == 0):
                nc.all_engine_barrier()
                all_keys(k, name, dict(xs=xs, wqkv=wqkv, bqkv=bqkv, wo=wo, spread=spread, qk=qk, left=left, qp=qp,
                                       kp=kp, mp=mp, mx=mx, mleft=mleft, V=V[:, 0], ks=kT[:, 0], qs=qT[:, 0],
                                       q2=q2[:, 0], osb=osb, rec=rec, on=on, X0=X0), tmp)
            nc.all_engine_barrier()


def split_in_parts(k, pool, y, qk, qp, kp, left, s_sp, first=True):
    g = k.nc.gpsimd
    HEADS, HD = qk.shape[2], qk.shape[3]
    count = 5 if first else 4
    wide = lambda a, n: a[:, :, None, :].to_broadcast([P, HEADS, n, HD])
    src = qk
    for n, (qs, ks) in enumerate((((0, 3), ((0, 4, 3), (5, 6, 1))), ((3, 5), ((1, 5, 3),)), ((5, 6), ((2, 3, 1),)))):
        if n or first:
            g.tensor_copy(qp[:, :, qs[0]:qs[1], :], wide(src[:, 0], qs[1] - qs[0]))
            for a, b, stride in ks:
                last = g.tensor_copy(kp[:, :, a:b:stride, :], wide(src[:, 1], len(range(a, b, stride))))
            last.then_inc(s_sp, 1)
            if n == 2:
                break
            k.wait_alone(pool, s_sp, count * y + 2 * n + count - 4)
        rest = left[:, n]
        g.tensor_tensor(rest[:, 0], src[:, 0], qp[:, :, qs[0], :], ALU.subtract)
        g.tensor_tensor(rest[:, 1], src[:, 1], kp[:, :, n, :], ALU.subtract).then_inc(s_sp, 1)
        k.wait_alone(pool, s_sp, count * y + 2 * n + count - 3)
        src = rest


def all_keys(k, name, b, tmp):
    nc, T, bank = k.nc, k.T, k.bank
    HEADS, HD = 16, P // 16
    G, ROWS = HEADS // 2, 6 * HD + 4
    SCALE = float(HD) ** -0.5
    unit = lambda n: [2 * (4 * (n // 2) + m) + n % 2 for m in range(4)]
    sb = lambda n, shape, dt=F32: k.sb(f"{name}_all_{n}", shape, dt, tmp)
    sem = lambda n: k.sem(f"{name}_all_{n}")
    kT, qT = sb("kT", [P, T, G * P], BF16), sb("qT", [P, T, G * P], BF16)
    V = sb("V", [P, T, HEADS, HD])
    near_q, near_k = sb("near_q", [P, 4 * P], BF16), sb("near_k", [P, 4 * P], BF16)
    far_q, far_k = sb("far_q", [P, 2 * T - 1, P], BF16), sb("far_k", [P, 2 * T - 1, P], BF16)
    zeros = sb("zeros", [P, 4 * P], BF16)
    pb = sb("pb", [P, 4, 4 * P])
    gm, tile_max = sb("gm", [P, HEADS]), sb("tile_max", [P, HEADS])
    flat = lambda a: a.rearrange("p g q -> p (g q)")
    bf16_bank = lambda n: bank[n][:].bitcast(BF16)
    (s_bi, s_xs, s_qkv, s_raw, s_sp, s_kt, s_qt, s_ev, s_ks, s_s, s_tm, s_mx, s_mp, s_mt, s_q2, s_kv, s_t, s_ex, s_pv,
     s_osb, s_rep, s_rec, s_on, s_pr, s_x) = (
        sem(n) for n in ("bias", "xs", "qkv", "raw", "split", "kt", "qt", "ev", "ks", "s", "tile_max", "mx", "mp", "mt",
                         "q2", "kv", "t", "ex", "pv", "osb", "rep", "rec", "on", "proj", "x"))

    with nc.Block() as block:
        @block.tensor
        def _(pe):
            with pe.Fori(0, T) as y:
                pe.wait_ge(s_xs, y + 1)
                dst = bank[6][:, 0:3 * P]
                nc.tensor.matmul(dst, b["xs"][:], b["wqkv"][:], start=True, stop=False)
                nc.tensor.matmul(dst, k.ones[0:1, :], b["bqkv"][:], start=False, stop=True).then_inc(s_qkv, 1)
                pe.wait_ge(s_sp, 5 * y + 5)
                for n, src, done in ((5, b["kp"], s_kt), (6, b["qp"], s_qt)):
                    for g in range(G):
                        last = nc.tensor.transpose(bf16_bank(n)[:, g * P:(g + 1) * P],
                                                   src[:, 2 * g:2 * g + 2].rearrange("p h s d -> p (h s d)"),
                                                   k.identb[:])
                    last.then_inc(done, 1)

        @block.scalar
        def _(act):
            copy = lambda dst, src, **kw: nc.scalar.activation(dst, src, ACT.Copy, **kw)
            part = lambda a: bank[6][:, a * P:(a + 1) * P]
            tiles = k.xnT[:].rearrange("p (t q) -> p t q", q=P)
            with act.Fori(0, T) as y:
                one = bass.ds(y, 1)
                copy(b["xs"][:].rearrange("p (o q) -> p o q", o=1), tiles[:, one, :]).then_inc(s_xs, 1)
                k.wait_alone(act, s_qkv, y + 1)
                qk = b["qk"][:].rearrange("p a h d -> p a (h d)")
                copy(qk[:, 0], part(0), scale=SCALE)
                copy(qk[:, 1], part(1))
                copy(V[:, one].rearrange("p o h d -> p (o h d)"), part(2)).then_inc(s_raw, 1)
                k.wait_alone(act, s_kt, y + 1)
                copy(kT[:, one].rearrange("p o q -> p (o q)"), bf16_bank(5))
                k.wait_alone(act, s_qt, y + 1)
                copy(qT[:, one].rearrange("p o q -> p (o q)"), bf16_bank(6)).then_inc(s_ev, 1)

        @block.gpsimd
        def _(pool):
            g = nc.gpsimd
            n = 0

            def step(ins):
                nonlocal n
                n += 1
                ins.then_inc(s_bi, 1)
                pool.wait_ge(s_bi, n)

            g.memset(zeros[:], 0.0)
            for near, far, sign in ((near_q, far_q, 1), (near_k, far_k, -1)):
                step(g.iota(near[:], pattern=[[0, 4], [sign, P]], base=0, channel_multiplier=-sign,
                            allow_small_or_imprecise_dtypes=True))
                step(g.iota(far[:], pattern=[[-P, 2 * T - 1], [0, P]], base=P * (T - 1), channel_multiplier=0,
                            allow_small_or_imprecise_dtypes=True))
                step(g.memset(far[:, 0:T - 1, :], MASKED))
                step(g.affine_select(out=far[:, T - 1, :], in_=far[:, T - 1, :], compare_op=ALU.is_ge, fill=MASKED,
                                     base=0, pattern=[[-sign, P]], channel_multiplier=sign))
            with pool.Fori(0, T) as y:
                k.wait_alone(pool, s_raw, y + 1)
                split_in_parts(k, pool, y, b["qk"], b["qp"], b["kp"], b["left"], s_sp)

    with nc.Block() as block:
        def scores(near, far, y, z, n, operands, done):
            nc.tensor.matmul(bank[n][:], k.identb[:], near[:], start=True, stop=False, skip_group_check=True)
            for m, h in enumerate(unit(n)):
                dst = bank[n][:, m * P:(m + 1) * P]
                rows = slice(64 * (h % 2), 64 * (h % 2) + ROWS)
                lhsT, rhs = (a[rows, h // 2, :] for a in operands)
                nc.tensor.matmul(dst, k.identb[:], far[:, bass.ds(y - z + (T - 1), 1), :], start=False, stop=False,
                                 skip_group_check=True)
                last = nc.tensor.matmul(dst, lhsT, rhs, start=False, stop=(m == 3), skip_group_check=True)
            last.then_inc(done, 1)

        @block.tensor
        def _(pe):
            with pe.Fori(0, T) as y:
                with pe.Fori(0, T) as z:
                    pe.wait_ge(s_ks, y * T + (z + 1))
                    for n in range(4):
                        scores(near_q, far_q, y, z, n, (b["qs"], b["ks"]), s_s)
                pe.wait_ge(s_mp, 5 * y + 5)
                for g in range(G):
                    last = nc.tensor.transpose(bf16_bank(5)[:, g * P:(g + 1) * P],
                                               b["mp"][:, 2 * g:2 * g + 2].rearrange("p h s d -> p (h s d)"),
                                               k.identb[:])
                last.then_inc(s_mt, 1)
                pe.wait_ge(s_q2, y + 1)
                nc.tensor.matmul(bank[4][:], k.identb[:], zeros[:], start=True, stop=False, skip_group_check=True)
                with pe.Fori(0, T) as z:
                    pe.wait_ge(s_kv, y * T + (z + 1))
                    for n in range(4):
                        scores(near_k, far_k, y, z, n, (b["ks"], b["q2"]), s_t)
                    pe.wait_ge(s_ex, 4 * (y * T + (z + 1)))
                    for n in range(4):
                        for m, h in enumerate(unit(n)):
                            last = nc.tensor.matmul(bank[4][32 * (h % 4):32 * (h % 4) + 32, (h // 4) * P:(h // 4 + 1) * P],
                                                    b["V"][:, h, :], pb[:, n, m * P:(m + 1) * P],
                                                    start=False, stop=(n == 3 and m == 3), skip_group_check=True)
                    last.then_inc(s_pv, 1)
                pe.wait_ge(s_osb, y + 1)
                nc.tensor.matmul(bank[7][:], b["spread"][:], b["osb"][:], start=True, stop=True).then_inc(s_rep, 1)
                pe.wait_ge(s_on, y + 1)
                for g in range(4):
                    last = nc.tensor.matmul(bank[7][:, 0:P], b["on"][:, g * P:(g + 1) * P], b["wo"][:, g, :],
                                            start=(g == 0), stop=(g == 3))
                last.then_inc(s_pr, 1)

        @block.scalar
        def _(act):
            copy = lambda dst, src: nc.scalar.activation(dst, src, ACT.Copy)
            with act.Fori(0, T) as y:
                with act.Fori(0, T) as z:
                    k.wait_alone(act, s_mx, y * T + (z + 1))
                    k.wait_alone(act, s_x, y + 1)
                    copy(flat(b["qs"]), qT[:, bass.ds(y, 1)].rearrange("p o q -> p (o q)"))
                    copy(flat(b["ks"]), kT[:, bass.ds(z, 1)].rearrange("p o q -> p (o q)")).then_inc(s_ks, 1)
                k.wait_alone(act, s_q2, y + 1)
                with act.Fori(0, T) as z:
                    k.wait_alone(act, s_pv, y * T + (z + 1))
                    copy(flat(b["ks"]), kT[:, bass.ds(z, 1)].rearrange("p o q -> p (o q)"))
                    copy(b["V"][:, :, 0:HD], V[:, bass.ds(z, 1)].rearrange("p o h d -> p (o h) d")).then_inc(s_kv, 1)
                    for n in range(4):
                        act.wait_ge(s_t, 4 * (y * T + z) + (n + 1))
                        nc.scalar.activation(pb[:, n, :], bank[n][:], ACT.Exp).then_inc(s_ex, 1)

        @block.vector
        def _(dve):
            v = nc.vector
            v.sem_inc(s_mx, 1)
            v.sem_inc(s_x, 1)
            v.sem_inc(s_pv, 1)
            with dve.Fori(0, T) as y:
                v.memset(gm[:], -3.0e38).then_inc(s_tm, 1)
                k.wait_alone(dve, s_tm, (T + 1) * y + 1)
                with dve.Fori(0, T) as z:
                    for n in range(4):
                        dve.wait_ge(s_s, 4 * (y * T + z) + (n + 1))
                        h = unit(n)[0]
                        last = v.tensor_reduce(tile_max[:, h:h + 7:2], bank[n][:].rearrange("p (j q) -> p j q", j=4),
                                               AX.X, ALU.max)
                    last.then_inc(s_tm, 1)
                    dve.wait_ge(s_tm, (T + 1) * y + (z + 2))
                    v.tensor_tensor(gm[:], gm[:], tile_max[:], ALU.max).then_inc(s_mx, 1)
                    k.wait_alone(dve, s_mx, y * T + (z + 2))
                at = lambda n: b["mp"][:, :, 6, n]
                mx, mleft = b["mx"], b["mleft"]
                v.tensor_scalar(mx[:], gm[:], -1.0, None, ALU.mult).then_inc(s_rec, 1)
                dve.wait_ge(s_rec, 2 * y + 1)
                v.tensor_copy(at(0), mx[:]).then_inc(s_mp, 1)
                dve.wait_ge(s_mp, 5 * y + 1)
                v.tensor_tensor(mleft[:, 0], mx[:], at(0), ALU.subtract).then_inc(s_mp, 1)
                dve.wait_ge(s_mp, 5 * y + 2)
                v.tensor_copy(at(1), mleft[:, 0]).then_inc(s_mp, 1)
                dve.wait_ge(s_mp, 5 * y + 3)
                v.tensor_tensor(mleft[:, 1], mleft[:, 0], at(1), ALU.subtract).then_inc(s_mp, 1)
                dve.wait_ge(s_mp, 5 * y + 4)
                v.tensor_copy(at(2), mleft[:, 1]).then_inc(s_mp, 1)
                dve.wait_ge(s_mt, y + 1)
                v.tensor_tensor(flat(b["q2"]), flat(b["qs"]), bf16_bank(5), ALU.add).then_inc(s_q2, 1)
                dve.wait_ge(s_pv, T * y + (T + 1))
                v.tensor_copy(b["osb"][:], bank[4][:]).then_inc(s_osb, 1)
                dve.wait_ge(s_rep, y + 1)
                v.reciprocal(b["rec"][:], bank[7][:]).then_inc(s_rec, 1)
                dve.wait_ge(s_rec, 2 * y + 2)
                v.tensor_tensor(b["on"][:], b["osb"][:], b["rec"][:], ALU.mult).then_inc(s_on, 1)
                dve.wait_ge(s_pr, y + 1)
                v.tensor_tensor(k.X[:, bass.ds(y, 1), :], bank[7][:, 0:P].rearrange("p (o q) -> p o q", o=1),
                                b["X0"][:, bass.ds(y, 1), :], ALU.add).then_inc(s_x, 1)


def ffn3(k):
    nc, t, C = k.nc, k.t, k.C
    L0, bank = k.L, k.bank
    F = t["f3_w1"].shape[1]
    FB = F // P
    tmp = ExitStack()
    sb = lambda n, shape, dt=F32: k.sb("f3_" + n, shape, dt, tmp)
    sem = lambda n: k.sem("f3_" + n)
    with tmp:
        w1, w2 = sb("w1", [P, F]), sb("w2", [P, F])
        hw = [sb("h1w", [P, FB, F]), sb("h2w", [P, FB, F])]
        w3 = sb("w3", [P, FB, P])
        sc1, sc2, sch1, sch2 = (sb(n, [P, FB]) for n in ("sc1", "sc2", "sch1", "sch2"))
        s3 = sb("s3", [P, P])
        sg = sb("sg", [P, 2, CW])
        hA = [sb(f"hA{b}", [P, FB, CW]) for b in range(2)]
        hB = [sb(f"hB{b}", [P, FB, CW]) for b in range(2)]
        ys = sb("ys", [P, CT, P])
        lw, s_ab, s_sg, s_a, s_m, s_g, s_y, s_ys, s_x = (
            sem(n) for n in ("w", "ab", "sg", "a", "m", "g", "y", "ys", "x"))
        col = lambda n: t[n].rearrange("(f p) -> p f", p=P)
        mat = lambda n: t[n].rearrange("(f p) o -> p f o", p=P)
        loads = [(w1[:], t["f3_w1"]), (w2[:], t["f3_w2"]), (hw[0][:], mat("f3_h1")), (hw[1][:], mat("f3_h2")),
                 (w3[:], mat("f3_w3")), (sc1[:], col("f3_s1")), (sc2[:], col("f3_s2")), (sch1[:], col("f3_sh1")),
                 (sch2[:], col("f3_sh2")), (s3[:], t["f3_s3"].partition_broadcast(P))]
        with nc.Block() as block:
            @block.sync
            def _(sp):
                with nc.allow_non_contiguous_dma(reason="scale columns"):
                    for dst, src in loads:
                        sp.dma_start(dst, src).then_inc(lw, 16)

            @block.gpsimd
            def _(pool):
                for c in range(C):
                    k.norm_pool(L0 + c)

            @block.scalar
            def _(act):
                for c in range(C):
                    k.norm_scalar(L0 + c, k.xnT[:, c * CW:(c + 1) * CW])

            @block.tensor
            def _(pe):
                for c in range(C):
                    k.norm_tensor(L0 + c)
                pe.wait_ge(lw, 16 * len(loads))

            @block.vector
            def _(dve):
                for c in range(C):
                    k.norm_vector(L0 + c, c)
        k.L += C

        with nc.Block() as block:
            @block.tensor
            def _(pe):
                with pe.Fori(0, C // 2) as it:
                    for b in range(2):
                        if b == 0:
                            pe.wait_ge(s_ys, it * 2 + 2)
                        for f in range(FB):
                            pe.wait_ge(s_a, it * (2 * FB) + (b * FB + f) + 1)
                            for j, w in enumerate((w1, w2)):
                                nc.tensor.matmul(bank[2 * (f % 2) + j][:], w[:, f * P:(f + 1) * P],
                                                 k.xnT[:, bass.ds(it * (2 * CW) + b * CW, CW)], start=True, stop=True)\
                                    .then_inc(s_ab, 1)
                    for layer in range(2):
                        for b in range(2):
                            src = hA[b] if layer == 0 else hB[b]
                            if layer == 0:
                                pe.wait_ge(s_a, it * (2 * FB) + (b + 1) * FB + 2)
                            else:
                                pe.wait_ge(s_g, it * (4 * FB) + (b + 1) * FB + 4)
                            for f in range(FB):
                                m = (layer * 2 + b) * FB + f
                                pe.wait_ge(s_g, it * (4 * FB) + m + 1)
                                for i in range(FB):
                                    last = nc.tensor.matmul(bank[4 + m % 4][:], hw[layer][:, i, f * P:(f + 1) * P],
                                                            src[:, i, :], start=(i == 0), stop=(i == FB - 1))
                                last.then_inc(s_m, 1)
                    for b in range(2):
                        pe.wait_ge(s_g, it * (4 * FB) + (2 + b + 1) * FB + 4)
                        for i in range(CT):
                            for f in range(FB):
                                last = nc.tensor.matmul(bank[b][:, i * P:(i + 1) * P],
                                                        hA[b][:, f, i * P:(i + 1) * P], w3[:, f, :],
                                                        start=(f == 0), stop=(f == FB - 1))
                        last.then_inc(s_y, 1)

            @block.scalar
            def _(act):
                nc.scalar.sem_inc(s_g, 4)
                with act.Fori(0, C // 2) as it:
                    for b in range(2):
                        for f in range(FB):
                            n = it * (2 * FB) + (b * FB + f)
                            act.wait_ge(s_ab, n * 2 + 1)
                            act.wait_ge(s_a, n + 1)
                            nc.scalar.activation(sg[:, f % 2, :], bank[2 * (f % 2)][:], ACT.Silu, scale=sc1[:, f:f + 1])\
                                .then_inc(s_sg, 1)
                    for layer, (dst, sc) in enumerate(((hB, sch1), (hA, sch2))):
                        for b in range(2):
                            for f in range(FB):
                                m = (layer * 2 + b) * FB + f
                                act.wait_ge(s_m, it * (4 * FB) + m + 1)
                                nc.scalar.activation(dst[b][:, f, :], bank[4 + m % 4][:], ACT.Gelu, scale=sc[:, f:f + 1])\
                                    .then_inc(s_g, 1)

            @block.vector
            def _(dve):
                v = nc.vector
                v.sem_inc(s_a, 2)
                v.sem_inc(s_ys, 2)
                with dve.Fori(0, C // 2) as it:
                    for b in range(2):
                        for f in range(FB):
                            n = it * (2 * FB) + (b * FB + f)
                            dve.wait_ge(s_ab, n * 2 + 2)
                            dve.wait_ge(s_sg, n + 1)
                            v.scalar_tensor_tensor(out=hA[b][:, f, :], in0=bank[2 * (f % 2) + 1][:],
                                                   scalar=sc2[:, f:f + 1], in1=sg[:, f % 2, :], op0=ALU.mult,
                                                   op1=ALU.mult).then_inc(s_a, 1)
                    for b in range(2):
                        q = it * 2 + b
                        dve.wait_ge(s_y, q + 1)
                        v.tensor_tensor(ys[:], bank[b][:].rearrange("p (i d) -> p i d", i=CT),
                                        s3[:, None, :].to_broadcast([P, CT, P]), ALU.mult).then_inc(s_ys, 1)
                        dve.wait_ge(s_ys, q + 3)
                        xt = k.X[:, bass.ds(q * CT, CT), :]
                        v.tensor_tensor(xt, xt, ys[:], ALU.add).then_inc(s_x, 1)
                        dve.wait_ge(s_x, q + 1)


def store(k, out):
    with k.nc.Block() as block:
        @block.sync
        def _(sp):
            sp.dma_start(out.rearrange("(t p) d -> p t d", p=P), k.X[:]).then_inc(k.stored, 16)
            sp.wait_ge(k.stored, 16)


def program(nc, t, out, parts=PARTS):
    with ExitStack() as ctx:
        k = Core(nc, ctx, t)
        constants(k)
        for part in parts:
            if part == "mamba":
                mamba(k)
            elif part in ("moe0", "moe1"):
                experts(k, part, gated=(part == "moe1"))
            elif part == "linear":
                linear(k)
            elif part in ("decay", "window"):
                softmax_mixer(k, part, windowed=(part == "window"))
            elif part == "deep":
                deep(k)
            elif part == "ffn3":
                ffn3(k)
            k.end_part()
        store(k, out)


NAMES = {
    "x": ("L0_attn_x", lambda a: a.reshape(a.shape[1:])),
    "ln1_g": ("L0_attn_ln1_g", None), "ln1_b": ("L0_attn_ln1_b", None),
    "in_proj_w": ("L0_attn_in_proj_w", None),
    "conv_w": ("L0_attn_conv_w", lambda a: a.reshape(a.shape[0], a.shape[2])),
    "conv_b": ("L0_attn_conv_b", None), "x_proj_w": ("L0_attn_x_proj_w", None),
    "dt_proj_w": ("L0_attn_dt_proj_w", None), "dt_proj_b": ("L0_attn_dt_proj_b", None),
    "A_log": ("L0_attn_A_log", None), "D": ("L0_attn_D", None), "out_proj_w": ("L0_attn_out_proj_w", None),
    "ln2_g": ("L0_attn_ln2_g", None), "ln2_b": ("L0_attn_ln2_b", None),
    "ffn_w1": ("L0_attn_ffn_w1", None), "ffn_b1": ("L0_attn_ffn_b1", None),
    "ffn_w2": ("L0_attn_ffn_w2", None), "ffn_b2": ("L0_attn_ffn_b2", None),
    "moe0_gate_w": ("L0_ffn_gate_w", None), "moe0_gate_b": ("L0_ffn_gate_b", None),
    "moe0_w1": ("L0_ffn_w1", None), "moe0_b1": ("L0_ffn_b1", None),
    "moe0_w2": ("L0_ffn_w2", None), "moe0_b2": ("L0_ffn_b2", None),
    "lin_wqT": ("L1_attn_Wq", lambda a: a.T), "lin_wkT": ("L1_attn_Wk", lambda a: a.T), "lin_wv": ("L1_attn_Wv", None),
    "lin_bq": ("L1_attn_bq", None), "lin_bk": ("L1_attn_bk", None), "lin_bv": ("L1_attn_bv", None),
    "lin_gamma": ("L1_attn_gamma", None),
    "moe1_gate_w": ("L1_ffn_router_w", lambda a: a.T), "moe1_w1": ("L1_ffn_w_gate", None),
    "moe1_wu": ("L1_ffn_w_up", None), "moe1_w2": ("L1_ffn_w_down", None),
    "decay_wq": ("L2_attn_Wq", lambda a: a.T), "decay_wk": ("L2_attn_Wk", lambda a: a.T),
    "decay_wv": ("L2_attn_Wv", lambda a: a.T), "decay_wo": ("L2_attn_Wo", lambda a: a.T),
    "decay_bq": ("L2_attn_bq", None), "decay_bk": ("L2_attn_bk", None), "decay_bv": ("L2_attn_bv", None),
    "decay_bo": ("L2_attn_bo", None),
    "deep_gate_w": ("L2_ffn_gate_w", None), "deep_gate_b": ("L2_ffn_gate_b", None),
    "deep_w1": ("L2_ffn_w1", None), "deep_b1": ("L2_ffn_b1", None), "deep_w2": ("L2_ffn_w2", None),
    "deep_b2": ("L2_ffn_b2", None), "deep_w3": ("L2_ffn_w3", None), "deep_b3": ("L2_ffn_b3", None),
    "window_wqkv": ("L3_attn_w_qkv", None), "window_wo": ("L3_attn_w_o", None),
    "f3_w1": ("L3_ffn_w1_w", lambda a: a.T), "f3_s1": ("L3_ffn_w1_s", None),
    "f3_w2": ("L3_ffn_w2_w", lambda a: a.T), "f3_s2": ("L3_ffn_w2_s", None),
    "f3_h1": ("L3_ffn_h1_w", lambda a: a.T), "f3_sh1": ("L3_ffn_h1_s", None),
    "f3_h2": ("L3_ffn_h2_w", lambda a: a.T), "f3_sh2": ("L3_ffn_h2_s", None),
    "f3_w3": ("L3_ffn_w3_w", lambda a: a.T), "f3_s3": ("L3_ffn_w3_s", None),
}


def rotary_table(np, n, half, base=10000.0):
    inv = (np.float32(1.0) / np.float32(base) ** (np.arange(half, dtype=np.float32) / np.float32(half)))
    angle = np.arange(n, dtype=np.float32)[:, None] * inv.astype(np.float32)[None, :]
    return np.ascontiguousarray(np.stack([np.cos(angle), np.sin(angle)], axis=1).astype(np.float32))


def kernel(**inputs):
    import numpy as np
    import concourse.bacc as bacc
    from concourse.bass_utils import run_bass_kernel_spmd as run

    nc = bacc.Bacc("TRN2", target_bir_lowering=False, num_devices=1)
    arrays, t = {}, {}
    for name, (source, lay) in NAMES.items():
        a = np.asarray(inputs[source])
        a = np.ascontiguousarray(lay(a) if lay else a)
        arrays["in_" + name] = a
        t[name] = nc.dram_tensor("in_" + name, a.shape, mybir.dt.from_np(a.dtype), kind="ExternalInput").ap()
    shape = inputs["L0_attn_x"].shape
    arrays["in_rotary"] = rotary_table(np, shape[1], 4)
    t["rotary"] = nc.dram_tensor("in_rotary", arrays["in_rotary"].shape, F32, kind="ExternalInput").ap()
    out = nc.dram_tensor("out", shape[1:], F32, kind="ExternalOutput").ap()
    program(nc, t, out)
    r = run(nc, [arrays], core_ids=[0])
    return r.results[0]["out"].reshape(shape)
```
